# Optimizing a Trainium2 kernel written in Bass

```python
import numpy as np
import jax
import jax.numpy as jnp

def _softmax(x, axis=-1):
    return jax.nn.softmax(x, axis=axis)

def _gelu(x):
    return jax.nn.gelu(x, approximate=True)

def _silu(x):
    return jax.nn.silu(x)

def _sigmoid(x):
    return jax.nn.sigmoid(x)

def _layernorm(x, axis=-1, eps=1e-05):
    m = jnp.mean(x, axis=axis, keepdims=True)
    v = jnp.var(x, axis=axis, keepdims=True)
    return (x - m) / jnp.sqrt(v + eps)

def _scatter_add(tgt, idx, src, axis=0):
    return tgt.at[idx].add(src)

def _segment_sum(src, seg, n):
    return jax.ops.segment_sum(src, seg, n)
kernel_name = 'mk_gnn_ffn_d2_gnn_r16_2857bc'

def setup_inputs(seed: int=0):
    np.random.seed(seed)
    _w = jnp.asarray

    def _rec_inputs():
        import jax
        import jax.numpy as jnp
        _gk = jax.random.key(seed)
        x = -0.0002117 + 1 * jax.random.normal(jax.random.fold_in(_gk, 1), (6250, 256), jnp.float32)
        src = jax.random.randint(jax.random.fold_in(_gk, 2), (100000,), 0, 6250, jnp.int32)
        dst = jnp.minimum((6250 * jax.random.uniform(jax.random.fold_in(_gk, 3), (100000,)) ** 2.0).astype(jnp.int32), 99999)
        _o = jnp.argsort(dst, stable=True)
        src = src[_o]
        dst = dst[_o]
        edge_weight = jax.random.uniform(jax.random.fold_in(_gk, 13), (100000,), jnp.float32, 0.0, 1)
        return (x, src, dst, edge_weight)
    x, src, dst, edge_weight = _rec_inputs()

    def _L0_gnn_setup():
        import jax, jax.numpy as jnp
        import numpy as np
        N = 6250
        E = 200000
        DI = 256
        DO = 256
        BN_EPS = 1e-05

        def _bn_relu(h, gamma, beta):
            mean = jnp.mean(h, axis=0)
            var = jnp.var(h, axis=0)
            hn = (h - mean) * jax.lax.rsqrt(var + BN_EPS)
            return jax.nn.relu(hn * gamma + beta)
        key = jax.random.key(seed)
        ks = jax.random.split(key, 6)
        x = jax.random.normal(ks[0], (N, DI), dtype=jnp.float32)
        edge_row = jax.random.randint(ks[1], (E,), 0, N, dtype=jnp.int32)
        edge_col = jax.random.randint(ks[2], (E,), 0, N, dtype=jnp.int32)
        edge_vals = jnp.ones((E,), dtype=jnp.float32)
        eps = jnp.zeros((1,), dtype=jnp.float32)
        W1 = jax.random.normal(ks[3], (DI, DO), dtype=jnp.float32) * 0.05
        b1 = jnp.zeros((DO,), dtype=jnp.float32)
        g1 = jnp.ones((DO,), dtype=jnp.float32)
        be1 = jnp.zeros((DO,), dtype=jnp.float32)
        W2 = jax.random.normal(ks[4], (DO, DO), dtype=jnp.float32) * 0.05
        b2 = jnp.zeros((DO,), dtype=jnp.float32)
        g2 = jnp.ones((DO,), dtype=jnp.float32)
        be2 = jnp.zeros((DO,), dtype=jnp.float32)
        return {'x': x, 'edge_row': edge_row, 'edge_col': edge_col, 'edge_vals': edge_vals, 'eps': eps, 'W1': W1, 'b1': b1, 'g1': g1, 'be1': be1, 'W2': W2, 'b2': b2, 'g2': g2, 'be2': be2}
    _L0_gnn_all = _L0_gnn_setup()
    _L0_gnn_in = {k: v for k, v in _L0_gnn_all.items() if k in ('eps', 'W1', 'b1', 'g1', 'be1', 'W2', 'b2', 'g2', 'be2')}
    del _L0_gnn_all

    def _L0_ffn_setup():
        import jax, jax.numpy as jnp
        import numpy as np
        TOP_K = 2
        LN_EPS = 1e-05
        key = jax.random.key(seed)
        ks = jax.random.split(key, 8)
        B, S, D, E, H = (16, 1024, 256, 8, 1024)
        x = jax.random.normal(ks[0], (B, S, D), dtype=jnp.float32)
        Wr = jax.random.normal(ks[1], (D, E), dtype=jnp.float32) * 0.1
        br = jnp.zeros((E,), dtype=jnp.float32)
        ln_g = jnp.ones((E, D), dtype=jnp.float32)
        ln_b = jnp.zeros((E, D), dtype=jnp.float32)
        W1 = jax.random.normal(ks[2], (E, D, H), dtype=jnp.float32) * (1.0 / np.sqrt(D))
        b1 = jnp.zeros((E, H), dtype=jnp.float32)
        W2 = jax.random.normal(ks[3], (E, H, D), dtype=jnp.float32) * (1.0 / np.sqrt(H))
        b2 = jnp.zeros((E, D), dtype=jnp.float32)
        return {'x': x, 'Wr': Wr, 'br': br, 'ln_g': ln_g, 'ln_b': ln_b, 'W1': W1, 'b1': b1, 'W2': W2, 'b2': b2}
    _L0_ffn_all = _L0_ffn_setup()
    _L0_ffn_in = {k: v for k, v in _L0_ffn_all.items() if k in ('Wr', 'br', 'ln_g', 'ln_b', 'W1', 'b1', 'W2', 'b2')}
    del _L0_ffn_all

    def _L1_gnn_setup():
        import jax, jax.numpy as jnp
        import numpy as np
        EPS = 1e-05

        def _bn(x, gamma, beta):
            m = jnp.mean(x, axis=0)
            v = jnp.mean((x - m) ** 2, axis=0)
            return gamma * (x - m) * jax.lax.rsqrt(v + EPS) + beta

        def _hconv(x, src, dst, ew, w1, b1, w2, b2, g, b):
            h = jax.nn.relu(x @ w1 + b1)
            msg = ew[:, None] * h[src]
            agg = jax.ops.segment_sum(msg, dst, num_segments=x.shape[0])
            h = agg @ w2 + b2
            return jax.nn.relu(_bn(h, g, b))
        N, C, E = (3125, 256, 18750)
        key = jax.random.key(seed)
        ks = jax.random.split(key, 16)
        s = 1.0 / np.sqrt(C)
        inp = {'x': jax.random.normal(ks[0], (N, C), dtype=jnp.float32), 'hyperedge_index': jax.random.randint(ks[1], (2, E), 0, N, dtype=jnp.int32), 'hyperedge_weight': jax.random.uniform(ks[2], (E,), dtype=jnp.float32), 'c1_w1': jax.random.normal(ks[3], (C, C), dtype=jnp.float32) * s, 'c1_b1': jnp.zeros((C,), jnp.float32), 'c1_w2': jax.random.normal(ks[4], (C, C), dtype=jnp.float32) * s, 'c1_b2': jnp.zeros((C,), jnp.float32), 'c1_g': jnp.ones((C,), jnp.float32), 'c1_b': jnp.zeros((C,), jnp.float32), 'bn1_g': jnp.ones((C,), jnp.float32), 'bn1_b': jnp.zeros((C,), jnp.float32), 'c2_w1': jax.random.normal(ks[5], (C, C), dtype=jnp.float32) * s, 'c2_b1': jnp.zeros((C,), jnp.float32), 'c2_w2': jax.random.normal(ks[6], (C, C), dtype=jnp.float32) * s, 'c2_b2': jnp.zeros((C,), jnp.float32), 'c2_g': jnp.ones((C,), jnp.float32), 'c2_b': jnp.zeros((C,), jnp.float32), 'bn2_g': jnp.ones((C,), jnp.float32), 'bn2_b': jnp.zeros((C,), jnp.float32)}
        return inp
    _L1_gnn_all = _L1_gnn_setup()
    _L1_gnn_in = {k: v for k, v in _L1_gnn_all.items() if k in ('c1_w1', 'c1_b1', 'c1_w2', 'c1_b2', 'c1_g', 'c1_b', 'bn1_g', 'bn1_b', 'c2_w1', 'c2_b1', 'c2_w2', 'c2_b2', 'c2_g', 'c2_b', 'bn2_g', 'bn2_b')}
    del _L1_gnn_all

    def _L1_ffn_setup():
        import jax, jax.numpy as jnp
        import numpy as np
        B, A = (256, 8)
        IN, OUT = (256, 256)
        SH1, SH2 = (256, 128)
        EH1, EH2 = (128, 64)
        E, TOPK = (4, 2)

        def _shared_mlp(x, W1, b1, W2, b2, W3, b3):
            h = jax.nn.relu(x @ W1 + b1)
            h = jax.nn.relu(h @ W2 + b2)
            return h @ W3 + b3

        def _experts_mlp(x, eW1, eb1, eW2, eb2, eW3, eb3):
            h = jax.nn.relu(jnp.einsum('baf,efh->ebah', x, eW1) + eb1[:, None, None, :])
            h = jax.nn.relu(jnp.einsum('ebah,ehg->ebag', h, eW2) + eb2[:, None, None, :])
            o = jnp.einsum('ebag,ego->ebao', h, eW3) + eb3[:, None, None, :]
            return jnp.moveaxis(o, 0, -1)
        key = jax.random.key(seed)
        ks = jax.random.split(key, 16)
        s = 0.05
        return {'x': jax.random.normal(ks[0], (B, A, IN), jnp.float32), 'sW1': jax.random.normal(ks[1], (IN, SH1), jnp.float32) * s, 'sb1': jnp.zeros((SH1,), jnp.float32), 'sW2': jax.random.normal(ks[2], (SH1, SH2), jnp.float32) * s, 'sb2': jnp.zeros((SH2,), jnp.float32), 'sW3': jax.random.normal(ks[3], (SH2, OUT), jnp.float32) * s, 'sb3': jnp.zeros((OUT,), jnp.float32), 'eW1': jax.random.normal(ks[4], (E, IN, EH1), jnp.float32) * s, 'eb1': jnp.zeros((E, EH1), jnp.float32), 'eW2': jax.random.normal(ks[5], (E, EH1, EH2), jnp.float32) * s, 'eb2': jnp.zeros((E, EH2), jnp.float32), 'eW3': jax.random.normal(ks[6], (E, EH2, OUT), jnp.float32) * s, 'eb3': jnp.zeros((E, OUT), jnp.float32), 'gW': jax.random.normal(ks[7], (IN, E), jnp.float32) * s, 'gb': jnp.zeros((E,), jnp.float32)}
    _L1_ffn_all = _L1_ffn_setup()
    _L1_ffn_in = {k: v for k, v in _L1_ffn_all.items() if k in ('sW1', 'sb1', 'sW2', 'sb2', 'sW3', 'sb3', 'eW1', 'eb1', 'eW2', 'eb2', 'eW3', 'eb3', 'gW', 'gb')}
    del _L1_ffn_all
    return {'x': x, 'src': src, 'dst': dst, 'edge_weight': edge_weight, 'L0_gnn_eps': _L0_gnn_in['eps'], 'L0_gnn_W1': _L0_gnn_in['W1'], 'L0_gnn_b1': _L0_gnn_in['b1'], 'L0_gnn_g1': _L0_gnn_in['g1'], 'L0_gnn_be1': _L0_gnn_in['be1'], 'L0_gnn_W2': _L0_gnn_in['W2'], 'L0_gnn_b2': _L0_gnn_in['b2'], 'L0_gnn_g2': _L0_gnn_in['g2'], 'L0_gnn_be2': _L0_gnn_in['be2'], 'L0_ffn_Wr': _L0_ffn_in['Wr'], 'L0_ffn_br': _L0_ffn_in['br'], 'L0_ffn_ln_g': _L0_ffn_in['ln_g'], 'L0_ffn_ln_b': _L0_ffn_in['ln_b'], 'L0_ffn_W1': _L0_ffn_in['W1'], 'L0_ffn_b1': _L0_ffn_in['b1'], 'L0_ffn_W2': _L0_ffn_in['W2'], 'L0_ffn_b2': _L0_ffn_in['b2'], 'L1_gnn_c1_w1': _L1_gnn_in['c1_w1'], 'L1_gnn_c1_b1': _L1_gnn_in['c1_b1'], 'L1_gnn_c1_w2': _L1_gnn_in['c1_w2'], 'L1_gnn_c1_b2': _L1_gnn_in['c1_b2'], 'L1_gnn_c1_g': _L1_gnn_in['c1_g'], 'L1_gnn_c1_b': _L1_gnn_in['c1_b'], 'L1_gnn_bn1_g': _L1_gnn_in['bn1_g'], 'L1_gnn_bn1_b': _L1_gnn_in['bn1_b'], 'L1_gnn_c2_w1': _L1_gnn_in['c2_w1'], 'L1_gnn_c2_b1': _L1_gnn_in['c2_b1'], 'L1_gnn_c2_w2': _L1_gnn_in['c2_w2'], 'L1_gnn_c2_b2': _L1_gnn_in['c2_b2'], 'L1_gnn_c2_g': _L1_gnn_in['c2_g'], 'L1_gnn_c2_b': _L1_gnn_in['c2_b'], 'L1_gnn_bn2_g': _L1_gnn_in['bn2_g'], 'L1_gnn_bn2_b': _L1_gnn_in['bn2_b'], 'L1_ffn_sW1': _L1_ffn_in['sW1'], 'L1_ffn_sb1': _L1_ffn_in['sb1'], 'L1_ffn_sW2': _L1_ffn_in['sW2'], 'L1_ffn_sb2': _L1_ffn_in['sb2'], 'L1_ffn_sW3': _L1_ffn_in['sW3'], 'L1_ffn_sb3': _L1_ffn_in['sb3'], 'L1_ffn_eW1': _L1_ffn_in['eW1'], 'L1_ffn_eb1': _L1_ffn_in['eb1'], 'L1_ffn_eW2': _L1_ffn_in['eW2'], 'L1_ffn_eb2': _L1_ffn_in['eb2'], 'L1_ffn_eW3': _L1_ffn_in['eW3'], 'L1_ffn_eb3': _L1_ffn_in['eb3'], 'L1_ffn_gW': _L1_ffn_in['gW'], 'L1_ffn_gb': _L1_ffn_in['gb']}

def reference(x, src, dst, edge_weight, L0_gnn_eps, L0_gnn_W1, L0_gnn_b1, L0_gnn_g1, L0_gnn_be1, L0_gnn_W2, L0_gnn_b2, L0_gnn_g2, L0_gnn_be2, L0_ffn_Wr, L0_ffn_br, L0_ffn_ln_g, L0_ffn_ln_b, L0_ffn_W1, L0_ffn_b1, L0_ffn_W2, L0_ffn_b2, L1_gnn_c1_w1, L1_gnn_c1_b1, L1_gnn_c1_w2, L1_gnn_c1_b2, L1_gnn_c1_g, L1_gnn_c1_b, L1_gnn_bn1_g, L1_gnn_bn1_b, L1_gnn_c2_w1, L1_gnn_c2_b1, L1_gnn_c2_w2, L1_gnn_c2_b2, L1_gnn_c2_g, L1_gnn_c2_b, L1_gnn_bn2_g, L1_gnn_bn2_b, L1_ffn_sW1, L1_ffn_sb1, L1_ffn_sW2, L1_ffn_sb2, L1_ffn_sW3, L1_ffn_sb3, L1_ffn_eW1, L1_ffn_eb1, L1_ffn_eW2, L1_ffn_eb2, L1_ffn_eW3, L1_ffn_eb3, L1_ffn_gW, L1_ffn_gb):
    import jax
    import jax.numpy as jnp

    def _L0_gnn_ref(x, edge_row, edge_col, edge_vals, eps, W1, b1, g1, be1, W2, b2, g2, be2):
        import jax, jax.numpy as jnp
        import numpy as np
        N = 6250
        E = 200000
        DI = 256
        DO = 256
        BN_EPS = 1e-05

        def _bn_relu(h, gamma, beta):
            mean = jnp.mean(h, axis=0)
            var = jnp.var(h, axis=0)
            hn = (h - mean) * jax.lax.rsqrt(var + BN_EPS)
            return jax.nn.relu(hn * gamma + beta)
        n = x.shape[0]
        msgs = edge_vals[:, None] * x[edge_col]
        agg = jax.ops.segment_sum(msgs, edge_row, num_segments=n)
        h = (1.0 + eps[0]) * x + agg
        h = _bn_relu(h @ W1 + b1, g1, be1)
        h = _bn_relu(h @ W2 + b2, g2, be2)
        return h

    def _L0_ffn_ref(x, Wr, br, ln_g, ln_b, W1, b1, W2, b2):
        import jax, jax.numpy as jnp
        import numpy as np
        TOP_K = 2
        LN_EPS = 1e-05
        B, S, D = x.shape
        N = B * S
        xt = x.reshape(N, D)
        logits = xt @ Wr + br
        probs = jax.nn.softmax(logits, axis=-1)
        top_p, top_idx = jax.lax.top_k(probs, TOP_K)
        weights = top_p / top_p.sum(axis=-1, keepdims=True)
        mu = xt.mean(axis=-1, keepdims=True)
        var = ((xt - mu) ** 2).mean(axis=-1, keepdims=True)
        xn = (xt - mu) * jax.lax.rsqrt(var + LN_EPS)
        xe = xn[None, :, :] * ln_g[:, None, :] + ln_b[:, None, :]
        h = jax.nn.gelu(jnp.einsum('end,edh->enh', xe, W1) + b1[:, None, :], approximate=False)
        y = jnp.einsum('enh,ehd->end', h, W2) + b2[:, None, :]
        y_tok = jnp.transpose(y, (1, 0, 2))
        sel = jnp.take_along_axis(y_tok, top_idx[:, :, None], axis=1)
        out = (weights[:, :, None] * sel).sum(axis=1)
        return out.reshape(B, S, D)

    def _L1_gnn_ref(x, hyperedge_index, hyperedge_weight, c1_w1, c1_b1, c1_w2, c1_b2, c1_g, c1_b, bn1_g, bn1_b, c2_w1, c2_b1, c2_w2, c2_b2, c2_g, c2_b, bn2_g, bn2_b):
        import jax, jax.numpy as jnp
        import numpy as np
        EPS = 1e-05

        def _bn(x, gamma, beta):
            m = jnp.mean(x, axis=0)
            v = jnp.mean((x - m) ** 2, axis=0)
            return gamma * (x - m) * jax.lax.rsqrt(v + EPS) + beta

        def _hconv(x, src, dst, ew, w1, b1, w2, b2, g, b):
            h = jax.nn.relu(x @ w1 + b1)
            msg = ew[:, None] * h[src]
            agg = jax.ops.segment_sum(msg, dst, num_segments=x.shape[0])
            h = agg @ w2 + b2
            return jax.nn.relu(_bn(h, g, b))
        src, dst = (hyperedge_index[0], hyperedge_index[1])
        residual = x
        h = _hconv(x, src, dst, hyperedge_weight, c1_w1, c1_b1, c1_w2, c1_b2, c1_g, c1_b)
        h = jax.nn.relu(_bn(h, bn1_g, bn1_b))
        h = _hconv(h, src, dst, hyperedge_weight, c2_w1, c2_b1, c2_w2, c2_b2, c2_g, c2_b)
        h = _bn(h, bn2_g, bn2_b)
        return jax.nn.relu(h + residual)

    def _L1_ffn_ref(x, sW1, sb1, sW2, sb2, sW3, sb3, eW1, eb1, eW2, eb2, eW3, eb3, gW, gb):
        import jax, jax.numpy as jnp
        import numpy as np
        B, A = (256, 8)
        IN, OUT = (256, 256)
        SH1, SH2 = (256, 128)
        EH1, EH2 = (128, 64)
        E, TOPK = (4, 2)

        def _shared_mlp(x, W1, b1, W2, b2, W3, b3):
            h = jax.nn.relu(x @ W1 + b1)
            h = jax.nn.relu(h @ W2 + b2)
            return h @ W3 + b3

        def _experts_mlp(x, eW1, eb1, eW2, eb2, eW3, eb3):
            h = jax.nn.relu(jnp.einsum('baf,efh->ebah', x, eW1) + eb1[:, None, None, :])
            h = jax.nn.relu(jnp.einsum('ebah,ehg->ebag', h, eW2) + eb2[:, None, None, :])
            o = jnp.einsum('ebag,ego->ebao', h, eW3) + eb3[:, None, None, :]
            return jnp.moveaxis(o, 0, -1)
        all_out = _experts_mlp(x, eW1, eb1, eW2, eb2, eW3, eb3)
        shared = _shared_mlp(x, sW1, sb1, sW2, sb2, sW3, sb3)
        gates = jax.nn.softmax(x @ gW + gb, axis=-1)
        topv, topi = jax.lax.top_k(gates, TOPK)
        topw = jax.nn.softmax(topv, axis=-1)
        sel = jnp.take_along_axis(all_out, topi[:, :, None, :], axis=-1)
        gated = jnp.sum(sel * topw[:, :, None, :], axis=-1)
        return shared + gated
    edge_index = jnp.stack([src, dst])
    x = x + _L0_gnn_ref(_layernorm(x, axis=-1), src, dst, edge_weight, L0_gnn_eps, L0_gnn_W1, L0_gnn_b1, L0_gnn_g1, L0_gnn_be1, L0_gnn_W2, L0_gnn_b2, L0_gnn_g2, L0_gnn_be2)
    x = x + _L0_ffn_ref(_layernorm(x, axis=-1)[None], L0_ffn_Wr, L0_ffn_br, L0_ffn_ln_g, L0_ffn_ln_b, L0_ffn_W1, L0_ffn_b1, L0_ffn_W2, L0_ffn_b2)[0]
    x = x + _L1_gnn_ref(_layernorm(x, axis=-1), edge_index, edge_weight, L1_gnn_c1_w1, L1_gnn_c1_b1, L1_gnn_c1_w2, L1_gnn_c1_b2, L1_gnn_c1_g, L1_gnn_c1_b, L1_gnn_bn1_g, L1_gnn_bn1_b, L1_gnn_c2_w1, L1_gnn_c2_b1, L1_gnn_c2_w2, L1_gnn_c2_b2, L1_gnn_c2_g, L1_gnn_c2_b, L1_gnn_bn2_g, L1_gnn_bn2_b)
    x = x + _L1_ffn_ref(_layernorm(x, axis=-1)[None], L1_ffn_sW1, L1_ffn_sb1, L1_ffn_sW2, L1_ffn_sb2, L1_ffn_sW3, L1_ffn_sb3, L1_ffn_eW1, L1_ffn_eb1, L1_ffn_eW2, L1_ffn_eb2, L1_ffn_eW3, L1_ffn_eb3, L1_ffn_gW, L1_ffn_gb)[0]
    return x

_drawn_inputs = setup_inputs


def setup_inputs(seed=0):
    import zlib

    import numpy as np

    out = dict(_drawn_inputs(seed))
    spreads = {'L0_gnn_b1': (0.0, 2.0),
     'L0_gnn_g1': (1.0, 0.2),
     'L0_gnn_be1': (0.0, 0.1),
     'L0_gnn_b2': (0.0, 2.0),
     'L0_gnn_g2': (1.0, 0.2),
     'L0_gnn_be2': (0.0, 0.1),
     'L0_ffn_br': (0.0, 0.1),
     'L0_ffn_ln_g': (1.0, 0.2),
     'L0_ffn_ln_b': (0.0, 0.1),
     'L0_ffn_b1': (0.0, 0.1),
     'L0_ffn_b2': (0.0, 0.1),
     'L1_gnn_c1_b1': (0.0, 0.1),
     'L1_gnn_c1_b2': (0.0, 2.0),
     'L1_gnn_c1_g': (1.0, 0.6),
     'L1_gnn_c1_b': (0.0, 0.269),
     'L1_gnn_bn1_g': (1.0, 0.2),
     'L1_gnn_bn1_b': (0.0, 0.1),
     'L1_gnn_c2_b1': (0.0, 0.1),
     'L1_gnn_c2_b2': (0.0, 2.0),
     'L1_gnn_c2_g': (1.0, 0.6),
     'L1_gnn_c2_b': (0.0, 0.1),
     'L1_gnn_bn2_g': (1.0, 0.2),
     'L1_gnn_bn2_b': (0.0, 0.272),
     'L1_ffn_sb1': (0.0, 0.8),
     'L1_ffn_sb2': (0.0, 0.465),
     'L1_ffn_sb3': (0.0, 0.1),
     'L1_ffn_eb1': (0.0, 2.0),
     'L1_ffn_eb2': (0.0, 0.8),
     'L1_ffn_eb3': (0.0, 0.1),
     'L1_ffn_gb': (0.0, 0.8)}
    factors = {'L1_ffn_eW1': 2.82}
    for name, (base, spread) in spreads.items():
        noise = np.random.default_rng([zlib.crc32(name.encode()), seed]).standard_normal(out[name].shape)
        drawn = base * np.exp(spread * noise) if base else spread * noise
        out[name] = jnp.asarray(drawn.astype(out[name].dtype))
    for name, factor in factors.items():
        out[name] = (out[name] * factor).astype(out[name].dtype)
    return out
```

```python
from contextlib import ExitStack

import numpy as np
import concourse.bass as bass
from concourse import mybir

F32 = mybir.dt.float32
I32 = mybir.dt.int32
BF16 = mybir.dt.bfloat16
ALU = mybir.AluOpType
ACT = mybir.ActivationFunctionType
AX = mybir.AxisListType

P = 128
N = 6250
D = 256
KD = D // P
NB = 50
FULL = N // P
REST = N - FULL * P
BLK = 2 * P
NJ = NB // 2
LAST = N - (NJ - 1) * BLK
EDGES = 100000
EPT = 784
EC = 7
ER = EPT // EC
G = 4
NG = EPT // G
RING = 7
EPS = 1e-5
PARTS = 5
PW = NB // PARTS
E8, H = 8, 1024
KH = H // P
TOK = 256
MT = (2 * N - E8) // TOK + E8
DUMP = MT * TOK
XS_ROWS = DUMP + 4 * P
BIG = 1e4


def take(eng, sem, n=1):
    eng.wait_ge(sem, n)
    eng.sem_inc(sem, -n)


def chain(eng, ins, sem):
    ins.then_inc(sem, 1)
    take(eng, sem)


class Chip:
    pass


def stage(nc, fn, name):
    with ExitStack() as ctx:
        tag, used = f"{name}{nc.next_id()}", []

        def sb(what, shape, dt=F32):
            return ctx.enter_context(nc.sbuf_tensor(f"{tag}_{what}", shape, dt))

        def sem(what):
            used.append(nc.alloc_semaphore(f"{tag}_{what}"))
            return used[-1]

        with nc.Block() as block:
            fn(block, sb, sem)
        nc.clear_and_free_semaphores(used)
        nc.all_engine_barrier()


def flat(t):
    return t[:].rearrange("p a b -> p (a b)")


def carve(area, start, shape):
    size = int(np.prod(shape))
    v = area[:, start:start + size]
    if len(shape) == 2:
        v = v.rearrange("p (a b) -> p a b", b=shape[1])
    if len(shape) == 3:
        v = v.rearrange("p (a b c) -> p a b c", b=shape[1], c=shape[2])
    return v


def tile_at(t, i):
    return t[:, bass.ds(i, 1), :].rearrange("p a d -> p (a d)")


def turn_lists(pe, c, lists, low_high, list_turned, list_copied, range_rows):
    n = 0
    for rows in lists:
        for k in range(EC):
            if n >= 2:
                pe.wait_ge(list_copied, n - 1)
            pe.transpose(c.ps[n % 2][:, 0:ER], rows[:, k, :], c.ident[0:ER, 0:ER]).then_inc(list_turned, 1)
            n += 1
    take(pe, range_rows, 2)
    for w in range(2):
        pe.transpose(c.ps[2][0:EC, w * P:w * P + ER], low_high[0:ER, w, :], c.ident[0:ER, 0:ER]).then_inc(list_turned, 1)


def copy_lists(dve, c, tables, keys, low_high, low_high_cols, range_f, range_i, list_turned, list_copied,
               range_rows, range_ready, v):
    for w, op in ((0, ALU.min), (1, ALU.max)):
        dve.tensor_reduce(low_high[0:ER, w, :], keys, AX.X, op).then_inc(range_rows, 1)
    n = 0
    for table in tables:
        for k in range(EC):
            dve.wait_ge(list_turned, n + 1)
            dve.tensor_copy(table[:, k * ER:(k + 1) * ER], c.ps[n % 2][:, 0:ER]).then_inc(list_copied, 1)
            n += 1
    dve.wait_ge(list_turned, n + 2)
    chain(dve, dve.tensor_scalar(low_high_cols[:], c.ps[2][0:EC, 0:2 * P].rearrange("c (w e) -> c w e", w=2)[:, :, 0:ER],
                                 0.0, float(N - 1), ALU.max, ALU.min), v)
    for w, op in ((0, ALU.min), (1, ALU.max)):
        chain(dve, dve.tensor_reduce(range_f[:, :, w], low_high_cols[:, w, :].rearrange("c (g t) -> c g t", t=G),
                                     AX.X, op), v)
    chain(dve, dve.tensor_scalar(range_f[:, :, 1], range_f[:, :, 1], float(P), None, ALU.add), v)
    chain(dve, dve.tensor_copy(range_i[:], range_f[:]), v)
    dve.tensor_scalar(range_i[:], range_i[:], P.bit_length() - 1, None, ALU.logical_shift_right).then_inc(range_ready, 1)


def place_ranges(sp, c, ranges, range_i, range_ready, range_out, range_in):
    sp.wait_ge(range_ready, 1)
    sp.dma_start(c.range_dram.rearrange("(c g) -> c g", c=EC), range_i[:].rearrange("c g w -> c (g w)")).then_inc(range_out, 16)
    sp.wait_ge(range_out, 16)
    sp.dma_start(ranges[:], c.range_dram[None, :]).then_inc(range_in, 16)
    sp.wait_ge(range_in, 16)


def range_buffers(sb):
    return (sb("low_high", [P, 2, EC]), sb("low_high_cols", [EC, 2, ER]), sb("range_f", [EC, NG // EC, 2]),
            sb("range_i", [EC, NG // EC, 2], I32))


def prepare(nc, c, a):
    def run(block, sb, sem):
        af, tf = flat(c.A), flat(c.T)
        names = ("src", "dst", "edge_weight")
        raw = [af[:, i * EC * P:(i + 1) * EC * P] for i in range(3)]
        raw = [raw[0].bitcast(I32), raw[1].bitcast(I32), raw[2]]
        asf = [tf[:, 0:EC * P], tf[:, EC * P:2 * EC * P], raw[2]]
        lists = [x[0:ER, :].rearrange("r (k e) -> r k e", e=P) for x in asf]
        prow = carve(tf, 2 * EC * P, (2, P))
        low_high, low_high_cols, range_f, range_i = range_buffers(sb)
        x_in, edges_in, par_in = sem("x_in"), sem("edges_in"), sem("par_in")
        pads, consts, floats, made, v = (sem(n) for n in ("pads", "consts", "floats", "made", "v"))
        list_turned, list_copied, par_turned = sem("list_turned"), sem("list_copied"), sem("par_turned")
        range_rows, range_ready, range_out, range_in = (sem(n) for n in ("range_rows", "range_ready", "range_out", "range_in"))
        cols, record_out = sem("cols"), sem("record_out")

        @block.sync
        def _(sp):
            sp.wait_ge(pads, 1)
            whole = (EC - 1) * ER
            tail = EDGES // P - whole
            for i, name in enumerate(names):
                e = a[name]
                sp.dma_start(raw[i][0:ER, 0:(EC - 1) * P].rearrange("r (c e) -> r c e", e=P),
                             e[0:whole * P].rearrange("(c r e) -> r c e", r=ER, e=P)).then_inc(edges_in, 16)
                sp.dma_start(raw[i][0:tail, (EC - 1) * P:EC * P],
                             e[whole * P:(whole + tail) * P].rearrange("(r e) -> r e", e=P)).then_inc(edges_in, 16)
                sp.dma_start(raw[i][tail:tail + 1, (EC - 1) * P:(EC - 1) * P + EDGES % P],
                             e[(whole + tail) * P:EDGES].rearrange("(r e) -> r e", r=1)).then_inc(edges_in, 16)
            sp.wait_ge(pads, 2)
            for half in range(2):
                lo, hi = half * FULL // 2, (half + 1) * FULL // 2
                sp.dma_start(c.X[:, lo:hi, :],
                             a["x"][lo * P:hi * P, :].rearrange("(t p) d -> p t d", p=P)).then_inc(x_in, 16)
            sp.dma_start(c.X[0:REST, FULL, :], a["x"][FULL * P:N, :]).then_inc(x_in, 16)
            sp.dma_start(c.eps[:], a["L0_gnn_eps"][None, :].to_broadcast([P, 1])).then_inc(x_in, 16)
            place_ranges(sp, c, c.dst_ranges, range_i, range_ready, range_out, range_in)
            sp.wait_ge(cols, 1)
            for lo, w, at in ((0, KD, 0), (KD * E8, KD, KD), (2 * KD * E8, KH, 2 * KD)):
                sp.dma_start(c.expert_dram[:, :, at:at + w].rearrange("e p w -> p e w"),
                             c.pcol[:, P + lo:P + lo + E8 * w].rearrange("p (e w) -> p e w", w=w)).then_inc(record_out, 16)
            sp.wait_ge(x_in, 64)
            sp.wait_ge(record_out, 48)

        @block.scalar
        def _(act):
            act.wait_ge(pads, 2)
            for name, (at, rows) in c.pat.items():
                ap = a[name]
                if len(ap.shape) == 2:
                    ap = ap.rearrange("a b -> (a b)")
                act.dma_start(prow[at % P:at % P + rows, at // P, :],
                              ap.rearrange("(r e) -> r e", e=P)).then_inc(par_in, 16)
            act.wait_ge(par_in, 16 * len(c.pat))

        @block.gpsimd
        def _(pool):
            pool.memset(c.ident[:], 0.0).then_inc(made, 1)
            pool.memset(c.upper[:], 1.0).then_inc(made, 1)
            pool.memset(c.ones[:], 1.0).then_inc(made, 1)
            pool.wait_ge(made, 3)
            pool.affine_select(out=c.ident[:], in_=c.ident[:], compare_op=ALU.not_equal, fill=1.0,
                               base=0, pattern=[[-1, P]], channel_multiplier=1).then_inc(consts, 1)
            pool.affine_select(out=c.upper[:], in_=c.upper[:], compare_op=ALU.is_gt, fill=0.0,
                               base=0, pattern=[[1, P]], channel_multiplier=-1).then_inc(consts, 1)
            pool.iota(c.iota[:], pattern=[[1, c.iota.shape[1]]], base=0, channel_multiplier=0,
                      allow_small_or_imprecise_dtypes=True).then_inc(consts, 1)
            pool.iota(c.node[:], pattern=[[P, NB]], base=0, channel_multiplier=1,
                      allow_small_or_imprecise_dtypes=True).then_inc(consts, 1)
            pool.wait_ge(consts, 4)

        @block.tensor
        def _(pe):
            pe.wait_ge(consts, 1)
            pe.wait_ge(floats, 2)
            turn_lists(pe, c, lists, low_high, list_turned, list_copied, range_rows)
            pe.wait_ge(par_in, 16 * len(c.pat))
            for w in range(2):
                pe.transpose(c.ps[3][:, w * P:w * P + P], prow[:, w, :], c.ident[:]).then_inc(par_turned, 1)

        @block.vector
        def _(dve):
            last = slice((EC - 1) * P, EC * P)
            chain(dve, dve.memset(raw[0][0:ER, last], 0), v)
            chain(dve, dve.memset(raw[1][0:ER, last], N - 1), v)
            dve.memset(raw[2][0:ER, last], 0.0).then_inc(pads, 1)
            chain(dve, dve.memset(prow, 0.0), v)
            chain(dve, dve.memset(c.X[:, FULL:NB, :], 0.0), v)
            dve.sem_inc(pads, 1)
            dve.wait_ge(edges_in, 9 * 16)
            dve.tensor_copy(asf[0][0:ER, :], raw[0][0:ER, :]).then_inc(floats, 1)
            dve.tensor_copy(asf[1][0:ER, :], raw[1][0:ER, :]).then_inc(floats, 1)
            dve.wait_ge(floats, 2)
            copy_lists(dve, c, (c.e_src, c.e_dst, c.e_w), lists[1], low_high, low_high_cols, range_f, range_i,
                       list_turned, list_copied, range_rows, range_ready, v)
            dve.wait_ge(par_turned, 2)
            dve.tensor_copy(c.pcol[:], c.ps[3][:, 0:2 * P]).then_inc(cols, 1)
            dve.wait_ge(x_in, 64)
            chain(dve, dve.tensor_scalar(c.eps[:], c.eps[:], 1.0, None, ALU.add), v)
    stage(nc, run, "prepare")


def sort_edges(nc, c):
    NT = FULL + 1
    RB = 512 // ER
    RW = 8
    RP = 7
    STEPS = EPT // (RP * RW)

    def run(block, sb, sem):
        af, tf = flat(c.A), flat(c.T)
        tile_f, tile_i, place = tf[:, 0:EPT], tf[:, EPT:2 * EPT].bitcast(I32), tf[:, 2 * EPT:3 * EPT]
        rec = carve(tf, 3 * EPT, (EPT, 4))
        words = NT * ER // 2
        mask = af[:, 0:words].bitcast(BF16).rearrange("p (b t) -> p b t", t=ER)
        prod = carve(af, words, (NT, ER))
        incl, keep = af[:, 3 * words:3 * words + RB * ER], af[:, 3 * words + RB * ER:3 * words + 2 * RB * ER]
        count, total = carve(af, 3 * words + 2 * RB * ER, (EC, NT)), carve(af, 3 * words + 2 * RB * ER + EC * NT, (EC, NT))
        start, before, hist = sb("start", [P, EC, NT]), sb("before", [P, NT]), sb("hist", [P, NT])
        upper, ones = sb("upper", [P, P], BF16), sb("ones", [P, P], BF16)
        ring_rec, ring_idx = sb("ring_rec", [P, RP, RW, 4]), sb("ring_idx", [P, RP, RW], I32)
        back = carve(af, 0, (EC, 4 * P))[0:ER]
        lists = [back.rearrange("r k (e f) -> r k e f", f=4)[:, :, :, i] for i in range(3)]
        low_high, low_high_cols, range_f, range_i = range_buffers(sb)
        v, counted, totals, mask_ready, chunk_placed = (sem(n) for n in ("v", "counted", "totals", "mask_ready", "chunk_placed"))
        ranked, bank_free = pair(sem, "ranked"), pair(sem, "bank_free")
        ring_ready, scattered = ([sem(f"{n}{h}") for h in range(RP)] for n in ("ring_ready", "scattered"))
        laid, copied, back_in = sem("laid"), sem("copied"), sem("back_in")
        list_turned, list_copied = sem("list_turned"), sem("list_copied")
        range_rows, range_ready, range_out, range_in = (sem(n) for n in ("range_rows", "range_ready", "range_out", "range_in"))
        groups = [(g % 2, g * RB, min(RB, NT - g * RB)) for g in range(-(-NT // RB))]

        def build_mask(dve, k):
            return dve.tensor_tensor(mask, c.iota[:, 0:NT][:, :, None].to_broadcast([P, NT, ER]),
                                     tile_f[:, bass.ds(k * ER, ER)][:, None, :].to_broadcast([P, NT, ER]), ALU.is_equal)

        @block.vector
        def _(dve):
            tt, ts = dve.tensor_tensor, dve.tensor_scalar
            dve.tensor_copy(upper[:], c.upper[:]).then_inc(laid, 1)
            dve.tensor_copy(ones[:], c.ones[:]).then_inc(laid, 1)
            chain(dve, dve.memset(rec, 0.0), v)
            for i, e in enumerate((c.e_src, c.e_dst, c.e_w)):
                dve.tensor_copy(rec[:, :, i], e[:]).then_inc(laid, 1)
            chain(dve, dve.memset(keep, 1.0), v)
            dve.memset(keep.rearrange("p (b t) -> p b t", t=ER)[:, :, 0:1], 0.0).then_inc(laid, 1)
            chain(dve, dve.tensor_copy(tile_i, c.e_src[:]), v)
            chain(dve, ts(tile_i, tile_i, P.bit_length() - 1, None, ALU.logical_shift_right), v)
            dve.tensor_copy(tile_f, tile_i).then_inc(laid, 1)
            take(dve, laid, 7)
            with dve.Fori(0, EC) as k:
                chain(dve, build_mask(dve, k), v)
                chain(dve, dve.tensor_reduce(count[:, bass.ds(k, 1), :].rearrange("p k b -> p (k b)"), mask, AX.X, ALU.add), v)
            dve.sem_inc(counted, 1)
            take(dve, totals)
            chain(dve, dve.tensor_copy(total.rearrange("p k b -> p (k b)"), c.ps[4][:, 0:EC * NT]), v)
            chain(dve, dve.tensor_reduce(hist[:], total.rearrange("p k b -> p b k"), AX.X, ALU.add), v)
            chain(dve, dve.tensor_tensor_scan(before[:], c.ones[:, 0:NT], hist[:], 0.0, ALU.mult, ALU.add), v)
            chain(dve, tt(start[:, 0, :], before[:], hist[:], ALU.subtract), v)
            for k in range(1, EC):
                chain(dve, tt(start[:, k, :], start[:, k - 1, :], total[:, k - 1, :], ALU.add), v)
            for s in range(2):
                dve.sem_inc(bank_free[s], 1)
            with dve.Fori(0, EC) as k:
                chain(dve, build_mask(dve, k), v)
                dve.sem_inc(mask_ready, 1)
                for s, b0, nb in groups:
                    w = nb * ER
                    rank, tot = c.ps[s][:, 0:w], c.ps[2 + s][:, 0:w]
                    out = prod[:, b0:b0 + nb, :]
                    flat_out = out.rearrange("p b t -> p (b t)")
                    take(dve, ranked[s])
                    chain(dve, dve.tensor_tensor_scan(incl[:, 0:w], keep[:, 0:w], tot, 0.0, ALU.mult, ALU.add), v)
                    chain(dve, tt(incl[:, 0:w], incl[:, 0:w], tot, ALU.subtract), v)
                    chain(dve, tt(flat_out, incl[:, 0:w], rank, ALU.add), v)
                    dve.sem_inc(bank_free[s], 1)
                    first = start[:, bass.ds(k, 1), b0:b0 + nb].rearrange("p k b -> p (k b)")
                    chain(dve, tt(out, out, first[:, :, None].to_broadcast([P, nb, ER]), ALU.add), v)
                    chain(dve, tt(out, out, mask[:, b0:b0 + nb, :], ALU.mult), v)
                chain(dve, dve.tensor_reduce(place[:, bass.ds(k * ER, ER)], prod.rearrange("p b t -> p t b"), AX.X, ALU.add), v)
                dve.sem_inc(chunk_placed, ER // RW)
            dve.wait_ge(back_in, 16)
            copy_lists(dve, c, (c.s_src, c.s_dst, c.s_w), lists[0], low_high, low_high_cols, range_f, range_i,
                       list_turned, list_copied, range_rows, range_ready, v)

        @block.tensor
        def _(pe):
            take(pe, counted)
            pe.matmul(c.ps[4][:, 0:EC * NT], c.ones[:], count.rearrange("p k b -> p (k b)"), start=True, stop=True).then_inc(totals, 1)
            with pe.Fori(0, EC):
                take(pe, mask_ready)
                for s, b0, nb in groups:
                    m = mask[:, b0:b0 + nb, :].rearrange("p b t -> p (b t)")
                    take(pe, bank_free[s])
                    pe.matmul(c.ps[s][:, 0:nb * ER], upper[:], m, start=True, stop=True)
                    pe.matmul(c.ps[2 + s][:, 0:nb * ER], ones[:], m, start=True, stop=True).then_inc(ranked[s], 1)
            pe.wait_ge(back_in, 16)
            turn_lists(pe, c, lists, low_high, list_turned, list_copied, range_rows)

        @block.scalar
        def _(act):
            def fill(i, h):
                take(act, chunk_placed)
                t = i * (RP * RW) + h * RW
                act.copy(ring_rec[:, h], rec[:, bass.ds(t, RW), :]).then_inc(copied, 1)
                act.copy(ring_idx[:, h], place[:, bass.ds(t, RW)]).then_inc(copied, 1)
                take(act, copied, 2)
                act.sem_inc(ring_ready[h], 1)

            for h in range(RP):
                fill(0, h)
            with act.Fori(1, STEPS) as i:
                for h in range(RP):
                    act.wait_ge(scattered[h], i * (16 * RW))
                    fill(i, h)

        @block.gpsimd
        def _(pool):
            with pool.Fori(0, STEPS):
                for h in range(RP):
                    take(pool, ring_ready[h])
                    for j in range(RW):
                        pool.indirect_dma_start(c.record_dram, bass.IndirectOffsetOnAxis(ap=ring_idx[:, h, j:j + 1], axis=0),
                                                ring_rec[:, h, j, :], None).then_inc(scattered[h], 16)

        @block.sync
        def _(sp):
            for h in range(RP):
                sp.wait_ge(scattered[h], STEPS * RW * 16)
            sp.dma_start(back, c.record_dram.rearrange("(k r e) f -> r k (e f)", r=ER, e=P)).then_inc(back_in, 16)
            place_ranges(sp, c, c.src_ranges, range_i, range_ready, range_out, range_in)
    stage(nc, run, "sort_edges")


def norm_stats(dve, act_go, act_done, src, st, c, v):
    with dve.Fori(0, NB) as t:
        dve.bn_stats(st[:, bass.ds(t, 1), :].rearrange("p a s -> p (a s)"), tile_at(src, t))
    dve.drain().then_inc(v, 1)
    take(dve, v)
    chain(dve, dve.tensor_tensor(c.mean[:], st[:, :, 1], st[:, :, 4], ALU.add), v)
    chain(dve, dve.tensor_scalar(c.mean[:], c.mean[:], 0.5, None, ALU.mult), v)
    chain(dve, dve.tensor_tensor(st[:, :, 0], st[:, :, 1], st[:, :, 4], ALU.subtract), v)
    chain(dve, dve.scalar_tensor_tensor(st[:, :, 1], st[:, :, 0], 0.25, st[:, :, 0], ALU.mult, ALU.mult), v)
    chain(dve, dve.tensor_tensor(st[:, :, 2], st[:, :, 2], st[:, :, 5], ALU.add), v)
    chain(dve, dve.scalar_tensor_tensor(c.rstd[:], st[:, :, 2], 1.0 / D, st[:, :, 1], ALU.mult, ALU.add), v)
    dve.tensor_scalar(c.rstd[:], c.rstd[:], EPS, None, ALU.add).then_inc(act_go, 1)
    take(dve, act_done)
    chain(dve, dve.reciprocal(c.rstd[:], c.rstd[:]), v)


def norm_tile(dve, out, src, c, t):
    return dve.tensor_scalar(out, tile_at(src, t), c.mean[:, bass.ds(t, 1)], c.rstd[:, bass.ds(t, 1)],
                             ALU.subtract, ALU.mult)


def root(act, go, done, c):
    take(act, go)
    act.sqrt(c.rstd[:], c.rstd[:]).then_inc(done, 1)


def input_norm(nc, c):
    def run(block, sb, sem):
        st = sb("st", [P, NB, 6])
        v, go, done, part, scaled = (sem(s) for s in ("v", "go", "done", "part", "scaled"))
        out = [sem(f"out{k}") for k in range(PARTS)]

        @block.vector
        def _(dve):
            norm_stats(dve, go, done, c.X, st, c, v)
            for k in range(PARTS):
                with dve.Fori(k * PW, (k + 1) * PW) as t:
                    norm_tile(dve, tile_at(c.A, t), c.X, c, t)
                dve.drain().then_inc(part, 1)

        @block.scalar
        def _(act):
            root(act, go, done, c)
            for k in range(PARTS):
                act.wait_ge(out[k], 16)
                rows = c.A[:, k * PW:(k + 1) * PW, :]
                act.activation(rows, rows, ACT.Identity, scale=c.eps[:, 0:1]).then_inc(scaled, 1)
            act.wait_ge(scaled, PARTS)

        @block.sync
        def _(sp):
            for k in range(PARTS):
                sp.wait_ge(part, k + 1)
                sp.dma_start(c.h_dram[k * PW * P:(k + 1) * PW * P, :].rearrange("(t p) d -> p t d", p=P),
                             c.A[:, k * PW:(k + 1) * PW, :]).then_inc(out[k], 16)
            for k in range(PARTS):
                sp.wait_ge(out[k], 16)
    stage(nc, run, "input_norm")


def segment_sum(nc, c, take_from, add_to, weight, ranges, clear, fill):
    def run(block, sb, sem):
        free = flat(c.T)[:, D + 3 * EPT:]
        msg = carve(free, 0, (RING * G, D))
        hot = carve(free, RING * G * D, (3, G, P))
        ring = sb("ring", [P, RING, G], I32)
        acc = c.ps[0:3]
        rings = lambda name: [sem(f"{name}{h}") for h in range(RING)]
        idx_ready, landed, slots_free = rings("idx_ready"), rings("landed"), rings("slots_free")
        hot_ready, summed = [sem(f"hot_ready{s}") for s in range(3)], [sem(f"summed{s}") for s in range(3)]
        v, zero, zeroed, filled = sem("v"), sem("zero"), sem("zeroed"), sem("filled")
        zeros = flat(c.T)[:, 0:D]

        def node_tiles(eng, g):
            lo = eng.value_load(ranges[0:1, bass.ds(g * 2, 1)], min_val=0, max_val=FULL)
            hi = eng.value_load(ranges[0:1, bass.ds(g * 2 + 1, 1)], min_val=1, max_val=FULL + 1)
            return lo, hi

        if fill:
            @block.sync
            def _(sp):
                sp.wait_ge(zeroed, 1)
                parts, share = 4, XS_ROWS // P // 4
                for k in range(parts):
                    sp.dma_start(c.xs_dram[k * share * P:(k + 1) * share * P, :].rearrange("(p t) d -> p t d", p=P),
                                 zeros[:, None, :].to_broadcast([P, share, D])).then_inc(filled, 16)
                sp.wait_ge(filled, 16 * parts)

        @block.gpsimd
        def _(pool):
            with pool.Fori(0, NG // RING):
                for h in range(RING):
                    take(pool, idx_ready[h])
                    for j in range(G):
                        pool.indirect_dma_start(msg[:, h * G + j, :], None, c.h_dram,
                                                bass.IndirectOffsetOnAxis(ap=ring[:, h, j:j + 1], axis=0)
                                                ).then_inc(landed[h], 16)

        @block.scalar
        def _(act):
            for h in range(RING):
                act.sem_inc(slots_free[h], 1)
            with act.Fori(0, NG // RING) as q:
                for h in range(RING):
                    take(act, slots_free[h])
                    act.copy(ring[:, h, :], take_from[:, bass.ds(q * (RING * G) + h * G, G)]).then_inc(idx_ready[h], 1)

        @block.tensor
        def _(pe):
            def products(h, s):
                take(pe, hot_ready[s], G)
                for j in range(G):
                    mm = pe.matmul(acc[s][:, 0:D], hot[:, s, j, :], msg[:, h * G + j, :],
                                   start=(j == 0), stop=(j == G - 1))
                mm.then_inc(summed[s], 1)

            with pe.Fori(0, NG // RING) as q:
                for h in range(RING):
                    lo, hi = node_tiles(pe, q * RING + h)
                    pe.wait_ge(landed[h], q * (16 * G) + 16 * G)
                    products(h, h % 2)
                    with pe.If(lo + 1 < hi):
                        with pe.Fori(lo + 1, hi):
                            products(h, 2)

        @block.vector
        def _(dve):
            def matrices(e, b, s):
                for j in range(G):
                    dve.tensor_scalar(hot[:, s, j, :], c.iota[:, bass.ds(b * P, P)], add_to[:, bass.ds(e + j, 1)],
                                      weight[:, bass.ds(e + j, 1)], ALU.is_equal, ALU.mult).then_inc(hot_ready[s], 1)

            def add(b, s):
                take(dve, summed[s])
                chain(dve, dve.tensor_tensor(tile_at(c.A, b), tile_at(c.A, b), acc[s][:, 0:D], ALU.add), v)

            def finish(e, h, lo, hi):
                add(lo, h % 2)
                with dve.If(lo + 1 < hi):
                    with dve.Fori(lo + 1, hi) as b:
                        matrices(e, b, 2)
                        add(b, 2)
                dve.sem_inc(slots_free[h], 1)

            if fill:
                dve.memset(zeros, 0.0).then_inc(zeroed, 1)
            if clear:
                chain(dve, dve.memset(c.A[:], 0.0), zero)
            with dve.Fori(0, NG // RING) as q:
                at = [q * (RING * G) + h * G for h in range(RING)]
                last = None
                for h in range(RING):
                    lo, hi = node_tiles(dve, q * RING + h)
                    matrices(at[h], lo, h % 2)
                    if last:
                        finish(*last)
                    last = (at[h], h, lo, hi)
                finish(*last)
    stage(nc, run, "segment_sum")


def blocks(eng, body):
    with eng.Fori(0, NJ // 2) as q:
        body(q * 2, 0)
        body(q * 2 + 1, 1)
    body(NJ - 1, 0)


def ahead(pe, first, second):
    first(0)
    with pe.Fori(0, NJ // 2) as q:
        first(1)
        second(q * 2, 0)
        first(0)
        second(q * 2 + 1, 1)
    second(NJ - 1, 0)


def pair(sem, name):
    return [sem(f"{name}{s}") for s in range(2)]


def cols_block(c, j):
    return c.T[:, :, bass.ds(j * BLK, BLK)]


def pcols(c, name, n=KD, skip=0):
    at = c.pat[name][0] + skip
    return c.pcol[:, at:at + n]


def turn_to_cols(pe, c, row, turn):
    for s in range(2):
        for k in range(KD):
            mm = pe.transpose(turn[:, k * BLK + s * P:k * BLK + (s + 1) * P], row[:, s, k * P:(k + 1) * P], c.ident[:])
    return mm


def store_cols(act, c, j, src, bias):
    for m in range(KD):
        ins = act.activation(c.T[:, m, bass.ds(j * BLK, BLK)], src[:, m * BLK:(m + 1) * BLK], ACT.Identity,
                             bias=bias[:, m:m + 1])
    return ins


def apply_affine(act, c, out, src, func):
    for m in range(KD):
        ins = act.activation(out[:, m, :], src[:, m, :], func, bias=c.affine[:, 1, m:m + 1], scale=c.affine[:, 0, m:m + 1])
    return ins


def product_cols(pe, w, rhs, out):
    for m in range(KD):
        for k in range(KD):
            mm = pe.matmul(out[:, m * BLK:(m + 1) * BLK], w[:, k, m * P:(m + 1) * P], rhs[:, k, :],
                           start=(k == 0), stop=(k == KD - 1))
    return mm


def stats_blocks(dve, c, stats, stored):
    def one(j, n):
        take(dve, stored)
        for m in range(KD):
            ins = dve.bn_stats(stats[:, m, bass.ds(j, 1), :].rearrange("p a s -> p (a s)"), c.T[:, m, bass.ds(j * BLK, n)])
        return ins
    return one


def finish_affine(dve, c, stats, agg, gamma, beta, go, done, v):
    for m in range(KD):
        chain(dve, dve.bn_aggr(agg[:, m, :], stats[:, m, :, :].rearrange("p j s -> p (j s)")), v)
    dve.tensor_scalar(c.affine[:, 0, :], agg[:, :, 1], EPS, None, ALU.add).then_inc(go, 1)
    take(dve, done)
    chain(dve, dve.reciprocal(c.affine[:, 0, :], c.affine[:, 0, :]), v)
    chain(dve, dve.tensor_tensor(c.affine[:, 0, :], c.affine[:, 0, :], gamma, ALU.mult), v)
    chain(dve, dve.tensor_tensor(c.affine[:, 1, :], agg[:, :, 0], c.affine[:, 0, :], ALU.mult), v)
    chain(dve, dve.tensor_tensor(c.affine[:, 1, :], beta, c.affine[:, 1, :], ALU.subtract), v)


def root_affine(act, c, go, done):
    take(act, go)
    act.sqrt(c.affine[:, 0, :], c.affine[:, 0, :]).then_inc(done, 1)


def aggregate_product(nc, c, w_dram, bias, gamma, beta):
    def run(block, sb, sem):
        w, row = sb("w", [P, KD, D]), [sb(f"row{s}", [P, 2, D]) for s in range(2)]
        stats, agg = sb("stats", [P, KD, NJ, 6]), sb("agg", [P, KD, 2])
        turn, out = c.ps[0:2], c.ps[2:4]
        w_in, v, go, done, kept, stored = (sem(n) for n in ("w_in", "v", "go", "done", "kept", "stored"))
        row_ready, row_free = pair(sem, "row_ready"), pair(sem, "row_free")
        turned, in_t, prod, out_free = pair(sem, "turned"), sem("in_t"), pair(sem, "prod"), pair(sem, "out_free")

        @block.sync
        def _(sp):
            sp.dma_start(w[:], w_dram.rearrange("(k p) n -> p k n", p=P)).then_inc(w_in, 16)
            sp.wait_ge(w_in, 16)

        @block.scalar
        def _(act):
            def rows(j, s):
                take(act, row_free[s])
                act.copy(row[s][:], c.A[:, bass.ds(j * 2, 2), :]).then_inc(row_ready[s], 1)

            def store(j, s):
                take(act, prod[s])
                chain(act, store_cols(act, c, j, out[s], bias), kept)
                act.sem_inc(out_free[s], 1)
                act.sem_inc(stored, 1)

            rows(0, 0)
            with act.Fori(0, NJ // 2) as q:
                rows(q * 2 + 1, 1)
                store(q * 2, 0)
                rows(q * 2 + 2, 0)
                store(q * 2 + 1, 1)
            store(NJ - 1, 0)
            root_affine(act, c, go, done)

        @block.tensor
        def _(pe):
            def turn_rows(s):
                take(pe, row_ready[s])
                turn_to_cols(pe, c, row[s], turn[s]).then_inc(turned[s], 1)

            def product(j, s):
                take(pe, in_t)
                take(pe, out_free[s])
                product_cols(pe, w, cols_block(c, j), out[s]).then_inc(prod[s], 1)

            pe.wait_ge(w_in, 16)
            ahead(pe, turn_rows, product)

        @block.vector
        def _(dve):
            def copy(j, s):
                take(dve, turned[s])
                dve.sem_inc(row_free[s], 1)
                dve.tensor_copy(cols_block(c, j), turn[s][:].rearrange("p (k n) -> p k n", k=KD)).then_inc(in_t, 1)

            stat = stats_blocks(dve, c, stats, stored)
            for s in range(2):
                dve.sem_inc(row_free[s], 1)
                dve.sem_inc(out_free[s], 1)
            copy(0, 0)
            with dve.Fori(0, NJ // 2) as q:
                copy(q * 2 + 1, 1)
                stat(q * 2, BLK)
                copy(q * 2 + 2, 0)
                stat(q * 2 + 1, BLK)
            chain(dve, stat(NJ - 1, LAST), v)
            finish_affine(dve, c, stats, agg, gamma, beta, go, done, v)
    stage(nc, run, "aggregate_product")


def norm_product(nc, c, w_dram, bias, gamma, beta):
    def run(block, sb, sem):
        w = sb("w", [P, KD, D])
        stats, agg = sb("stats", [P, KD, NJ, 6]), sb("agg", [P, KD, 2])
        out = c.ps[2:4]
        w_in, v, go, done, kept, stored = (sem(n) for n in ("w_in", "v", "go", "done", "kept", "stored"))
        normed, prod, out_free = sem("normed"), pair(sem, "prod"), pair(sem, "out_free")

        @block.sync
        def _(sp):
            sp.dma_start(w[:], w_dram.rearrange("(k p) n -> p k n", p=P)).then_inc(w_in, 16)
            sp.wait_ge(w_in, 16)

        @block.scalar
        def _(act):
            def norm(j, s):
                apply_affine(act, c, cols_block(c, j), cols_block(c, j), ACT.Relu).then_inc(normed, 1)

            def store(j, s):
                take(act, prod[s])
                chain(act, store_cols(act, c, j, out[s], bias), kept)
                act.sem_inc(out_free[s], 1)
                act.sem_inc(stored, 1)

            norm(0, 0)
            with act.Fori(0, NJ // 2) as q:
                norm(q * 2 + 1, 1)
                store(q * 2, 0)
                norm(q * 2 + 2, 0)
                store(q * 2 + 1, 1)
            store(NJ - 1, 0)
            root_affine(act, c, go, done)

        @block.tensor
        def _(pe):
            def product(j, s):
                take(pe, normed)
                take(pe, out_free[s])
                product_cols(pe, w, cols_block(c, j), out[s]).then_inc(prod[s], 1)

            pe.wait_ge(w_in, 16)
            blocks(pe, product)

        @block.vector
        def _(dve):
            stat = stats_blocks(dve, c, stats, stored)
            for s in range(2):
                dve.sem_inc(out_free[s], 1)
            with dve.Fori(0, NJ - 1) as j:
                stat(j, BLK)
            chain(dve, stat(NJ - 1, LAST), v)
            finish_affine(dve, c, stats, agg, gamma, beta, go, done, v)
    stage(nc, run, "norm_product")


def norm_relu(nc, c, gamma, beta):
    def run(block, sb, sem):
        stats, agg = sb("stats", [P, KD, NJ, 6]), sb("agg", [P, KD, 2])
        v, go, done, stored = (sem(n) for n in ("v", "go", "done", "stored"))

        @block.scalar
        def _(act):
            with act.Fori(0, NJ) as j:
                apply_affine(act, c, cols_block(c, j), cols_block(c, j), ACT.Relu).then_inc(stored, 1)
            root_affine(act, c, go, done)

        @block.vector
        def _(dve):
            stat = stats_blocks(dve, c, stats, stored)
            with dve.Fori(0, NJ - 1) as j:
                stat(j, BLK)
            chain(dve, stat(NJ - 1, LAST), v)
            finish_affine(dve, c, stats, agg, gamma, beta, go, done, v)
    stage(nc, run, "norm_relu")


def norm_to_rows(nc, c, residual):
    def run(block, sb, sem):
        col = [sb(f"col{s}", [P, KD, BLK]) for s in range(2)]
        sum_ = sb("sum", [P, 2, D])
        turn = c.ps[0:2]
        ready, free, turned, v = pair(sem, "ready"), pair(sem, "free"), pair(sem, "turned"), sem("v")
        func = ACT.Identity if residual else ACT.Relu

        @block.scalar
        def _(act):
            def norm(j, s):
                take(act, free[s])
                apply_affine(act, c, col[s], cols_block(c, j), func).then_inc(ready[s], 1)
            blocks(act, norm)

        @block.tensor
        def _(pe):
            def turn_cols(j, s):
                take(pe, ready[s])
                for q in range(2):
                    for k in range(KD):
                        mm = pe.transpose(turn[s][:, q * D + k * P:q * D + (k + 1) * P],
                                          col[s][:, k, q * P:(q + 1) * P], c.ident[:])
                mm.then_inc(turned[s], 1)
            blocks(pe, turn_cols)

        @block.vector
        def _(dve):
            for s in range(2):
                dve.sem_inc(free[s], 1)

            def add(j, s):
                x = c.X[:, bass.ds(j * 2, 2), :]
                h = turn[s][:].rearrange("p (t d) -> p t d", t=2)
                if residual:
                    for q in range(2):
                        norm_tile(dve, sum_[:, q, :], c.X, c, j * 2 + q).then_inc(v, 1)
                    take(dve, v, 2)
                    take(dve, turned[s])
                    chain(dve, dve.tensor_tensor(sum_[:], sum_[:], h, ALU.add), v)
                    chain(dve, dve.scalar_tensor_tensor(x, sum_[:], 0.0, x, ALU.max, ALU.add), v)
                else:
                    take(dve, turned[s])
                    chain(dve, dve.tensor_tensor(x, x, h, ALU.add), v)
                dve.sem_inc(free[s], 1)
            blocks(dve, add)
    stage(nc, run, "norm_to_rows")


def message_rows(nc, c, w_dram, b_dram, from_x):
    def run(block, sb, sem):
        w, bias = sb("w", [P, KD, D]), sb("bias", [P, D])
        col = [sb(f"col{s}", [P, KD, BLK]) for s in range(2)]
        row = [sb(f"row{s}", [P, 2, D]) for s in range(2)]
        st = sb("st", [P, NB, 6])
        rows = c.A
        turn, out = c.ps[0:2], c.ps[2:4]
        w_in, v, go, done, kept, stored = (sem(n) for n in ("w_in", "v", "go", "done", "kept", "stored"))
        h_out = sem("h_out")
        row_ready, turned, col_ready, col_free = (pair(sem, n) for n in ("row_ready", "turned", "col_ready", "col_free"))
        prod, out_free, added = pair(sem, "prod"), pair(sem, "out_free"), sem("added")

        @block.sync
        def _(sp):
            sp.dma_start(w[:], w_dram.rearrange("(k p) n -> p k n", p=P)).then_inc(w_in, 16)
            sp.dma_start(bias[:], b_dram[None, :].to_broadcast([P, D])).then_inc(w_in, 16)
            sp.wait_ge(w_in, 32)
            with sp.Fori(0, NJ) as j:
                take(sp, stored)
                sp.dma_start(c.h_dram[bass.ds(j * BLK, BLK), :].rearrange("(t p) d -> p t d", p=P),
                             rows[:, bass.ds(j * 2, 2), :]).then_inc(h_out, 16)
            sp.wait_ge(h_out, 16 * NJ)

        @block.scalar
        def _(act):
            if from_x:
                root(act, go, done, c)
            else:
                def norm(j, s):
                    take(act, col_free[s])
                    apply_affine(act, c, col[s], cols_block(c, j), ACT.Relu).then_inc(col_ready[s], 1)

            def relu(j):
                take(act, added)
                r = rows[:, bass.ds(j * 2, 2), :]
                act.activation(r, r, ACT.Relu).then_inc(stored, 1)

            if from_x:
                with act.Fori(0, NJ) as j:
                    relu(j)
            else:
                norm(0, 0)
                with act.Fori(0, NJ // 2) as q:
                    norm(q * 2 + 1, 1)
                    relu(q * 2)
                    norm(q * 2 + 2, 0)
                    relu(q * 2 + 1)
                relu(NJ - 1)

        @block.tensor
        def _(pe):
            def turn_rows(s):
                take(pe, row_ready[s])
                turn_to_cols(pe, c, row[s], turn[s]).then_inc(turned[s], 1)

            def product(j, s):
                take(pe, col_ready[s])
                take(pe, out_free[s])
                for q in range(2):
                    for k in range(KD):
                        mm = pe.matmul(out[s][:, q * D:(q + 1) * D], col[s][:, k, q * P:(q + 1) * P], w[:, k, :],
                                       start=(k == 0), stop=(k == KD - 1))
                mm.then_inc(prod[s], 1)

            pe.wait_ge(w_in, 32)
            if from_x:
                ahead(pe, turn_rows, product)
            else:
                blocks(pe, product)

        @block.vector
        def _(dve):
            def norm(j, s):
                for q in range(2):
                    ins = norm_tile(dve, row[s][:, q, :], c.X, c, j * 2 + q)
                ins.then_inc(row_ready[s], 1)

            def copy(s):
                take(dve, turned[s])
                take(dve, col_free[s])
                dve.tensor_copy(col[s][:], turn[s][:].rearrange("p (k n) -> p k n", k=KD)).then_inc(col_ready[s], 1)

            def add(j, s):
                take(dve, prod[s])
                dve.sem_inc(col_free[s], 1)
                for q in range(2):
                    dve.tensor_tensor(tile_at(rows, j * 2 + q), out[s][:, q * D:(q + 1) * D], bias[:], ALU.add).then_inc(kept, 1)
                take(dve, kept, 2)
                dve.sem_inc(out_free[s], 1)
                dve.sem_inc(added, 1)

            for s in range(2):
                dve.sem_inc(col_free[s], 1)
                dve.sem_inc(out_free[s], 1)
            dve.wait_ge(w_in, 32)
            if from_x:
                norm_stats(dve, go, done, c.X, st, c, v)
                norm(0, 0)
                norm(1, 1)
                copy(0)
                with dve.Fori(0, NJ // 2 - 1) as q:
                    norm(q * 2 + 2, 0)
                    copy(1)
                    add(q * 2, 0)
                    norm(q * 2 + 3, 1)
                    copy(0)
                    add(q * 2 + 1, 1)
                norm(NJ - 1, 0)
                copy(1)
                add(NJ - 3, 0)
                copy(0)
                add(NJ - 2, 1)
                add(NJ - 1, 0)
            else:
                blocks(dve, add)
    stage(nc, run, "message_rows")


def bcast(ap, n):
    return ap[:, :, None].to_broadcast([ap.shape[0], ap.shape[1], n])


def router(nc, c, a, wr_name, br_name, ne, moe):
    def run(block, sb, sem):
        wr, br = sb("wr", [P, KD, ne]), sb("br", [P, ne])
        row = [sb(f"row{s}", [P, 2, D]) for s in range(2)]
        col = [sb(f"col{s}", [P, KD, BLK]) for s in range(2)]
        work = flat(c.A) if not moe else flat(c.T)
        n3 = NB * ne
        logit, prob, eid, cand, pick1, pick2 = (carve(work, i * n3, (NB, ne)) for i in range(6))
        small = [carve(work, 6 * n3 + i * NB, (NB,)) for i in range(12)]
        top, total, p1, p2, first, q1, q2 = small[:7]
        rank, tot, cum, pos = (carve(work, 3600 + i * n3, (NB, ne)) for i in range(4))
        cum2 = carve(work, 3600 + 4 * n3, (NB, ne))
        st = sb("st", [P, NB, 6])
        turn, lg = c.ps[0:2], c.ps[2:4]
        w_in, v, go, done = (sem(n) for n in ("w_in", "v", "go", "done"))
        row_ready, turned, col_ready, col_free, lg_ready = (pair(sem, n) for n in ("row_ready", "turned", "col_ready", "col_free", "lg_ready"))
        iota_done, exp_go, exp_done, kept = (sem(n) for n in ("iota_done", "exp_go", "exp_done", "kept"))
        rank_go, rank_done = sem("rank_go"), sem("rank_done")
        x_ready, scattered, in_t = pair(sem, "x_ready"), pair(sem, "scattered"), sem("in_t")
        xr, ring = [sb(f"xr{s}", [P, D]) for s in range(2)], [sb(f"ring{s}", [P, 2], I32) for s in range(2)]
        idx = sb("idx", [P, NB, 2]) if moe else None
        end, endi = sb("end", [P, E8]), sb("endi", [P, E8], I32)
        base = sb("base", [P, E8])
        tiles = sb("tiles", [P, MT]) if moe else None
        tmp_t = sb("tmp_t", [P, MT]) if moe else None

        @block.sync
        def _(sp):
            sp.dma_start(wr[:], a[wr_name].rearrange("(k p) n -> p k n", p=P)).then_inc(w_in, 16)
            sp.dma_start(br[:], a[br_name][None, :].to_broadcast([P, ne])).then_inc(w_in, 16)
            sp.wait_ge(w_in, 32)

        @block.gpsimd
        def _(pool):
            pool.iota(eid, pattern=[[0, NB], [1, ne]], base=0, channel_multiplier=0,
                      allow_small_or_imprecise_dtypes=True).then_inc(iota_done, 1)
            if moe:
                pool.iota(tiles[:], pattern=[[1, MT]], base=0, channel_multiplier=0,
                          allow_small_or_imprecise_dtypes=True).then_inc(iota_done, 1)

                def scatter(s):
                    take(pool, x_ready[s])
                    for i in range(2):
                        pool.indirect_dma_start(c.xs_dram, bass.IndirectOffsetOnAxis(ap=ring[s][:, i:i + 1], axis=0),
                                                xr[s][:], None).then_inc(scattered[s], 16)
                with pool.Fori(0, NB // 2):
                    scatter(0)
                    scatter(1)
                for s in range(2):
                    pool.wait_ge(scattered[s], 16 * NB)
            else:
                pool.wait_ge(iota_done, 1)

        @block.scalar
        def _(act):
            root(act, go, done, c)
            if moe:
                root(act, go, done, c)
            if not moe:
                def to_t(j, s):
                    take(act, in_t)
                    chain(act, act.copy(cols_block(c, j), col[s][:]), kept)
                    act.sem_inc(col_free[s], 1)
                blocks(act, to_t)
            take(act, exp_go)
            act.activation(prob, logit, ACT.Exp).then_inc(exp_done, 1)
            if not moe:
                take(act, exp_go)
                act.activation(q1, q1, ACT.Exp).then_inc(exp_done, 1)
                act.activation(q2, q2, ACT.Exp).then_inc(exp_done, 1)

        @block.tensor
        def _(pe):
            def turn_rows(s):
                take(pe, row_ready[s])
                turn_to_cols(pe, c, row[s], turn[s]).then_inc(turned[s], 1)

            def logits(j, s):
                take(pe, col_ready[s])
                for q in range(2):
                    for k in range(KD):
                        mm = pe.matmul(lg[s][:, q * ne:(q + 1) * ne], col[s][:, k, q * P:(q + 1) * P], wr[:, k, :],
                                       start=(k == 0), stop=(k == KD - 1))
                mm.then_inc(lg_ready[s], 1)

            pe.wait_ge(w_in, 32)
            ahead(pe, turn_rows, logits)
            if moe:
                take(pe, rank_go)
                pe.matmul(c.ps[4][:, 0:n3], c.upper[:], cand.rearrange("p t e -> p (t e)"), start=True, stop=True)
                pe.matmul(c.ps[5][:, 0:n3], c.ones[:], cand.rearrange("p t e -> p (t e)"), start=True, stop=True).then_inc(rank_done, 1)

        @block.vector
        def _(dve):
            tt, ts = dve.tensor_tensor, dve.tensor_scalar
            norm_stats(dve, go, done, c.X, st, c, v)
            src = c.X
            if moe:
                with dve.Fori(0, NB) as t:
                    norm_tile(dve, tile_at(c.A, t), c.X, c, t)
                dve.drain().then_inc(v, 1)
                take(dve, v)
                norm_stats(dve, go, done, c.A, st, c, v)

            def rows(j, s):
                for q in range(2):
                    if moe:
                        ins = dve.tensor_copy(row[s][:, q, :], tile_at(c.A, j * 2 + q))
                    else:
                        ins = norm_tile(dve, row[s][:, q, :], c.X, c, j * 2 + q)
                ins.then_inc(row_ready[s], 1)

            def copy(s):
                take(dve, turned[s])
                if not moe:
                    take(dve, col_free[s])
                chain(dve, dve.tensor_copy(col[s][:], turn[s][:].rearrange("p (k n) -> p k n", k=KD)), v)
                dve.sem_inc(col_ready[s], 1)
                if not moe:
                    dve.sem_inc(in_t, 1)

            def read(j, s):
                take(dve, lg_ready[s])
                for q in range(2):
                    tt(logit[:, bass.ds(j * 2 + q, 1), :].rearrange("p t e -> p (t e)"),
                       lg[s][:, q * ne:(q + 1) * ne], br[:], ALU.add).then_inc(v, 1)
                take(dve, v, 2)

            if not moe:
                for s in range(2):
                    dve.sem_inc(col_free[s], 1)
            dve.wait_ge(w_in, 32)
            rows(0, 0)
            rows(1, 1)
            copy(0)
            with dve.Fori(0, NJ // 2 - 1) as q:
                rows(q * 2 + 2, 0)
                copy(1)
                read(q * 2, 0)
                rows(q * 2 + 3, 1)
                copy(0)
                read(q * 2 + 1, 1)
            rows(NJ - 1, 0)
            copy(1)
            read(NJ - 3, 0)
            copy(0)
            read(NJ - 2, 1)
            read(NJ - 1, 0)

            dve.wait_ge(iota_done, 2 if moe else 1)
            chain(dve, dve.tensor_reduce(top, logit, AX.X, ALU.max), v)
            tt(logit, logit, bcast(top, ne), ALU.subtract).then_inc(exp_go, 1)
            take(dve, exp_done)
            chain(dve, dve.tensor_reduce(total, prob, AX.X, ALU.add), v)
            chain(dve, dve.reciprocal(total, total), v)
            chain(dve, tt(prob, prob, bcast(total, ne), ALU.mult), v)

            def choose(pick, p):
                chain(dve, dve.tensor_reduce(p, prob, AX.X, ALU.max), v)
                chain(dve, tt(cand, prob, bcast(p, ne), ALU.is_equal), v)
                chain(dve, dve.scalar_tensor_tensor(cand, cand, -BIG, eid, ALU.mult, ALU.add), v)
                chain(dve, dve.tensor_reduce(first, cand, AX.X, ALU.min), v)
                chain(dve, tt(pick, cand, bcast(first, ne), ALU.is_equal), v)

            choose(pick1, p1)
            chain(dve, dve.scalar_tensor_tensor(prob, pick1, -2.0, prob, ALU.mult, ALU.add), v)
            choose(pick2, p2)
            if moe:
                chain(dve, tt(total, p1, p2, ALU.add), v)
                chain(dve, dve.reciprocal(total, total), v)
                chain(dve, tt(c.pick[:, :, 0], p1, total, ALU.mult), v)
                chain(dve, tt(c.pick[:, :, 1], p2, total, ALU.mult), v)
            else:
                chain(dve, tt(q1, p1, p1, ALU.subtract), v)
                tt(q2, p2, p1, ALU.subtract).then_inc(exp_go, 1)
                take(dve, exp_done, 2)
                chain(dve, tt(total, q1, q2, ALU.add), v)
                chain(dve, dve.reciprocal(total, total), v)
                chain(dve, tt(q1, q1, total, ALU.mult), v)
                chain(dve, tt(q2, q2, total, ALU.mult), v)
                chain(dve, tt(pick1, pick1, bcast(q1, ne), ALU.mult), v)
                chain(dve, tt(pick2, pick2, bcast(q2, ne), ALU.mult), v)
                chain(dve, tt(c.gate[:], pick1, pick2, ALU.add), v)
                return

            real, pad_at = small[7], small[8]
            chain(dve, ts(real, c.node[:], float(N), None, ALU.is_lt), v)
            chain(dve, tt(pick1, pick1, bcast(real, ne), ALU.mult), v)
            chain(dve, tt(pick2, pick2, bcast(real, ne), ALU.mult), v)
            tt(cand, pick1, pick2, ALU.add).then_inc(rank_go, 1)
            take(dve, rank_done)
            chain(dve, dve.tensor_copy(tot.rearrange("p t e -> p (t e)"), c.ps[5][:, 0:n3]), v)
            chain(dve, dve.tensor_copy(cum, tot), v)
            here, there = cum, cum2
            step = 1
            while step < NB:
                chain(dve, dve.tensor_copy(there[:, 0:step, :], here[:, 0:step, :]), v)
                chain(dve, tt(there[:, step:NB, :], here[:, step:NB, :], here[:, 0:NB - step, :], ALU.add), v)
                here, there = there, here
                step *= 2
            chain(dve, ts(end[:], here[:, NB - 1, :], 1.0, float(TOK - 1), ALU.max, ALU.add), v)
            chain(dve, dve.tensor_copy(endi[:], end[:]), v)
            chain(dve, ts(endi[:], endi[:], TOK.bit_length() - 1, None, ALU.logical_shift_right), v)
            chain(dve, dve.tensor_copy(end[:], endi[:]), v)
            for e in range(1, E8):
                chain(dve, tt(end[:, e:e + 1], end[:, e:e + 1], end[:, e - 1:e], ALU.add), v)
            chain(dve, dve.memset(base[:, 0:1], 0.0), v)
            chain(dve, ts(base[:, 1:E8], end[:, 0:E8 - 1], float(TOK), None, ALU.mult), v)
            chain(dve, tt(pos, here, tot, ALU.subtract), v)
            chain(dve, tt(pos.rearrange("p t e -> p (t e)"), pos.rearrange("p t e -> p (t e)"), c.ps[4][:, 0:n3], ALU.add), v)
            chain(dve, tt(pos, pos, base[:, None, :].to_broadcast([P, NB, E8]), ALU.add), v)
            chain(dve, ts(pad_at, c.node[:], float(DUMP - (NB - 2) * P), None, ALU.add), v)
            chain(dve, ts(real, real, -1.0, 1.0, ALU.mult, ALU.add), v)
            chain(dve, tt(pad_at, pad_at, real, ALU.mult), v)
            for i, pick in enumerate((pick1, pick2)):
                chain(dve, tt(pick, pick, pos, ALU.mult), v)
                chain(dve, dve.tensor_reduce(idx[:, :, i], pick, AX.X, ALU.add), v)
                chain(dve, dve.scalar_tensor_tensor(first, real, float(i * 2 * P), pad_at, ALU.mult, ALU.add), v)
                chain(dve, tt(idx[:, :, i], idx[:, :, i], first, ALU.add), v)
            chain(dve, dve.tensor_copy(c.slot[:], idx[:]), v)
            chain(dve, ts(tmp_t[:], tiles[:], end[:, 0:1], None, ALU.is_ge), v)
            for e in range(1, E8 - 1):
                chain(dve, dve.scalar_tensor_tensor(tmp_t[:], tiles[:], end[:, e:e + 1], tmp_t[:], ALU.is_ge, ALU.add), v)
            chain(dve, dve.tensor_copy(c.tile_expert[:], tmp_t[:]), v)

            def send(t, s):
                dve.tensor_copy(ring[s][:], c.slot[:, bass.ds(t, 1), :].rearrange("p t i -> p (t i)")).then_inc(v, 1)
                norm_tile(dve, xr[s][:], c.A, c, t).then_inc(v, 1)
                take(dve, v, 2)
                dve.sem_inc(x_ready[s], 1)
            send(0, 0)
            send(1, 1)
            with dve.Fori(1, NB // 2) as q:
                for s in range(2):
                    dve.wait_ge(scattered[s], q * 32)
                    send(q * 2 + s, s)
    stage(nc, run, "router")


def expert_ffn(nc, c, a):
    SLOTS = 4
    STEPS = MT // SLOTS
    LOADS = 5 * 16

    def run(block, sb, sem):
        tf, af = flat(c.T), flat(c.A)
        WW = KD * H
        places = [(tf, 0), (tf, 2 * WW), (af, 0), (af, 2 * WW)]
        w1 = [carve(area, o, (KD, H)) for area, o in places]
        w2 = [carve(area, o + WW, (KH, D)) for area, o in places]
        hid = carve(tf, 4 * WW, (KH, TOK))
        xs = [carve(tf, 4 * WW + KH * TOK + s * 2 * D, (2, D)) for s in range(SLOTS)]
        rest = af[:, 4 * WW:]
        ys = [carve(rest, s * 2 * D, (2, D)) for s in range(SLOTS)]
        b2 = [carve(rest, (2 * SLOTS + s) * D, (D,)) for s in range(SLOTS)]
        xe = carve(rest, 3 * SLOTS * D, (KD, TOK))
        par = [carve(rest, 3 * SLOTS * D + KD * TOK + s * (2 * KD + KH), (2 * KD + KH,)) for s in range(SLOTS)]
        turn, ph, py = c.ps[0], c.ps[1:3], c.ps[3:5]
        slots = lambda name: [sem(f"{name}{s}") for s in range(SLOTS)]
        slot_in, y_done, y_free, y_out = (slots(n) for n in ("slot_in", "y_done", "y_free", "y_out"))
        turned, xe_ready, h_ready, g_ready, y_read = (sem(n) for n in ("turned", "xe_ready", "h_ready", "g_ready", "y_read"))
        v, y_sum, pad_out = sem("v"), sem("y_sum"), sem("pad_out")

        @block.sync
        def _(sp):
            def load(i, s):
                e = sp.value_load(c.tile_expert[0:1, bass.ds(i, 1)], min_val=0, max_val=E8 - 1)
                one = lambda t: t[bass.ds(e, 1)]
                sp.dma_start(xs[s], c.xs_dram[bass.ds(i * TOK, TOK), :].rearrange("(t p) d -> p t d", p=P)).then_inc(slot_in[s], 16)
                sp.dma_start(w1[s], one(a["L0_ffn_W1"]).rearrange("e (k p) h -> p (e k) h", p=P)).then_inc(slot_in[s], 16)
                sp.dma_start(w2[s], one(a["L0_ffn_W2"]).rearrange("e (k p) d -> p (e k) d", p=P)).then_inc(slot_in[s], 16)
                sp.dma_start(par[s], one(c.expert_dram).rearrange("e p w -> p (e w)")).then_inc(slot_in[s], 16)
                sp.dma_start(b2[s], one(a["L0_ffn_b2"]).to_broadcast([P, D])).then_inc(slot_in[s], 16)

            def store(q, s):
                take(sp, y_done[s])
                sp.dma_start(c.ys_dram[bass.ds((q * SLOTS + s) * TOK, TOK), :].rearrange("(t p) d -> p t d", p=P),
                             ys[s]).then_inc(y_out[s], 16)

            for s in range(SLOTS):
                load(s, s)
            with sp.Fori(0, STEPS - 1) as q:
                for s in range(SLOTS):
                    store(q, s)
                    load((q + 1) * SLOTS + s, s)
                    sp.wait_ge(y_out[s], q * 16 + 16)
                    sp.sem_inc(y_free[s], 1)
            for s in range(SLOTS):
                store(STEPS - 1, s)
            sp.dma_start(c.ys_dram[DUMP:XS_ROWS, :], c.xs_dram[DUMP:XS_ROWS, :]).then_inc(pad_out, 16)
            for s in range(SLOTS):
                sp.wait_ge(y_out[s], 16 * STEPS)
            sp.wait_ge(pad_out, 16)

        @block.scalar
        def _(act):
            with act.Fori(0, STEPS) as q:
                for s in range(SLOTS):
                    for k in range(KH):
                        take(act, h_ready)
                        if k == 0:
                            act.wait_ge(slot_in[s], q * LOADS + LOADS)
                        act.activation(hid[:, k, :], ph[k % 2][:, 0:TOK], ACT.Gelu,
                                       bias=par[s][:, 2 * KD + k:2 * KD + k + 1]).then_inc(g_ready, 1)

        @block.tensor
        def _(pe):
            def turn_x(q, s):
                pe.wait_ge(slot_in[s], q * LOADS + LOADS)
                turn_to_cols(pe, c, xs[s], turn).then_inc(turned, 1)

            def body(q, s, last=False):
                take(pe, xe_ready)
                for k in range(KH):
                    if k >= 2:
                        take(pe, g_ready)
                    for d in range(KD):
                        mm = pe.matmul(ph[k % 2][:, 0:TOK], w1[s][:, d, k * P:(k + 1) * P], xe[:, d, :],
                                       start=(d == 0), stop=(d == KD - 1))
                    mm.then_inc(h_ready, 1)
                if not last:
                    turn_x(q + (s + 1) // SLOTS, (s + 1) % SLOTS)
                take(pe, y_read)
                for k in range(KH):
                    if k >= KH - 2:
                        take(pe, g_ready)
                    for t in range(2):
                        mm = pe.matmul(py[t][:, 0:D], hid[:, k, t * P:(t + 1) * P], w2[s][:, k, :],
                                       start=(k == 0), stop=(k == KH - 1))
                mm.then_inc(y_sum, 1)

            turn_x(0, 0)
            with pe.Fori(0, STEPS - 1) as q:
                for s in range(SLOTS):
                    body(q, s)
            for s in range(SLOTS):
                body(STEPS - 1, s, last=(s == SLOTS - 1))

        @block.vector
        def _(dve):
            def scale(q, s):
                dve.wait_ge(slot_in[s], q * LOADS + LOADS)
                take(dve, turned)
                for k in range(KD):
                    dve.tensor_scalar(xe[:, k, :], turn[:, k * TOK:(k + 1) * TOK], par[s][:, k:k + 1],
                                      par[s][:, KD + k:KD + k + 1], ALU.mult, ALU.add).then_inc(v, 1)
                take(dve, v, 2)
                dve.sem_inc(xe_ready, 1)

            def result(s):
                take(dve, y_sum)
                take(dve, y_free[s])
                for t in range(2):
                    dve.tensor_tensor(ys[s][:, t, :], py[t][:, 0:D], b2[s], ALU.add).then_inc(v, 1)
                take(dve, v, 2)
                dve.sem_inc(y_read, 1)
                dve.sem_inc(y_done[s], 1)

            dve.sem_inc(y_read, 1)
            for s in range(SLOTS):
                dve.sem_inc(y_free[s], 1)
            scale(0, 0)
            with dve.Fori(0, STEPS - 1) as q:
                for s in range(SLOTS):
                    scale(q + (s + 1) // SLOTS, (s + 1) % SLOTS)
                    result(s)
            for s in range(SLOTS):
                if s + 1 < SLOTS:
                    scale(STEPS - 1, s + 1)
                result(s)
    stage(nc, run, "expert_ffn")


def combine(nc, c):
    def run(block, sb, sem):
        ring = [sb(f"ring{s}", [P, 2], I32) for s in range(2)]
        y = [sb(f"y{s}", [P, 2, D]) for s in range(2)]
        idx_ready, landed, v = pair(sem, "idx_ready"), pair(sem, "landed"), sem("v")

        @block.gpsimd
        def _(pool):
            with pool.Fori(0, NB // 2):
                for s in range(2):
                    take(pool, idx_ready[s])
                    for i in range(2):
                        pool.indirect_dma_start(y[s][:, i, :], None, c.ys_dram,
                                                bass.IndirectOffsetOnAxis(ap=ring[s][:, i:i + 1], axis=0)
                                                ).then_inc(landed[s], 16)

        @block.vector
        def _(dve):
            def ask(t, s):
                dve.tensor_copy(ring[s][:], c.slot[:, bass.ds(t, 1), :].rearrange("p t i -> p (t i)")).then_inc(idx_ready[s], 1)

            def add(t, s):
                x = tile_at(c.X, t)
                for i in range(2):
                    chain(dve, dve.scalar_tensor_tensor(
                        x, y[s][:, i, :], c.pick[:, bass.ds(t, 1), i:i + 1].rearrange("p t i -> p (t i)"), x,
                        ALU.mult, ALU.add), v)

            ask(0, 0)
            ask(1, 1)
            with dve.Fori(0, NB // 2 - 1) as q:
                for s in range(2):
                    dve.wait_ge(landed[s], q * 32 + 32)
                    add(q * 2 + s, s)
                    ask(q * 2 + 2 + s, s)
            for s in range(2):
                dve.wait_ge(landed[s], 16 * NB)
                add(NB - 2 + s, s)
    stage(nc, run, "combine")


def gated_mlp(nc, c, a, out_dram):
    SH2, EN, EH1, EH2 = 128, 4, 128, 64
    EP = EN // 2

    def run(block, sb, sem):
        af = flat(c.A)
        sw1, sw2, sw3 = carve(af, 0, (KD, D)), carve(af, 512, (KD, SH2)), carve(af, 768, (D,))
        ew1 = carve(af, 1024, (EN, KD, EH1))
        ew2, ew3 = carve(af, 2048, (EN, EH2)), carve(af, 2304, (EP, D))
        sb3, eb3 = carve(af, 2816, (D,)), carve(af, 3072, (EN, D))
        h1, e1 = carve(af, 4096, (KD, BLK)), carve(af, 4608, (EN, BLK))
        h2, e2 = [carve(af, 5632 + s * BLK, (BLK,)) for s in range(2)], [carve(af, 6144 + s * EP * BLK, (EP, BLK)) for s in range(2)]
        w_in, up_ready, up_done, low_ready, low_done = (sem(n) for n in ("w_in", "up_ready", "up_done", "low_ready", "low_done"))
        res_ready, res_free, stored, written, v = (sem(n) for n in ("res_ready", "res_free", "stored", "written", "v"))
        up = c.ps[0:3]
        low = c.ps[3:5]
        res = c.ps[5:8]
        res_at = lambda e: res[0][:, 0:D] if e < 0 else res[1 + e % 2][:, e // 2 * D:(e // 2 + 1) * D]
        loads = [(sw1, a["L1_ffn_sW1"].rearrange("(k p) n -> p k n", p=P)),
                 (sw2, a["L1_ffn_sW2"].rearrange("(k p) n -> p k n", p=P)),
                 (sw3, a["L1_ffn_sW3"]),
                 (ew2, a["L1_ffn_eW2"].rearrange("e h g -> h e g")),
                 (sb3, a["L1_ffn_sb3"][None, :].to_broadcast([P, D]))]
        loads += [(ew3[:, u], a["L1_ffn_eW3"][2 * u:2 * u + 2].rearrange("v g o -> (v g) o")) for u in range(EP)]
        loads += [(ew1[:, e], a["L1_ffn_eW1"][e].rearrange("(k p) h -> p k h", p=P)) for e in range(EN)]
        loads += [(eb3[:, e], a["L1_ffn_eb3"][e:e + 1, :].to_broadcast([P, D])) for e in range(EN)]

        @block.sync
        def _(sp):
            for dst, src in loads:
                sp.dma_start(dst, src).then_inc(w_in, 16)
            with sp.Fori(0, NJ - 1) as j:
                take(sp, stored)
                sp.dma_start(out_dram[bass.ds(j * BLK, BLK), :].rearrange("(t p) d -> p t d", p=P),
                             c.X[:, bass.ds(j * 2, 2), :]).then_inc(written, 16)
            take(sp, stored)
            sp.dma_start(out_dram[FULL * P:N, :], c.X[0:REST, FULL, :]).then_inc(written, 16)
            sp.wait_ge(written, 16 * NJ)

        @block.scalar
        def _(act):
            def layer(dst, src, bias):
                return act.activation(dst, src, ACT.Relu, bias=bias)

            def upper(s):
                take(act, up_ready)
                b, e = pcols(c, "L1_ffn_sb1"), pcols(c, "L1_ffn_eb1", EN)
                for m in range(KD):
                    layer(h1[:, m, :], up[0][:, m * BLK:(m + 1) * BLK], b[:, m:m + 1])
                for i in range(EN):
                    ins = layer(e1[:, i, :], up[1 + i // 2][:, i % 2 * BLK:(i % 2 + 1) * BLK], e[:, i:i + 1])
                ins.then_inc(up_done, 1)

            def lower(s):
                take(act, low_ready)
                b, e = pcols(c, "L1_ffn_sb2", 1), pcols(c, "L1_ffn_eb2", EP)
                layer(h2[s], low[0][:, 0:BLK], b)
                for u in range(EP):
                    ins = layer(e2[s][:, u, :], low[1][:, u * BLK:(u + 1) * BLK], e[:, u:u + 1])
                ins.then_inc(low_done, 1)

            upper(0)
            lower(0)
            with act.Fori(0, NJ // 2):
                for s in (1, 0):
                    upper(s)
                    lower(s)

        @block.tensor
        def _(pe):
            def upper(j):
                x = cols_block(c, j)
                for m in range(KD):
                    for k in range(KD):
                        pe.matmul(up[0][:, m * BLK:(m + 1) * BLK], sw1[:, k, m * P:(m + 1) * P], x[:, k, :],
                                  start=(k == 0), stop=(k == KD - 1))
                for i in range(EN):
                    for k in range(KD):
                        mm = pe.matmul(up[1 + i // 2][:, i % 2 * BLK:(i % 2 + 1) * BLK], ew1[:, i, k, :], x[:, k, :],
                                       start=(k == 0), stop=(k == KD - 1))
                mm.then_inc(up_ready, 1)

            def lower():
                take(pe, up_done)
                for k in range(KD):
                    pe.matmul(low[0][:, 0:BLK], sw2[:, k, :], h1[:, k, :], start=(k == 0), stop=(k == KD - 1))
                for i in range(EN):
                    half = i % 2 * EH2
                    mm = pe.matmul(low[1][half:half + EH2, i // 2 * BLK:(i // 2 + 1) * BLK], ew2[:, i, :], e1[:, i, :],
                                   start=True, stop=True)
                mm.then_inc(low_ready, 1)

            def third(s, q):
                if q == 0:
                    take(pe, low_done)
                take(pe, res_free)
                at = slice(q * P, (q + 1) * P)
                pe.matmul(res_at(-1), h2[s][:, at], sw3, start=True, stop=True)
                for i in range(EN):
                    half = i % 2 * EH2
                    mm = pe.matmul(res_at(i), e2[s][half:half + EH2, i // 2, at], ew3[half:half + EH2, i // 2, :],
                                   start=True, stop=True)
                mm.then_inc(res_ready, 1)

            pe.wait_ge(w_in, 16 * len(loads))
            upper(0)
            lower()
            with pe.Fori(0, NJ // 2) as q2:
                for s in range(2):
                    upper(q2 * 2 + s + 1)
                    third(s, 0)
                    lower()
                    third(s, 1)
            third(0, 0)
            third(0, 1)

        @block.vector
        def _(dve):
            def add(t):
                x = tile_at(c.X, t)
                gate = lambda e: c.gate[:, bass.ds(t, 1), e:e + 1].rearrange("p t e -> p (t e)")
                take(dve, res_ready)
                chain(dve, dve.tensor_tensor(x, x, res_at(-1), ALU.add), v)
                for e in range(EN):
                    chain(dve, dve.scalar_tensor_tensor(x, res_at(e), gate(e), x, ALU.mult, ALU.add), v)
                dve.sem_inc(res_free, 1)
                chain(dve, dve.tensor_tensor(x, x, sb3, ALU.add), v)
                for e in range(EN):
                    chain(dve, dve.scalar_tensor_tensor(x, eb3[:, e, :], gate(e), x, ALU.mult, ALU.add), v)

            dve.sem_inc(res_free, 1)
            dve.wait_ge(w_in, 16 * len(loads))
            with dve.Fori(0, NJ) as j:
                add(j * 2)
                add(j * 2 + 1)
                dve.sem_inc(stored, 1)
    stage(nc, run, "gated_mlp")


def build(nc, a, out_dram):
    c = Chip()
    c.pat = {}
    at = 0
    for name, rows in (("L0_gnn_b1", 2), ("L0_gnn_g1", 2), ("L0_gnn_be1", 2), ("L0_gnn_b2", 2), ("L0_gnn_g2", 2),
                       ("L0_gnn_be2", 2), ("L1_gnn_c1_b2", 2), ("L1_gnn_c1_g", 2), ("L1_gnn_c1_b", 2),
                       ("L1_gnn_bn1_g", 2), ("L1_gnn_bn1_b", 2), ("L1_gnn_c2_b2", 2), ("L1_gnn_c2_g", 2),
                       ("L1_gnn_c2_b", 2), ("L1_gnn_bn2_g", 2), ("L1_gnn_bn2_b", 2), ("L1_ffn_sb1", 2),
                       ("L1_ffn_sb2", 1), ("L1_ffn_eb1", 4), ("L1_ffn_eb2", 2)):
        c.pat[name] = (at, rows)
        at += rows
    assert at <= P
    for name, at, rows in (("L0_ffn_ln_g", P, KD * E8), ("L0_ffn_ln_b", P + KD * E8, KD * E8),
                           ("L0_ffn_b1", P + 2 * KD * E8, KH * E8)):
        c.pat[name] = (at, rows)
    c.h_dram = nc.dram_tensor("h_rows", (NB * P, D), F32).ap()
    c.xs_dram = nc.dram_tensor("xs_rows", (XS_ROWS, D), F32).ap()
    c.ys_dram = nc.dram_tensor("ys_rows", (XS_ROWS, D), F32).ap()
    c.range_dram = nc.dram_tensor("ranges", (NG * 2,), I32).ap()
    c.record_dram = nc.dram_tensor("sorted_records", (EPT * P, 4), F32).ap()
    c.expert_dram = nc.dram_tensor("expert_cols", (E8, P, 2 * KD + KH), F32).ap()
    with ExitStack() as ctx:
        def sb(name, shape, dt=F32):
            return ctx.enter_context(nc.sbuf_tensor(name, shape, dt))

        c.X, c.A = sb("X", [P, NB, D]), sb("A", [P, NB, D])
        c.T = sb("T", [P, KD, NB * P])
        c.iota = sb("iota", [P, (FULL + 1) * P])
        c.e_src, c.e_dst, c.e_w = (sb(n, [P, EPT]) for n in ("e_src", "e_dst", "e_w"))
        c.ident, c.upper, c.ones = (sb(n, [P, P]) for n in ("ident", "upper", "ones"))
        c.node, c.mean, c.rstd = (sb(n, [P, NB]) for n in ("node", "mean", "rstd"))
        c.pcol, c.affine, c.eps = sb("pcol", [P, 2 * P]), sb("affine", [P, 2, KD]), sb("eps", [P, 1])
        c.dst_ranges, c.src_ranges = sb("dst_ranges", [1, NG * 2], I32), sb("src_ranges", [1, NG * 2], I32)
        c.s_src, c.s_dst, c.s_w = (flat(c.T)[:, D + i * EPT:][:, 0:EPT] for i in range(3))
        c.gate, c.pick = sb("gate", [P, NB, 4]), sb("pick", [P, NB, 2])
        c.slot, c.tile_expert = sb("slot", [P, NB, 2], I32), sb("tile_expert", [P, MT], I32)
        c.ps = [ctx.enter_context(nc.psum_tensor(f"bank{i}", [P, 512], F32)) for i in range(8)]
        col = lambda name: pcols(c, name)

        prepare(nc, c, a)
        sort_edges(nc, c)
        input_norm(nc, c)
        segment_sum(nc, c, c.s_dst, c.s_src, c.s_w, c.src_ranges, clear=False, fill=True)
        aggregate_product(nc, c, a["L0_gnn_W1"], col("L0_gnn_b1"), col("L0_gnn_g1"), col("L0_gnn_be1"))
        norm_product(nc, c, a["L0_gnn_W2"], col("L0_gnn_b2"), col("L0_gnn_g2"), col("L0_gnn_be2"))
        norm_to_rows(nc, c, residual=False)
        router(nc, c, a, "L0_ffn_Wr", "L0_ffn_br", E8, moe=True)
        expert_ffn(nc, c, a)
        combine(nc, c)
        message_rows(nc, c, a["L1_gnn_c1_w1"], a["L1_gnn_c1_b1"], from_x=True)
        segment_sum(nc, c, c.e_src, c.e_dst, c.e_w, c.dst_ranges, clear=True, fill=False)
        aggregate_product(nc, c, a["L1_gnn_c1_w2"], col("L1_gnn_c1_b2"), col("L1_gnn_c1_g"), col("L1_gnn_c1_b"))
        norm_relu(nc, c, col("L1_gnn_bn1_g"), col("L1_gnn_bn1_b"))
        message_rows(nc, c, a["L1_gnn_c2_w1"], a["L1_gnn_c2_b1"], from_x=False)
        segment_sum(nc, c, c.e_src, c.e_dst, c.e_w, c.dst_ranges, clear=True, fill=False)
        aggregate_product(nc, c, a["L1_gnn_c2_w2"], col("L1_gnn_c2_b2"), col("L1_gnn_c2_g"), col("L1_gnn_c2_b"))
        norm_relu(nc, c, col("L1_gnn_bn2_g"), col("L1_gnn_bn2_b"))
        norm_to_rows(nc, c, residual=True)
        router(nc, c, a, "L1_ffn_gW", "L1_ffn_gb", 4, moe=False)
        gated_mlp(nc, c, a, out_dram)


def kernel(**inputs):
    import concourse.bacc as _bacc
    from concourse.bass_utils import run_bass_kernel_spmd as _run

    nc = _bacc.Bacc("TRN2", target_bir_lowering=False, num_devices=1)
    arrays, args = {}, {}
    for name, value in inputs.items():
        v = np.ascontiguousarray(value)
        arrays[f"in_{name}"] = v
        args[name] = nc.dram_tensor(f"in_{name}", v.shape, mybir.dt.from_np(v.dtype), kind="ExternalInput").ap()
    out = nc.dram_tensor("out_x", (N, D), F32, kind="ExternalOutput").ap()
    build(nc, args, out)
    r = _run(nc, [arrays], core_ids=[0])
    return r.results[0]["out_x"]
```

```python
from contextlib import ExitStack

import numpy as np
import concourse.bass as bass
from concourse import mybir

F32 = mybir.dt.float32
I32 = mybir.dt.int32
BF16 = mybir.dt.bfloat16
ALU = mybir.AluOpType
ACT = mybir.ActivationFunctionType
AX = mybir.AxisListType

P = 128
N = 6250
D = 256
KD = D // P
NB = 50
FULL = N // P
REST = N - FULL * P
BLK = 2 * P
NJ = NB // 2
LAST = N - (NJ - 1) * BLK
EDGES = 100000
SRC, DST, WEIGHT = range(3)
EPT = 784
EC = 7
ER = EPT // EC
G = 4
NG = EPT // G
RING = 7
EPS = 1e-5
PARTS = 5
PW = NB // PARTS
E8, H = 8, 1024
KH = H // P
TOK = 256
MT = (2 * N - E8) // TOK + E8
DUMP = MT * TOK
XS_ROWS = DUMP + 4 * P
BIG = 1e4
CLAMPED = "node numbers are clamped to 0..N-1 before the ranges are made"


def take(eng, sem, n=1):
    eng.wait_ge(sem, n)
    eng.sem_inc(sem, -n)


def chain(eng, ins, sem):
    ins.then_inc(sem, 1)
    take(eng, sem)


class Chip:
    pass


def stage(nc, fn, name):
    with ExitStack() as ctx:
        tag, used = f"{name}{nc.next_id()}", []

        def sb(what, shape, dt=F32):
            return ctx.enter_context(nc.sbuf_tensor(f"{tag}_{what}", shape, dt))

        def sem(what):
            used.append(nc.alloc_semaphore(f"{tag}_{what}"))
            return used[-1]

        with nc.Block() as block:
            fn(block, sb, sem)
        nc.clear_and_free_semaphores(used)
        nc.all_engine_barrier()


def flat(t):
    return t[:].rearrange("p a b -> p (a b)")


def carve(area, start, shape):
    size = int(np.prod(shape))
    v = area[:, start:start + size]
    if len(shape) == 2:
        v = v.rearrange("p (a b) -> p a b", b=shape[1])
    if len(shape) == 3:
        v = v.rearrange("p (a b c) -> p a b c", b=shape[1], c=shape[2])
    return v


def tile_at(t, i):
    return t[:, bass.ds(i, 1), :].rearrange("p a d -> p (a d)")


def turn_lists(pe, c, lists, low_high, list_turned, list_copied, range_rows):
    n = 0
    for rows in lists:
        for k in range(EC):
            if n >= 2:
                pe.wait_ge(list_copied, n - 1)
            pe.transpose(c.ps[n % 2][:, 0:ER], rows[:, k, :], c.ident[0:ER, 0:ER]).then_inc(list_turned, 1)
            n += 1
    take(pe, range_rows, 2)
    for w in range(2):
        pe.transpose(c.ps[2][0:EC, w * P:w * P + ER], low_high[0:ER, w, :], c.ident[0:ER, 0:ER]).then_inc(list_turned, 1)


def copy_lists(dve, c, tables, keys, low_high, low_high_cols, range_f, range_i, list_turned, list_copied,
               range_rows, range_ready, v):
    for w, op in ((0, ALU.min), (1, ALU.max)):
        dve.tensor_reduce(low_high[0:ER, w, :], keys, AX.X, op).then_inc(range_rows, 1)
    n = 0
    for table in tables:
        for k in range(EC):
            dve.wait_ge(list_turned, n + 1)
            dve.tensor_copy(table[:, k * ER:(k + 1) * ER], c.ps[n % 2][:, 0:ER]).then_inc(list_copied, 1)
            n += 1
    dve.wait_ge(list_turned, n + 2)
    chain(dve, dve.tensor_scalar(low_high_cols[:], c.ps[2][0:EC, 0:2 * P].rearrange("c (w e) -> c w e", w=2)[:, :, 0:ER],
                                 0.0, float(N - 1), ALU.max, ALU.min), v)
    for w, op in ((0, ALU.min), (1, ALU.max)):
        chain(dve, dve.tensor_reduce(range_f[:, :, w], low_high_cols[:, w, :].rearrange("c (g t) -> c g t", t=G),
                                     AX.X, op), v)
    chain(dve, dve.tensor_scalar(range_f[:, :, 1], range_f[:, :, 1], float(P), None, ALU.add), v)
    chain(dve, dve.tensor_copy(range_i[:], range_f[:]), v)
    dve.tensor_scalar(range_i[:], range_i[:], P.bit_length() - 1, None, ALU.logical_shift_right).then_inc(range_ready, 1)


def place_ranges(sp, c, ranges, range_i, range_ready, range_out, range_in):
    sp.wait_ge(range_ready, 1)
    sp.dma_start(c.range_dram.rearrange("(c g) -> c g", c=EC), range_i[:].rearrange("c g w -> c (g w)")).then_inc(range_out, 16)
    sp.wait_ge(range_out, 16)
    sp.dma_start(ranges[:], c.range_dram[None, :].to_broadcast([P, NG * 2])).then_inc(range_in, 16)
    sp.wait_ge(range_in, 16)


def range_buffers(sb):
    return (sb("low_high", [P, 2, EC]), sb("low_high_cols", [EC, 2, ER]), sb("range_f", [EC, NG // EC, 2]),
            sb("range_i", [EC, NG // EC, 2], I32))


def prepare(nc, c, a):
    def run(block, sb, sem):
        af, tf = flat(c.A), flat(c.T)
        names = ("src", "dst", "edge_weight")
        raw = [af[:, i * EC * P:(i + 1) * EC * P] for i in range(3)]
        raw = [raw[0].bitcast(I32), raw[1].bitcast(I32), raw[2]]
        asf = [tf[:, 0:EC * P], tf[:, EC * P:2 * EC * P], raw[2]]
        lists = [x[0:ER, :].rearrange("r (k e) -> r k e", e=P) for x in asf]
        prow = carve(tf, 2 * EC * P, (2, P))
        low_high, low_high_cols, range_f, range_i = range_buffers(sb)
        x_in, edges_in, par_in = sem("x_in"), sem("edges_in"), sem("par_in")
        pads, consts, floats, made, v = (sem(n) for n in ("pads", "consts", "floats", "made", "v"))
        list_turned, list_copied, par_turned = sem("list_turned"), sem("list_copied"), sem("par_turned")
        range_rows, range_ready, range_out, range_in = (sem(n) for n in ("range_rows", "range_ready", "range_out", "range_in"))
        cols, record_out = sem("cols"), sem("record_out")

        @block.sync
        def _(sp):
            sp.wait_ge(pads, 1)
            whole = (EC - 1) * ER
            tail = EDGES // P - whole
            for i, name in enumerate(names):
                e = a[name]
                sp.dma_start(raw[i][0:ER, 0:(EC - 1) * P].rearrange("r (c e) -> r c e", e=P),
                             e[0:whole * P].rearrange("(c r e) -> r c e", r=ER, e=P)).then_inc(edges_in, 16)
                sp.dma_start(raw[i][0:tail, (EC - 1) * P:EC * P],
                             e[whole * P:(whole + tail) * P].rearrange("(r e) -> r e", e=P)).then_inc(edges_in, 16)
                sp.dma_start(raw[i][tail:tail + 1, (EC - 1) * P:(EC - 1) * P + EDGES % P],
                             e[(whole + tail) * P:EDGES].rearrange("(r e) -> r e", r=1)).then_inc(edges_in, 16)
            sp.wait_ge(pads, 2)
            for half in range(2):
                lo, hi = half * FULL // 2, (half + 1) * FULL // 2
                sp.dma_start(c.X[:, lo:hi, :],
                             a["x"][lo * P:hi * P, :].rearrange("(t p) d -> p t d", p=P)).then_inc(x_in, 16)
            sp.dma_start(c.X[0:REST, FULL, :], a["x"][FULL * P:N, :]).then_inc(x_in, 16)
            sp.dma_start(c.eps[:], a["L0_gnn_eps"][None, :].to_broadcast([P, 1])).then_inc(x_in, 16)
            place_ranges(sp, c, c.dst_ranges, range_i, range_ready, range_out, range_in)
            sp.wait_ge(cols, 1)
            for lo, w, at in ((0, KD, 0), (KD * E8, KD, KD), (2 * KD * E8, KH, 2 * KD)):
                sp.dma_start(c.expert_dram[:, :, at:at + w].rearrange("e p w -> p e w"),
                             c.pcol[:, P + lo:P + lo + E8 * w].rearrange("p (e w) -> p e w", w=w)).then_inc(record_out, 16)
            sp.wait_ge(x_in, 64)
            sp.wait_ge(record_out, 48)

        @block.scalar
        def _(act):
            act.wait_ge(pads, 2)
            for name, (at, rows) in c.pat.items():
                ap = a[name]
                if len(ap.shape) == 2:
                    ap = ap.rearrange("a b -> (a b)")
                act.dma_start(prow[at % P:at % P + rows, at // P, :],
                              ap.rearrange("(r e) -> r e", e=P)).then_inc(par_in, 16)
            act.wait_ge(par_in, 16 * len(c.pat))

        @block.gpsimd
        def _(pool):
            pool.memset(c.ident[:], 0.0).then_inc(made, 1)
            pool.memset(c.upper[:], 1.0).then_inc(made, 1)
            pool.memset(c.ones[:], 1.0).then_inc(made, 1)
            pool.wait_ge(made, 3)
            pool.affine_select(out=c.ident[:], in_=c.ident[:], compare_op=ALU.not_equal, fill=1.0,
                               base=0, pattern=[[-1, P]], channel_multiplier=1).then_inc(consts, 1)
            pool.affine_select(out=c.upper[:], in_=c.upper[:], compare_op=ALU.is_gt, fill=0.0,
                               base=0, pattern=[[1, P]], channel_multiplier=-1).then_inc(consts, 1)
            pool.iota(c.iota[:], pattern=[[1, c.iota.shape[1]]], base=0, channel_multiplier=0,
                      allow_small_or_imprecise_dtypes=True).then_inc(consts, 1)
            pool.iota(c.node[:], pattern=[[P, NB]], base=0, channel_multiplier=1,
                      allow_small_or_imprecise_dtypes=True).then_inc(consts, 1)
            pool.wait_ge(consts, 4)

        @block.tensor
        def _(pe):
            pe.wait_ge(consts, 1)
            pe.wait_ge(floats, 2)
            turn_lists(pe, c, lists, low_high, list_turned, list_copied, range_rows)
            pe.wait_ge(par_in, 16 * len(c.pat))
            for w in range(2):
                pe.transpose(c.ps[3][:, w * P:w * P + P], prow[:, w, :], c.ident[:]).then_inc(par_turned, 1)

        @block.vector
        def _(dve):
            last = slice((EC - 1) * P, EC * P)
            chain(dve, dve.memset(raw[0][0:ER, last], 0), v)
            chain(dve, dve.memset(raw[1][0:ER, last], N - 1), v)
            dve.memset(raw[2][0:ER, last], 0.0).then_inc(pads, 1)
            chain(dve, dve.memset(prow, 0.0), v)
            chain(dve, dve.memset(c.X[:, FULL:NB, :], 0.0), v)
            dve.sem_inc(pads, 1)
            dve.wait_ge(edges_in, 9 * 16)
            dve.tensor_copy(asf[0][0:ER, :], raw[0][0:ER, :]).then_inc(floats, 1)
            dve.tensor_copy(asf[1][0:ER, :], raw[1][0:ER, :]).then_inc(floats, 1)
            dve.wait_ge(floats, 2)
            copy_lists(dve, c, [c.edges[:, i, :] for i in range(3)], lists[1], low_high, low_high_cols, range_f, range_i,
                       list_turned, list_copied, range_rows, range_ready, v)
            dve.wait_ge(par_turned, 2)
            dve.tensor_copy(c.pcol[:], c.ps[3][:, 0:2 * P]).then_inc(cols, 1)
            dve.wait_ge(x_in, 64)
            chain(dve, dve.tensor_scalar(c.eps[:], c.eps[:], 1.0, None, ALU.add), v)
    stage(nc, run, "prepare")


def sort_edges(nc, c):
    NT = FULL + 1
    RB = 512 // ER
    RW = 8
    RP = 7
    STEPS = EPT // (RP * RW)

    def run(block, sb, sem):
        af, tf = flat(c.A), flat(c.T)
        tile_f, tile_i, place = tf[:, 0:EPT], tf[:, EPT:2 * EPT].bitcast(I32), tf[:, 2 * EPT:3 * EPT]
        rec = carve(tf, 3 * EPT, (EPT, 4))
        words = NT * ER // 2
        mask = af[:, 0:words].bitcast(BF16).rearrange("p (b t) -> p b t", t=ER)
        prod = carve(af, words, (NT, ER))
        incl, keep = af[:, 3 * words:3 * words + RB * ER], af[:, 3 * words + RB * ER:3 * words + 2 * RB * ER]
        count, total = carve(af, 3 * words + 2 * RB * ER, (EC, NT)), carve(af, 3 * words + 2 * RB * ER + EC * NT, (EC, NT))
        start, before, hist = sb("start", [P, EC, NT]), sb("before", [P, NT]), sb("hist", [P, NT])
        upper, ones = sb("upper", [P, P], BF16), sb("ones", [P, P], BF16)
        ring_rec, ring_idx = sb("ring_rec", [P, RP, RW, 4]), sb("ring_idx", [P, RP, RW], I32)
        first_node = sb("first_node", [P, NG])
        back = carve(tf, 7 * EPT, (EC, 4 * P))[0:ER]
        lists = [back.rearrange("r k (e f) -> r k e f", f=4)[:, :, :, i] for i in range(3)]
        low_high, low_high_cols, range_f, range_i = range_buffers(sb)
        v, counted, totals, mask_ready, chunk_placed = (sem(n) for n in ("v", "counted", "totals", "mask_ready", "chunk_placed"))
        ranked, bank_free = pair(sem, "ranked"), pair(sem, "bank_free")
        ring_ready, scattered = ([sem(f"{n}{h}") for h in range(RP)] for n in ("ring_ready", "scattered"))
        laid, copied, back_in = sem("laid"), sem("copied"), sem("back_in")
        go, done, normed, h_out = sem("go"), sem("done"), sem("normed"), [sem(f"h_out{i}") for i in range(PARTS)]
        list_turned, list_copied = sem("list_turned"), sem("list_copied")
        range_rows, range_ready, range_out, range_in = (sem(n) for n in ("range_rows", "range_ready", "range_out", "range_in"))
        groups = [(g % 2, g * RB, min(RB, NT - g * RB)) for g in range(-(-NT // RB))]

        def build_mask(dve, k):
            return dve.tensor_tensor(mask, c.iota[:, 0:NT][:, :, None].to_broadcast([P, NT, ER]),
                                     tile_f[:, bass.ds(k * ER, ER)][:, None, :].to_broadcast([P, NT, ER]), ALU.is_equal)

        @block.vector
        def _(dve):
            tt, ts = dve.tensor_tensor, dve.tensor_scalar
            dve.tensor_copy(upper[:], c.upper[:]).then_inc(laid, 1)
            dve.tensor_copy(ones[:], c.ones[:]).then_inc(laid, 1)
            chain(dve, dve.memset(rec, 0.0), v)
            for i in range(3):
                dve.tensor_copy(rec[:, :, i], c.edges[:, i, :]).then_inc(laid, 1)
            chain(dve, dve.memset(keep, 1.0), v)
            dve.memset(keep.rearrange("p (b t) -> p b t", t=ER)[:, :, 0:1], 0.0).then_inc(laid, 1)
            chain(dve, dve.tensor_copy(tile_i, c.edges[:, SRC, :]), v)
            chain(dve, ts(tile_i, tile_i, P.bit_length() - 1, None, ALU.logical_shift_right), v)
            dve.tensor_copy(tile_f, tile_i).then_inc(laid, 1)
            take(dve, laid, 7)
            with dve.Fori(0, EC) as k:
                chain(dve, build_mask(dve, k), v)
                chain(dve, dve.tensor_reduce(count[:, bass.ds(k, 1), :].rearrange("p k b -> p (k b)"), mask, AX.X, ALU.add), v)
            dve.sem_inc(counted, 1)
            take(dve, totals)
            chain(dve, dve.tensor_copy(total.rearrange("p k b -> p (k b)"), c.ps[4][:, 0:EC * NT]), v)
            chain(dve, dve.tensor_reduce(hist[:], total.rearrange("p k b -> p b k"), AX.X, ALU.add), v)
            chain(dve, dve.tensor_tensor_scan(before[:], c.ones[:, 0:NT], hist[:], 0.0, ALU.mult, ALU.add), v)
            chain(dve, tt(start[:, 0, :], before[:], hist[:], ALU.subtract), v)
            for k in range(1, EC):
                chain(dve, tt(start[:, k, :], start[:, k - 1, :], total[:, k - 1, :], ALU.add), v)
            for s in range(2):
                dve.sem_inc(bank_free[s], 1)

            def place_chunk(k):
                chain(dve, build_mask(dve, k), v)
                dve.sem_inc(mask_ready, 1)
                for s, b0, nb in groups:
                    w = nb * ER
                    rank, tot = c.ps[s][:, 0:w], c.ps[2 + s][:, 0:w]
                    out = prod[:, b0:b0 + nb, :]
                    flat_out = out.rearrange("p b t -> p (b t)")
                    take(dve, ranked[s])
                    chain(dve, dve.tensor_tensor_scan(incl[:, 0:w], keep[:, 0:w], tot, 0.0, ALU.mult, ALU.add), v)
                    chain(dve, tt(incl[:, 0:w], incl[:, 0:w], tot, ALU.subtract), v)
                    chain(dve, tt(flat_out, incl[:, 0:w], rank, ALU.add), v)
                    dve.sem_inc(bank_free[s], 1)
                    first = start[:, bass.ds(k, 1), b0:b0 + nb].rearrange("p k b -> p (k b)")
                    chain(dve, tt(out, out, first[:, :, None].to_broadcast([P, nb, ER]), ALU.add), v)
                    chain(dve, tt(out, out, mask[:, b0:b0 + nb, :], ALU.mult), v)
                chain(dve, dve.tensor_reduce(place[:, bass.ds(k * ER, ER)], prod.rearrange("p b t -> p t b"), AX.X, ALU.add), v)
                dve.sem_inc(chunk_placed, ER // RW)

            place_chunk(0)
            with dve.Fori(0, NB) as t:
                stat_tile(dve, c, t)
            dve.drain().then_inc(v, 1)
            take(dve, v)
            finish_stats(dve, go, done, c, v)
            with dve.Fori(1, EC) as k:
                place_chunk(k)
            for i in range(PARTS):
                x, h = (t[:, i * PW:(i + 1) * PW, :] for t in (c.X, c.A))
                mean, rstd = (bcast(t[:, i * PW:(i + 1) * PW], D) for t in (c.mean, c.rstd))
                chain(dve, tt(h, x, mean, ALU.subtract), v)
                tt(h, h, rstd, ALU.mult).then_inc(normed, 1)
            for i in range(PARTS):
                dve.wait_ge(h_out[i], 16)
                rows = c.A[:, i * PW:(i + 1) * PW, :]
                chain(dve, ts(rows, rows, c.eps[:, 0:1], None, ALU.mult), v)
            dve.wait_ge(back_in, 16)
            copy_lists(dve, c, [c.sorted[:, i, :] for i in range(3)], lists[0], low_high, low_high_cols, range_f, range_i,
                       list_turned, list_copied, range_rows, range_ready, v)
            dve.wait_ge(range_in, 16)
            for table, key, ranges in ((c.sorted, SRC, c.src_ranges), (c.edges, DST, c.dst_ranges)):
                first = ranges[:].rearrange("p (g w) -> p g w", w=2)[:, :, 0]
                keys = table[:, key, :].rearrange("p (g t) -> p g t", t=G)
                chain(dve, ts(first_node[:], first, float(P), None, ALU.mult), v)
                chain(dve, tt(keys, keys, bcast(first_node[:], G), ALU.subtract), v)

        @block.tensor
        def _(pe):
            take(pe, counted)
            pe.matmul(c.ps[4][:, 0:EC * NT], c.ones[:], count.rearrange("p k b -> p (k b)"), start=True, stop=True).then_inc(totals, 1)
            with pe.Fori(0, EC):
                take(pe, mask_ready)
                for s, b0, nb in groups:
                    m = mask[:, b0:b0 + nb, :].rearrange("p b t -> p (b t)")
                    take(pe, bank_free[s])
                    pe.matmul(c.ps[s][:, 0:nb * ER], upper[:], m, start=True, stop=True)
                    pe.matmul(c.ps[2 + s][:, 0:nb * ER], ones[:], m, start=True, stop=True).then_inc(ranked[s], 1)
            pe.wait_ge(back_in, 16)
            turn_lists(pe, c, lists, low_high, list_turned, list_copied, range_rows)

        @block.scalar
        def _(act):
            def fill(i, h):
                take(act, chunk_placed)
                t = i * (RP * RW) + h * RW
                act.copy(ring_rec[:, h], rec[:, bass.ds(t, RW), :]).then_inc(copied, 1)
                act.copy(ring_idx[:, h], place[:, bass.ds(t, RW)]).then_inc(copied, 1)
                take(act, copied, 2)
                act.sem_inc(ring_ready[h], 1)

            for h in range(RP):
                fill(0, h)
            root(act, go, done, c.rstd)
            with act.Fori(1, STEPS) as i:
                for h in range(RP):
                    act.wait_ge(scattered[h], i * (16 * RW))
                    fill(i, h)

        @block.gpsimd
        def _(pool):
            with pool.Fori(0, STEPS):
                for h in range(RP):
                    take(pool, ring_ready[h])
                    for j in range(RW):
                        pool.indirect_dma_start(c.record_dram, bass.IndirectOffsetOnAxis(ap=ring_idx[:, h, j:j + 1], axis=0),
                                                ring_rec[:, h, j, :], None).then_inc(scattered[h], 16)

        @block.sync
        def _(sp):
            for i in range(PARTS):
                sp.wait_ge(normed, i + 1)
                sp.dma_start(c.h_dram[i * PW * P:(i + 1) * PW * P, :].rearrange("(t p) d -> p t d", p=P),
                             c.A[:, i * PW:(i + 1) * PW, :]).then_inc(h_out[i], 16)
            for i in range(PARTS):
                sp.wait_ge(h_out[i], 16)
            for h in range(RP):
                sp.wait_ge(scattered[h], STEPS * RW * 16)
            sp.dma_start(back, c.record_dram.rearrange("(k r e) f -> r k (e f)", r=ER, e=P)).then_inc(back_in, 16)
            place_ranges(sp, c, c.src_ranges, range_i, range_ready, range_out, range_in)
    stage(nc, run, "sort_edges")


def stat_tile(dve, c, t):
    return dve.bn_stats(c.st[:, bass.ds(t, 1), :].rearrange("p a s -> p (a s)"), tile_at(c.X, t))


def finish_stats(dve, act_go, act_done, c, v):
    st = c.st
    chain(dve, dve.tensor_tensor(c.mean[:], st[:, :, 1], st[:, :, 4], ALU.add), v)
    chain(dve, dve.tensor_scalar(c.mean[:], c.mean[:], 0.5, None, ALU.mult), v)
    chain(dve, dve.tensor_tensor(st[:, :, 0], st[:, :, 1], st[:, :, 4], ALU.subtract), v)
    chain(dve, dve.scalar_tensor_tensor(st[:, :, 1], st[:, :, 0], 0.25, st[:, :, 0], ALU.mult, ALU.mult), v)
    chain(dve, dve.tensor_tensor(st[:, :, 2], st[:, :, 2], st[:, :, 5], ALU.add), v)
    chain(dve, dve.scalar_tensor_tensor(c.var[:], st[:, :, 2], 1.0 / D, st[:, :, 1], ALU.mult, ALU.add), v)
    dve.tensor_scalar(c.rstd[:], c.var[:], EPS, None, ALU.add).then_inc(act_go, 1)
    take(dve, act_done)
    chain(dve, dve.reciprocal(c.rstd[:], c.rstd[:]), v)


def norm_tile(dve, out, c, t, scale):
    return dve.tensor_scalar(out, tile_at(c.X, t), c.mean[:, bass.ds(t, 1)], scale[:, bass.ds(t, 1)],
                             ALU.subtract, ALU.mult)


def root(act, go, done, x):
    take(act, go)
    act.sqrt(x[:], x[:]).then_inc(done, 1)


def segment_sum(nc, c, edges, take_from, add_to, ranges, clear, fill):
    def run(block, sb, sem):
        free = flat(c.T)[:, D + 3 * EPT:]
        msg = carve(free, 0, (RING * G, D))
        hot = carve(free, RING * G * D, (3, G, P))
        idx, edge = sb("idx", [P, RING, G], I32), sb("edge", [P, RING, 3, G])
        acc = c.ps[0:3]
        rings = lambda name: [sem(f"{name}{h}") for h in range(RING)]
        copied, idx_ready, keys_ready = sem("copied"), rings("idx_ready"), rings("keys_ready")
        landed, scaled, slots_free = rings("landed"), rings("scaled"), rings("slots_free")
        hot_ready, summed = [sem(f"hot_ready{s}") for s in range(3)], [sem(f"summed{s}") for s in range(3)]
        v, zero, zeroed, filled = sem("v"), sem("zero"), sem("zeroed"), sem("filled")
        zeros = flat(c.T)[:, 0:D]

        def node_tiles(eng, g):
            _, (lo, hi) = nc.values_load_multi_w_load_instructions(
                ranges[0:1, bass.ds(g * 2, 2)], engines=[eng], min_val=0, max_val=FULL + 1, skip_runtime_bounds_check_because=CLAMPED)
            return nc.s_assert_within(lo, 0, FULL, skip_runtime_bounds_check_because=CLAMPED), hi

        if fill:
            @block.sync
            def _(sp):
                sp.wait_ge(zeroed, 1)
                parts, share = 4, XS_ROWS // P // 4
                for k in range(parts):
                    sp.dma_start(c.xs_dram[k * share * P:(k + 1) * share * P, :].rearrange("(p t) d -> p t d", p=P),
                                 zeros[:, None, :].to_broadcast([P, share, D])).then_inc(filled, 16)
                sp.wait_ge(filled, 16 * parts)

        @block.gpsimd
        def _(pool):
            with pool.Fori(0, NG // RING):
                for h in range(RING):
                    take(pool, idx_ready[h])
                    for j in range(G):
                        pool.indirect_dma_start(msg[:, h * G + j, :], None, c.h_dram,
                                                bass.IndirectOffsetOnAxis(ap=idx[:, h, j:j + 1], axis=0)
                                                ).then_inc(landed[h], 16)

        @block.scalar
        def _(act):
            def fetch(g, h):
                chain(act, act.copy(edge[:, h], edges[:, :, bass.ds(g * G, G)]), copied)
                act.sem_inc(keys_ready[h], 1)
                act.copy(idx[:, h, :], edge[:, h, take_from, :]).then_inc(idx_ready[h], 1)

            def scale(q, h):
                act.wait_ge(landed[h], q * (16 * G) + 16 * G)
                for j in range(G):
                    m = msg[:, h * G + j, :]
                    ins = act.activation(m, m, ACT.Identity, scale=edge[:, h, WEIGHT, j:j + 1])
                ins.then_inc(scaled[h], 1)

            for h in range(RING):
                fetch(h, h)
            with act.Fori(0, NG // RING - 1) as q:
                scale(q, 0)
                for h in range(RING):
                    if h + 1 < RING:
                        scale(q, h + 1)
                    take(act, slots_free[h])
                    fetch((q + 1) * RING + h, h)
            for h in range(RING):
                scale(NG // RING - 1, h)

        @block.tensor
        def _(pe):
            def products(h, s):
                take(pe, hot_ready[s])
                for j in range(G):
                    mm = pe.matmul(acc[s][:, 0:D], hot[:, s, j, :], msg[:, h * G + j, :],
                                   start=(j == 0), stop=(j == G - 1))
                mm.then_inc(summed[s], 1)

            with pe.Fori(0, NG // RING) as q:
                for h in range(RING):
                    take(pe, scaled[h])
                    products(h, h % 2)
                    lo, hi = node_tiles(mybir.EngineType.PE, q * RING + h)
                    with pe.If(lo + 1 < hi):
                        with pe.Fori(lo + 1, hi):
                            products(h, 2)

        @block.vector
        def _(dve):
            def matrices(h, skip, s):
                cols = c.iota[:, 0:P] if skip is None else c.iota[:, bass.ds(skip * P, P)]
                dve.tensor_tensor(hot[:, s], cols[:, None, :].to_broadcast([P, G, P]),
                                  edge[:, h, add_to, :][:, :, None].to_broadcast([P, G, P]), ALU.is_equal).then_inc(hot_ready[s], 1)

            def add(b, s):
                take(dve, summed[s])
                chain(dve, dve.tensor_tensor(tile_at(c.A, b), tile_at(c.A, b), acc[s][:, 0:D], ALU.add), v)

            def finish(h, lo, hi):
                with dve.If(lo + 1 < hi):
                    with dve.Fori(lo + 1, hi) as b:
                        skip = nc.s_assert_within(b - lo, 1, FULL, skip_runtime_bounds_check_because=CLAMPED)
                        matrices(h, skip, 2)
                        add(b, 2)
                add(lo, h % 2)
                dve.sem_inc(slots_free[h], 1)

            if fill:
                dve.memset(zeros, 0.0).then_inc(zeroed, 1)
            if clear:
                chain(dve, dve.memset(c.A[:], 0.0), zero)
            with dve.Fori(0, NG // RING) as q:
                last = None
                for h in range(RING):
                    take(dve, keys_ready[h])
                    matrices(h, None, h % 2)
                    if last:
                        finish(*last)
                    last = (h, *node_tiles(mybir.EngineType.DVE, q * RING + h))
                finish(*last)
    stage(nc, run, "segment_sum")


def blocks(eng, body):
    with eng.Fori(0, NJ // 2) as q:
        body(q * 2, 0)
        body(q * 2 + 1, 1)
    body(NJ - 1, 0)


def ahead(pe, first, second):
    first(0)
    with pe.Fori(0, NJ // 2) as q:
        first(1)
        second(q * 2, 0)
        first(0)
        second(q * 2 + 1, 1)
    second(NJ - 1, 0)


def two_ahead(eng, first, second):
    first(0, 0)
    first(1, 1)
    with eng.Fori(0, NJ // 2 - 1) as q:
        first(q * 2 + 2, 0)
        second(q * 2, 0)
        first(q * 2 + 3, 1)
        second(q * 2 + 1, 1)
    first(NJ - 1, 0)
    second(NJ - 3, 0)
    second(NJ - 2, 1)
    second(NJ - 1, 0)


def pair(sem, name):
    return [sem(f"{name}{s}") for s in range(2)]


def cols_block(c, j):
    return c.T[:, :, bass.ds(j * BLK, BLK)]


def pcols(c, name, n=KD, skip=0):
    at = c.pat[name][0] + skip
    return c.pcol[:, at:at + n]


def turn_to_cols(pe, c, row, turn):
    for s in range(2):
        for k in range(KD):
            mm = pe.transpose(turn[:, k * BLK + s * P:k * BLK + (s + 1) * P], row[:, s, k * P:(k + 1) * P], c.ident[:])
    return mm


def store_cols(act, c, j, src, bias):
    for m in range(KD):
        ins = act.activation(c.T[:, m, bass.ds(j * BLK, BLK)], src[:, m * BLK:(m + 1) * BLK], ACT.Identity,
                             bias=bias[:, m:m + 1])
    return ins


def apply_affine(act, c, out, src, func):
    for m in range(KD):
        ins = act.activation(out[:, m, :], src[:, m, :], func, bias=c.affine[:, 1, m:m + 1], scale=c.affine[:, 0, m:m + 1])
    return ins


def product_cols(pe, w, rhs, out):
    for m in range(KD):
        for k in range(KD):
            mm = pe.matmul(out[:, m * BLK:(m + 1) * BLK], w[:, k, m * P:(m + 1) * P], rhs[:, k, :],
                           start=(k == 0), stop=(k == KD - 1))
    return mm


def stats_blocks(dve, c, stats, stored):
    def one(j, n):
        take(dve, stored)
        for m in range(KD):
            ins = dve.bn_stats(stats[:, m, bass.ds(j, 1), :].rearrange("p a s -> p (a s)"), c.T[:, m, bass.ds(j * BLK, n)])
        return ins
    return one


def finish_affine(dve, c, stats, agg, gamma, beta, go, done, v):
    for m in range(KD):
        chain(dve, dve.bn_aggr(agg[:, m, :], stats[:, m, :, :].rearrange("p j s -> p (j s)")), v)
    dve.tensor_scalar(c.affine[:, 0, :], agg[:, :, 1], EPS, None, ALU.add).then_inc(go, 1)
    take(dve, done)
    chain(dve, dve.reciprocal(c.affine[:, 0, :], c.affine[:, 0, :]), v)
    chain(dve, dve.tensor_tensor(c.affine[:, 0, :], c.affine[:, 0, :], gamma, ALU.mult), v)
    chain(dve, dve.tensor_tensor(c.affine[:, 1, :], agg[:, :, 0], c.affine[:, 0, :], ALU.mult), v)
    chain(dve, dve.tensor_tensor(c.affine[:, 1, :], beta, c.affine[:, 1, :], ALU.subtract), v)


def root_affine(act, c, go, done):
    take(act, go)
    act.sqrt(c.affine[:, 0, :], c.affine[:, 0, :]).then_inc(done, 1)


def aggregate_product(nc, c, w_dram, bias, gamma, beta):
    def run(block, sb, sem):
        w, row = sb("w", [P, KD, D]), [sb(f"row{s}", [P, 2, D]) for s in range(2)]
        stats, agg = sb("stats", [P, KD, NJ, 6]), sb("agg", [P, KD, 2])
        turn, out = c.ps[0:2], c.ps[2:4]
        w_in, v, go, done, kept, stored = (sem(n) for n in ("w_in", "v", "go", "done", "kept", "stored"))
        row_ready, row_free = pair(sem, "row_ready"), pair(sem, "row_free")
        turned, in_t, prod, out_free = pair(sem, "turned"), sem("in_t"), pair(sem, "prod"), pair(sem, "out_free")

        @block.sync
        def _(sp):
            sp.dma_start(w[:], w_dram.rearrange("(k p) n -> p k n", p=P)).then_inc(w_in, 16)
            sp.wait_ge(w_in, 16)

        @block.scalar
        def _(act):
            def rows(j, s):
                take(act, row_free[s])
                act.copy(row[s][:], c.A[:, bass.ds(j * 2, 2), :]).then_inc(row_ready[s], 1)

            def store(j, s):
                take(act, prod[s])
                chain(act, store_cols(act, c, j, out[s], bias), kept)
                act.sem_inc(out_free[s], 1)
                act.sem_inc(stored, 1)

            two_ahead(act, rows, store)
            root_affine(act, c, go, done)

        @block.tensor
        def _(pe):
            def turn_rows(s):
                take(pe, row_ready[s])
                turn_to_cols(pe, c, row[s], turn[s]).then_inc(turned[s], 1)

            def product(j, s):
                take(pe, in_t)
                take(pe, out_free[s])
                product_cols(pe, w, cols_block(c, j), out[s]).then_inc(prod[s], 1)

            pe.wait_ge(w_in, 16)
            ahead(pe, turn_rows, product)

        @block.vector
        def _(dve):
            def copy(j, s):
                take(dve, turned[s])
                dve.sem_inc(row_free[s], 1)
                dve.tensor_copy(cols_block(c, j), turn[s][:].rearrange("p (k n) -> p k n", k=KD)).then_inc(in_t, 1)

            stat = stats_blocks(dve, c, stats, stored)
            for s in range(2):
                dve.sem_inc(row_free[s], 1)
                dve.sem_inc(out_free[s], 1)
            copy(0, 0)
            with dve.Fori(0, NJ // 2) as q:
                copy(q * 2 + 1, 1)
                stat(q * 2, BLK)
                copy(q * 2 + 2, 0)
                stat(q * 2 + 1, BLK)
            chain(dve, stat(NJ - 1, LAST), v)
            finish_affine(dve, c, stats, agg, gamma, beta, go, done, v)
    stage(nc, run, "aggregate_product")


def norm_product(nc, c, w_dram, bias, gamma, beta):
    def run(block, sb, sem):
        w = sb("w", [P, KD, D])
        stats, agg = sb("stats", [P, KD, NJ, 6]), sb("agg", [P, KD, 2])
        out = c.ps[2:4]
        w_in, v, go, done, kept, stored = (sem(n) for n in ("w_in", "v", "go", "done", "kept", "stored"))
        normed, prod, out_free = sem("normed"), pair(sem, "prod"), pair(sem, "out_free")

        @block.sync
        def _(sp):
            sp.dma_start(w[:], w_dram.rearrange("(k p) n -> p k n", p=P)).then_inc(w_in, 16)
            sp.wait_ge(w_in, 16)

        @block.scalar
        def _(act):
            def norm(j, s):
                apply_affine(act, c, cols_block(c, j), cols_block(c, j), ACT.Relu).then_inc(normed, 1)

            def store(j, s):
                take(act, prod[s])
                chain(act, store_cols(act, c, j, out[s], bias), kept)
                act.sem_inc(out_free[s], 1)
                act.sem_inc(stored, 1)

            two_ahead(act, norm, store)
            root_affine(act, c, go, done)

        @block.tensor
        def _(pe):
            def product(j, s):
                take(pe, normed)
                take(pe, out_free[s])
                product_cols(pe, w, cols_block(c, j), out[s]).then_inc(prod[s], 1)

            pe.wait_ge(w_in, 16)
            blocks(pe, product)

        @block.vector
        def _(dve):
            stat = stats_blocks(dve, c, stats, stored)
            for s in range(2):
                dve.sem_inc(out_free[s], 1)
            with dve.Fori(0, NJ - 1) as j:
                stat(j, BLK)
            chain(dve, stat(NJ - 1, LAST), v)
            finish_affine(dve, c, stats, agg, gamma, beta, go, done, v)
    stage(nc, run, "norm_product")


def norm_relu(nc, c, gamma, beta):
    def run(block, sb, sem):
        stats, agg = sb("stats", [P, KD, NJ, 6]), sb("agg", [P, KD, 2])
        v, go, done, stored = (sem(n) for n in ("v", "go", "done", "stored"))

        @block.scalar
        def _(act):
            with act.Fori(0, NJ) as j:
                apply_affine(act, c, cols_block(c, j), cols_block(c, j), ACT.Relu).then_inc(stored, 1)
            root_affine(act, c, go, done)

        @block.vector
        def _(dve):
            stat = stats_blocks(dve, c, stats, stored)
            with dve.Fori(0, NJ - 1) as j:
                stat(j, BLK)
            chain(dve, stat(NJ - 1, LAST), v)
            finish_affine(dve, c, stats, agg, gamma, beta, go, done, v)
    stage(nc, run, "norm_relu")


def norm_to_rows(nc, c, residual):
    def run(block, sb, sem):
        col = [sb(f"col{s}", [P, KD, BLK]) for s in range(2)]
        sum_ = sb("sum", [P, 2, D])
        turn = c.ps[0:2]
        ready, free, turned, v = pair(sem, "ready"), pair(sem, "free"), pair(sem, "turned"), sem("v")
        func = ACT.Identity if residual else ACT.Relu

        @block.scalar
        def _(act):
            def norm(j, s):
                take(act, free[s])
                apply_affine(act, c, col[s], cols_block(c, j), func).then_inc(ready[s], 1)
            blocks(act, norm)

        @block.tensor
        def _(pe):
            def turn_cols(j, s):
                take(pe, ready[s])
                for q in range(2):
                    for k in range(KD):
                        mm = pe.transpose(turn[s][:, q * D + k * P:q * D + (k + 1) * P],
                                          col[s][:, k, q * P:(q + 1) * P], c.ident[:])
                mm.then_inc(turned[s], 1)
            blocks(pe, turn_cols)

        @block.vector
        def _(dve):
            for s in range(2):
                dve.sem_inc(free[s], 1)

            def add(j, s):
                x = c.X[:, bass.ds(j * 2, 2), :]
                h = turn[s][:].rearrange("p (t d) -> p t d", t=2)
                if residual:
                    for q in range(2):
                        norm_tile(dve, sum_[:, q, :], c, j * 2 + q, c.rstd).then_inc(v, 1)
                    take(dve, v, 2)
                    take(dve, turned[s])
                    chain(dve, dve.tensor_tensor(sum_[:], sum_[:], h, ALU.add), v)
                    chain(dve, dve.scalar_tensor_tensor(x, sum_[:], 0.0, x, ALU.max, ALU.add), v)
                else:
                    take(dve, turned[s])
                    chain(dve, dve.tensor_tensor(x, x, h, ALU.add), v)
                dve.sem_inc(free[s], 1)
                for q in range(2):
                    stat_tile(dve, c, j * 2 + q)
            blocks(dve, add)
    stage(nc, run, "norm_to_rows")


def message_rows(nc, c, w_dram, b_dram, from_x):
    def run(block, sb, sem):
        w, bias = sb("w", [P, KD, D]), sb("bias", [P, D])
        col = [sb(f"col{s}", [P, KD, BLK]) for s in range(2)]
        row = [sb(f"row{s}", [P, 2, D]) for s in range(2)]
        rows = c.A
        turn, out = c.ps[0:2], c.ps[2:4]
        w_in, v, go, done, kept, stored = (sem(n) for n in ("w_in", "v", "go", "done", "kept", "stored"))
        h_out = sem("h_out")
        row_ready, turned, col_ready, col_free = (pair(sem, n) for n in ("row_ready", "turned", "col_ready", "col_free"))
        prod, out_free, added = pair(sem, "prod"), pair(sem, "out_free"), sem("added")

        @block.sync
        def _(sp):
            sp.dma_start(w[:], w_dram.rearrange("(k p) n -> p k n", p=P)).then_inc(w_in, 16)
            sp.dma_start(bias[:], b_dram[None, :].to_broadcast([P, D])).then_inc(w_in, 16)
            sp.wait_ge(w_in, 32)
            with sp.Fori(0, NJ) as j:
                take(sp, stored)
                sp.dma_start(c.h_dram[bass.ds(j * BLK, BLK), :].rearrange("(t p) d -> p t d", p=P),
                             rows[:, bass.ds(j * 2, 2), :]).then_inc(h_out, 16)
            sp.wait_ge(h_out, 16 * NJ)

        @block.scalar
        def _(act):
            if from_x:
                root(act, go, done, c.rstd)
            else:
                def norm(j, s):
                    take(act, col_free[s])
                    apply_affine(act, c, col[s], cols_block(c, j), ACT.Relu).then_inc(col_ready[s], 1)

            def relu(j):
                take(act, added)
                r = rows[:, bass.ds(j * 2, 2), :]
                act.activation(r, r, ACT.Relu).then_inc(stored, 1)

            if from_x:
                with act.Fori(0, NJ) as j:
                    relu(j)
            else:
                two_ahead(act, norm, lambda j, s: relu(j))

        @block.tensor
        def _(pe):
            def turn_rows(s):
                take(pe, row_ready[s])
                turn_to_cols(pe, c, row[s], turn[s]).then_inc(turned[s], 1)

            def product(j, s):
                take(pe, col_ready[s])
                take(pe, out_free[s])
                for q in range(2):
                    for k in range(KD):
                        mm = pe.matmul(out[s][:, q * D:(q + 1) * D], col[s][:, k, q * P:(q + 1) * P], w[:, k, :],
                                       start=(k == 0), stop=(k == KD - 1))
                mm.then_inc(prod[s], 1)

            pe.wait_ge(w_in, 32)
            if from_x:
                ahead(pe, turn_rows, product)
            else:
                blocks(pe, product)

        @block.vector
        def _(dve):
            def norm(j, s):
                for q in range(2):
                    ins = norm_tile(dve, row[s][:, q, :], c, j * 2 + q, c.rstd)
                ins.then_inc(row_ready[s], 1)

            def copy(s):
                take(dve, turned[s])
                take(dve, col_free[s])
                dve.tensor_copy(col[s][:], turn[s][:].rearrange("p (k n) -> p k n", k=KD)).then_inc(col_ready[s], 1)

            def add(j, s):
                take(dve, prod[s])
                dve.sem_inc(col_free[s], 1)
                for q in range(2):
                    dve.tensor_tensor(tile_at(rows, j * 2 + q), out[s][:, q * D:(q + 1) * D], bias[:], ALU.add).then_inc(kept, 1)
                take(dve, kept, 2)
                dve.sem_inc(out_free[s], 1)
                dve.sem_inc(added, 1)

            for s in range(2):
                dve.sem_inc(col_free[s], 1)
                dve.sem_inc(out_free[s], 1)
            dve.wait_ge(w_in, 32)
            if from_x:
                finish_stats(dve, go, done, c, v)
                norm(0, 0)
                norm(1, 1)
                copy(0)
                with dve.Fori(0, NJ // 2 - 1) as q:
                    norm(q * 2 + 2, 0)
                    copy(1)
                    add(q * 2, 0)
                    norm(q * 2 + 3, 1)
                    copy(0)
                    add(q * 2 + 1, 1)
                norm(NJ - 1, 0)
                copy(1)
                add(NJ - 3, 0)
                copy(0)
                add(NJ - 2, 1)
                add(NJ - 1, 0)
            else:
                blocks(dve, add)
    stage(nc, run, "message_rows")


def bcast(ap, n):
    return ap[:, :, None].to_broadcast([ap.shape[0], ap.shape[1], n])


def router(nc, c, a, wr_name, br_name, ne, moe):
    SLOTS = 10

    def run(block, sb, sem):
        wr, br = sb("wr", [P, KD, ne]), sb("br", [P, ne])
        row = [sb(f"row{s}", [P, 2, D]) for s in range(2)]
        col = [sb(f"col{s}", [P, KD, BLK]) for s in range(2)]
        work = flat(c.A) if not moe else flat(c.T)
        n3 = NB * ne
        logit, prob, eid, cand, pick1, pick2 = (carve(work, i * n3, (NB, ne)) for i in range(6))
        small = [carve(work, 6 * n3 + i * NB, (NB,)) for i in range(12)]
        top, total, p1, p2, first, q1, q2 = small[:7]
        rank, tot, cum, pos = (carve(work, 3600 + i * n3, (NB, ne)) for i in range(4))
        cum2 = carve(work, 3600 + 4 * n3, (NB, ne))
        turn, lg = c.ps[0:2], c.ps[2:4]
        w_in, v, go, done = (sem(n) for n in ("w_in", "v", "go", "done"))
        row_ready, turned, col_ready, col_free, lg_ready = (pair(sem, n) for n in ("row_ready", "turned", "col_ready", "col_free", "lg_ready"))
        iota_done, exp_go, exp_done, kept = (sem(n) for n in ("iota_done", "exp_go", "exp_done", "kept"))
        rank_go, rank_done = sem("rank_go"), sem("rank_done")
        x_ready, scattered = ([sem(f"{n}{s}") for s in range(SLOTS)] for n in ("x_ready", "scattered"))
        in_t = sem("in_t")
        xr = carve(flat(c.T), 8192, (SLOTS, D)) if moe else None
        ring = sb("ring", [P, SLOTS, 2], I32) if moe else None
        idx = sb("idx", [P, NB, 2]) if moe else None
        scale2 = sb("scale2", [P, NB]) if moe else None
        end, endi = sb("end", [P, E8]), sb("endi", [P, E8], I32)
        base = sb("base", [P, E8])
        tiles = sb("tiles", [P, MT]) if moe else None
        tmp_t = sb("tmp_t", [P, MT]) if moe else None

        @block.sync
        def _(sp):
            sp.dma_start(wr[:], a[wr_name].rearrange("(k p) n -> p k n", p=P)).then_inc(w_in, 16)
            sp.dma_start(br[:], a[br_name][None, :].to_broadcast([P, ne])).then_inc(w_in, 16)
            sp.wait_ge(w_in, 32)

        @block.gpsimd
        def _(pool):
            pool.iota(eid, pattern=[[0, NB], [1, ne]], base=0, channel_multiplier=0,
                      allow_small_or_imprecise_dtypes=True).then_inc(iota_done, 1)
            if moe:
                pool.iota(tiles[:], pattern=[[1, MT]], base=0, channel_multiplier=0,
                          allow_small_or_imprecise_dtypes=True).then_inc(iota_done, 1)

                def scatter(s):
                    take(pool, x_ready[s])
                    for i in range(2):
                        pool.indirect_dma_start(c.xs_dram, bass.IndirectOffsetOnAxis(ap=ring[:, s, i:i + 1], axis=0),
                                                xr[:, s, :], None).then_inc(scattered[s], 16)
                with pool.Fori(0, NB // SLOTS):
                    for s in range(SLOTS):
                        scatter(s)
                for s in range(SLOTS):
                    pool.wait_ge(scattered[s], 32 * (NB // SLOTS))
            else:
                pool.wait_ge(iota_done, 1)

        @block.scalar
        def _(act):
            root(act, go, done, c.rstd)
            if moe:
                root(act, go, done, scale2)
            if not moe:
                def to_t(j, s):
                    take(act, in_t)
                    chain(act, act.copy(cols_block(c, j), col[s][:]), kept)
                    act.sem_inc(col_free[s], 1)
                blocks(act, to_t)
            take(act, exp_go)
            act.activation(prob, logit, ACT.Exp).then_inc(exp_done, 1)
            if not moe:
                take(act, exp_go)
                act.activation(q1, q1, ACT.Exp).then_inc(exp_done, 1)
                act.activation(q2, q2, ACT.Exp).then_inc(exp_done, 1)

        @block.tensor
        def _(pe):
            def turn_rows(s):
                take(pe, row_ready[s])
                turn_to_cols(pe, c, row[s], turn[s]).then_inc(turned[s], 1)

            def logits(j, s):
                take(pe, col_ready[s])
                for q in range(2):
                    for k in range(KD):
                        mm = pe.matmul(lg[s][:, q * ne:(q + 1) * ne], col[s][:, k, q * P:(q + 1) * P], wr[:, k, :],
                                       start=(k == 0), stop=(k == KD - 1))
                mm.then_inc(lg_ready[s], 1)

            pe.wait_ge(w_in, 32)
            ahead(pe, turn_rows, logits)
            if moe:
                take(pe, rank_go)
                pe.matmul(c.ps[4][:, 0:n3], c.upper[:], cand.rearrange("p t e -> p (t e)"), start=True, stop=True)
                pe.matmul(c.ps[5][:, 0:n3], c.ones[:], cand.rearrange("p t e -> p (t e)"), start=True, stop=True).then_inc(rank_done, 1)

        @block.vector
        def _(dve):
            tt, ts = dve.tensor_tensor, dve.tensor_scalar
            finish_stats(dve, go, done, c, v)
            if moe:
                chain(dve, tt(scale2[:], c.rstd[:], c.rstd[:], ALU.mult), v)
                chain(dve, tt(scale2[:], scale2[:], c.var[:], ALU.mult), v)
                ts(scale2[:], scale2[:], EPS, None, ALU.add).then_inc(go, 1)
                take(dve, done)
                chain(dve, dve.reciprocal(scale2[:], scale2[:]), v)
                chain(dve, tt(scale2[:], scale2[:], c.rstd[:], ALU.mult), v)

            def rows(j, s):
                for q in range(2):
                    ins = norm_tile(dve, row[s][:, q, :], c, j * 2 + q, c.rstd)
                ins.then_inc(row_ready[s], 1)

            def copy(s):
                take(dve, turned[s])
                if not moe:
                    take(dve, col_free[s])
                chain(dve, dve.tensor_copy(col[s][:], turn[s][:].rearrange("p (k n) -> p k n", k=KD)), v)
                dve.sem_inc(col_ready[s], 1)
                if not moe:
                    dve.sem_inc(in_t, 1)

            def read(j, s):
                take(dve, lg_ready[s])
                for q in range(2):
                    tt(logit[:, bass.ds(j * 2 + q, 1), :].rearrange("p t e -> p (t e)"),
                       lg[s][:, q * ne:(q + 1) * ne], br[:], ALU.add).then_inc(v, 1)
                take(dve, v, 2)

            if not moe:
                for s in range(2):
                    dve.sem_inc(col_free[s], 1)
            dve.wait_ge(w_in, 32)
            rows(0, 0)
            rows(1, 1)
            copy(0)
            with dve.Fori(0, NJ // 2 - 1) as q:
                rows(q * 2 + 2, 0)
                copy(1)
                read(q * 2, 0)
                rows(q * 2 + 3, 1)
                copy(0)
                read(q * 2 + 1, 1)
            rows(NJ - 1, 0)
            copy(1)
            read(NJ - 3, 0)
            copy(0)
            read(NJ - 2, 1)
            read(NJ - 1, 0)

            dve.wait_ge(iota_done, 2 if moe else 1)
            chain(dve, dve.tensor_reduce(top, logit, AX.X, ALU.max), v)
            tt(logit, logit, bcast(top, ne), ALU.subtract).then_inc(exp_go, 1)
            take(dve, exp_done)
            chain(dve, dve.tensor_reduce(total, prob, AX.X, ALU.add), v)
            chain(dve, dve.reciprocal(total, total), v)
            chain(dve, tt(prob, prob, bcast(total, ne), ALU.mult), v)

            def choose(pick, p):
                chain(dve, dve.tensor_reduce(p, prob, AX.X, ALU.max), v)
                chain(dve, tt(cand, prob, bcast(p, ne), ALU.is_equal), v)
                chain(dve, dve.scalar_tensor_tensor(cand, cand, -BIG, eid, ALU.mult, ALU.add), v)
                chain(dve, dve.tensor_reduce(first, cand, AX.X, ALU.min), v)
                chain(dve, tt(pick, cand, bcast(first, ne), ALU.is_equal), v)

            choose(pick1, p1)
            chain(dve, dve.scalar_tensor_tensor(prob, pick1, -2.0, prob, ALU.mult, ALU.add), v)
            choose(pick2, p2)
            if moe:
                chain(dve, tt(total, p1, p2, ALU.add), v)
                chain(dve, dve.reciprocal(total, total), v)
                chain(dve, tt(c.pick[:, :, 0], p1, total, ALU.mult), v)
                chain(dve, tt(c.pick[:, :, 1], p2, total, ALU.mult), v)
            else:
                chain(dve, tt(q1, p1, p1, ALU.subtract), v)
                tt(q2, p2, p1, ALU.subtract).then_inc(exp_go, 1)
                take(dve, exp_done, 2)
                chain(dve, tt(total, q1, q2, ALU.add), v)
                chain(dve, dve.reciprocal(total, total), v)
                chain(dve, tt(q1, q1, total, ALU.mult), v)
                chain(dve, tt(q2, q2, total, ALU.mult), v)
                chain(dve, tt(pick1, pick1, bcast(q1, ne), ALU.mult), v)
                chain(dve, tt(pick2, pick2, bcast(q2, ne), ALU.mult), v)
                chain(dve, tt(c.gate[:, :, 0:ne], pick1, pick2, ALU.add), v)
                chain(dve, dve.memset(c.gate[:, :, ne:ne + 1], 1.0), v)
                return

            real, pad_at = small[7], small[8]
            chain(dve, ts(real, c.node[:], float(N), None, ALU.is_lt), v)
            chain(dve, tt(pick1, pick1, bcast(real, ne), ALU.mult), v)
            chain(dve, tt(pick2, pick2, bcast(real, ne), ALU.mult), v)
            tt(cand, pick1, pick2, ALU.add).then_inc(rank_go, 1)
            take(dve, rank_done)
            chain(dve, dve.tensor_copy(tot.rearrange("p t e -> p (t e)"), c.ps[5][:, 0:n3]), v)
            chain(dve, dve.tensor_copy(cum, tot), v)
            here, there = cum, cum2
            step = 1
            while step < NB:
                chain(dve, dve.tensor_copy(there[:, 0:step, :], here[:, 0:step, :]), v)
                chain(dve, tt(there[:, step:NB, :], here[:, step:NB, :], here[:, 0:NB - step, :], ALU.add), v)
                here, there = there, here
                step *= 2
            chain(dve, ts(end[:], here[:, NB - 1, :], 1.0, float(TOK - 1), ALU.max, ALU.add), v)
            chain(dve, dve.tensor_copy(endi[:], end[:]), v)
            chain(dve, ts(endi[:], endi[:], TOK.bit_length() - 1, None, ALU.logical_shift_right), v)
            chain(dve, dve.tensor_copy(end[:], endi[:]), v)
            for e in range(1, E8):
                chain(dve, tt(end[:, e:e + 1], end[:, e:e + 1], end[:, e - 1:e], ALU.add), v)
            chain(dve, dve.memset(base[:, 0:1], 0.0), v)
            chain(dve, ts(base[:, 1:E8], end[:, 0:E8 - 1], float(TOK), None, ALU.mult), v)
            chain(dve, tt(pos, here, tot, ALU.subtract), v)
            chain(dve, tt(pos.rearrange("p t e -> p (t e)"), pos.rearrange("p t e -> p (t e)"), c.ps[4][:, 0:n3], ALU.add), v)
            chain(dve, tt(pos, pos, base[:, None, :].to_broadcast([P, NB, E8]), ALU.add), v)
            chain(dve, ts(pad_at, c.node[:], float(DUMP - (NB - 2) * P), None, ALU.add), v)
            chain(dve, ts(real, real, -1.0, 1.0, ALU.mult, ALU.add), v)
            chain(dve, tt(pad_at, pad_at, real, ALU.mult), v)
            for i, pick in enumerate((pick1, pick2)):
                chain(dve, tt(pick, pick, pos, ALU.mult), v)
                chain(dve, dve.tensor_reduce(idx[:, :, i], pick, AX.X, ALU.add), v)
                chain(dve, dve.scalar_tensor_tensor(first, real, float(i * 2 * P), pad_at, ALU.mult, ALU.add), v)
                chain(dve, tt(idx[:, :, i], idx[:, :, i], first, ALU.add), v)
            chain(dve, dve.tensor_copy(c.slot[:], idx[:]), v)
            chain(dve, ts(tmp_t[:], tiles[:], end[:, 0:1], None, ALU.is_ge), v)
            for e in range(1, E8 - 1):
                chain(dve, dve.scalar_tensor_tensor(tmp_t[:], tiles[:], end[:, e:e + 1], tmp_t[:], ALU.is_ge, ALU.add), v)
            chain(dve, dve.tensor_copy(c.tile_expert[:], tmp_t[:]), v)

            def send(t, s):
                dve.tensor_copy(ring[:, s, :], c.slot[:, bass.ds(t, 1), :].rearrange("p t i -> p (t i)")).then_inc(v, 1)
                norm_tile(dve, xr[:, s, :], c, t, scale2).then_inc(v, 1)
                take(dve, v, 2)
                dve.sem_inc(x_ready[s], 1)
            for s in range(SLOTS):
                send(s, s)
            with dve.Fori(1, NB // SLOTS) as q:
                for s in range(SLOTS):
                    dve.wait_ge(scattered[s], q * 32)
                    send(q * SLOTS + s, s)
    stage(nc, run, "router")


def expert_ffn(nc, c, a):
    SLOTS = 4
    STEPS = MT // SLOTS
    LOADS = 5 * 16

    def run(block, sb, sem):
        tf, af = flat(c.T), flat(c.A)
        WW = KD * H
        places = [(tf, 0), (tf, 2 * WW), (af, 0), (af, 2 * WW)]
        w1 = [carve(area, o, (KD, H)) for area, o in places]
        w2 = [carve(area, o + WW, (KH, D)) for area, o in places]
        hid = carve(tf, 4 * WW, (KH, TOK))
        xs = [carve(tf, 4 * WW + KH * TOK + s * 2 * D, (2, D)) for s in range(SLOTS)]
        rest = af[:, 4 * WW:]
        ys = [carve(rest, s * 2 * D, (2, D)) for s in range(SLOTS)]
        b2 = [carve(rest, (2 * SLOTS + s) * D, (D,)) for s in range(SLOTS)]
        xe = carve(rest, 3 * SLOTS * D, (KD, TOK))
        par = [carve(rest, 3 * SLOTS * D + KD * TOK + s * (2 * KD + KH), (2 * KD + KH,)) for s in range(SLOTS)]
        turn, ph, py = c.ps[0], c.ps[1:3], c.ps[3:5]
        slots = lambda name: [sem(f"{name}{s}") for s in range(SLOTS)]
        slot_in, y_done, y_free, y_out = (slots(n) for n in ("slot_in", "y_done", "y_free", "y_out"))
        turned, xe_ready, h_ready, g_ready, y_read = (sem(n) for n in ("turned", "xe_ready", "h_ready", "g_ready", "y_read"))
        v, y_sum, pad_out = sem("v"), sem("y_sum"), sem("pad_out")

        @block.sync
        def _(sp):
            def load(i, s):
                e = sp.value_load(c.tile_expert[0:1, bass.ds(i, 1)], min_val=0, max_val=E8 - 1)
                one = lambda t: t[bass.ds(e, 1)]
                sp.dma_start(xs[s], c.xs_dram[bass.ds(i * TOK, TOK), :].rearrange("(t p) d -> p t d", p=P)).then_inc(slot_in[s], 16)
                sp.dma_start(w1[s], one(a["L0_ffn_W1"]).rearrange("e (k p) h -> p (e k) h", p=P)).then_inc(slot_in[s], 16)
                sp.dma_start(w2[s], one(a["L0_ffn_W2"]).rearrange("e (k p) d -> p (e k) d", p=P)).then_inc(slot_in[s], 16)
                sp.dma_start(par[s], one(c.expert_dram).rearrange("e p w -> p (e w)")).then_inc(slot_in[s], 16)
                sp.dma_start(b2[s], one(a["L0_ffn_b2"]).to_broadcast([P, D])).then_inc(slot_in[s], 16)

            def store(q, s):
                take(sp, y_done[s])
                sp.dma_start(c.ys_dram[bass.ds((q * SLOTS + s) * TOK, TOK), :].rearrange("(t p) d -> p t d", p=P),
                             ys[s]).then_inc(y_out[s], 16)

            for s in range(SLOTS):
                load(s, s)
            with sp.Fori(0, STEPS - 1) as q:
                for s in range(SLOTS):
                    store(q, s)
                    load((q + 1) * SLOTS + s, s)
                    sp.wait_ge(y_out[s], q * 16 + 16)
                    sp.sem_inc(y_free[s], 1)
            for s in range(SLOTS):
                store(STEPS - 1, s)
            sp.dma_start(c.ys_dram[DUMP:XS_ROWS, :], c.xs_dram[DUMP:XS_ROWS, :]).then_inc(pad_out, 16)
            for s in range(SLOTS):
                sp.wait_ge(y_out[s], 16 * STEPS)
            sp.wait_ge(pad_out, 16)

        @block.scalar
        def _(act):
            with act.Fori(0, STEPS) as q:
                for s in range(SLOTS):
                    for k in range(KH):
                        take(act, h_ready)
                        if k == 0:
                            act.wait_ge(slot_in[s], q * LOADS + LOADS)
                        act.activation(hid[:, k, :], ph[k % 2][:, 0:TOK], ACT.Gelu,
                                       bias=par[s][:, 2 * KD + k:2 * KD + k + 1]).then_inc(g_ready, 1)

        @block.tensor
        def _(pe):
            def turn_x(q, s):
                pe.wait_ge(slot_in[s], q * LOADS + LOADS)
                turn_to_cols(pe, c, xs[s], turn).then_inc(turned, 1)

            def body(q, s, last=False):
                take(pe, xe_ready)
                for k in range(KH):
                    if k >= 2:
                        take(pe, g_ready)
                    for d in range(KD):
                        mm = pe.matmul(ph[k % 2][:, 0:TOK], w1[s][:, d, k * P:(k + 1) * P], xe[:, d, :],
                                       start=(d == 0), stop=(d == KD - 1))
                    mm.then_inc(h_ready, 1)
                if not last:
                    turn_x(q + (s + 1) // SLOTS, (s + 1) % SLOTS)
                take(pe, y_read)
                for k in range(KH):
                    if k >= KH - 2:
                        take(pe, g_ready)
                    for t in range(2):
                        mm = pe.matmul(py[t][:, 0:D], hid[:, k, t * P:(t + 1) * P], w2[s][:, k, :],
                                       start=(k == 0), stop=(k == KH - 1))
                mm.then_inc(y_sum, 1)

            turn_x(0, 0)
            with pe.Fori(0, STEPS - 1) as q:
                for s in range(SLOTS):
                    body(q, s)
            for s in range(SLOTS):
                body(STEPS - 1, s, last=(s == SLOTS - 1))

        @block.vector
        def _(dve):
            def scale(q, s):
                dve.wait_ge(slot_in[s], q * LOADS + LOADS)
                take(dve, turned)
                for k in range(KD):
                    dve.tensor_scalar(xe[:, k, :], turn[:, k * TOK:(k + 1) * TOK], par[s][:, k:k + 1],
                                      par[s][:, KD + k:KD + k + 1], ALU.mult, ALU.add).then_inc(v, 1)
                take(dve, v, 2)
                dve.sem_inc(xe_ready, 1)

            def result(s):
                take(dve, y_sum)
                take(dve, y_free[s])
                for t in range(2):
                    dve.tensor_tensor(ys[s][:, t, :], py[t][:, 0:D], b2[s], ALU.add).then_inc(v, 1)
                take(dve, v, 2)
                dve.sem_inc(y_read, 1)
                dve.sem_inc(y_done[s], 1)

            dve.sem_inc(y_read, 1)
            for s in range(SLOTS):
                dve.sem_inc(y_free[s], 1)
            scale(0, 0)
            with dve.Fori(0, STEPS - 1) as q:
                for s in range(SLOTS):
                    scale(q + (s + 1) // SLOTS, (s + 1) % SLOTS)
                    result(s)
            for s in range(SLOTS):
                if s + 1 < SLOTS:
                    scale(STEPS - 1, s + 1)
                result(s)
    stage(nc, run, "expert_ffn")


def combine(nc, c):
    SLOTS = 10
    STEPS = NB // SLOTS

    def run(block, sb, sem):
        y = carve(flat(c.T), 0, (SLOTS * 2, D))
        slots_free, landed, v = ([sem(f"{n}{s}") for s in range(SLOTS)] for n in ("slots_free", "landed", "v"))
        idx_ready, ring = [sem(f"idx_ready{s}") for s in range(SLOTS)], sb("ring", [P, SLOTS, 2], I32)

        @block.gpsimd
        def _(pool):
            with pool.Fori(0, STEPS):
                for s in range(SLOTS):
                    take(pool, idx_ready[s])
                    for i in range(2):
                        pool.indirect_dma_start(y[:, s * 2 + i, :], None, c.ys_dram,
                                                bass.IndirectOffsetOnAxis(ap=ring[:, s, i:i + 1], axis=0)
                                                ).then_inc(landed[s], 16)

        @block.scalar
        def _(act):
            for s in range(SLOTS):
                act.sem_inc(slots_free[s], 1)
            with act.Fori(0, STEPS) as q:
                for s in range(SLOTS):
                    take(act, slots_free[s])
                    act.copy(ring[:, s, :], c.slot[:, bass.ds(q * SLOTS + s, 1), :].rearrange("p t i -> p (t i)")
                             ).then_inc(idx_ready[s], 1)

        @block.vector
        def _(dve):
            with dve.Fori(0, STEPS) as q:
                for s in range(SLOTS):
                    t = q * SLOTS + s
                    x = tile_at(c.X, t)
                    dve.wait_ge(landed[s], q * 32 + 32)
                    for i in range(2):
                        chain(dve, dve.scalar_tensor_tensor(
                            x, y[:, s * 2 + i, :], c.pick[:, bass.ds(t, 1), i:i + 1].rearrange("p t i -> p (t i)"), x,
                            ALU.mult, ALU.add), v[s])
                    dve.sem_inc(slots_free[s], 1)
                    stat_tile(dve, c, t)
    stage(nc, run, "combine")


def gated_mlp(nc, c, a, out_dram):
    SH2, EN, EH1, EH2 = 128, 4, 128, 64
    EP = EN // 2

    def run(block, sb, sem):
        af = flat(c.A)
        sw1, sw2, sw3 = carve(af, 0, (KD, D)), carve(af, 512, (KD, SH2)), carve(af, 768, (D,))
        ew1 = carve(af, 1024, (EN, KD, EH1))
        ew2, ew3 = carve(af, 2048, (EN, EH2)), carve(af, 2304, (EP, D))
        b3 = carve(af, 2816, (D,))[0:EN + 1]
        gate_row = carve(af, 3072, (2, EN + 1))
        gate_col = [carve(af, 3328 + s * BLK, (BLK,))[0:EN + 1] for s in range(2)]
        h1, e1 = carve(af, 4096, (KD, BLK)), carve(af, 4608, (EN, BLK))
        h2, e2 = [carve(af, 5632 + s * BLK, (BLK,)) for s in range(2)], [carve(af, 6144 + s * EP * BLK, (EP, BLK)) for s in range(2)]
        w_in, up_ready, up_done, low_ready, low_done = (sem(n) for n in ("w_in", "up_ready", "up_done", "low_ready", "low_done"))
        res_ready, res_free, stored, written, v = (sem(n) for n in ("res_ready", "res_free", "stored", "written", "v"))
        up = c.ps[0:3]
        low = c.ps[3:5]
        res = c.ps[5:8]
        res_at = lambda e: res[0][:, 0:D] if e < 0 else res[1 + e % 2][:, e // 2 * D:(e // 2 + 1) * D]
        loads = [(sw1, a["L1_ffn_sW1"].rearrange("(k p) n -> p k n", p=P)),
                 (sw2, a["L1_ffn_sW2"].rearrange("(k p) n -> p k n", p=P)),
                 (sw3, a["L1_ffn_sW3"]),
                 (ew2, a["L1_ffn_eW2"].rearrange("e h g -> h e g")),
                 (b3[0:EN], a["L1_ffn_eb3"]), (b3[EN:EN + 1], a["L1_ffn_sb3"][None, :])]
        loads += [(ew3[:, u], a["L1_ffn_eW3"][2 * u:2 * u + 2].rearrange("v g o -> (v g) o")) for u in range(EP)]
        loads += [(ew1[:, e], a["L1_ffn_eW1"][e].rearrange("(k p) h -> p k h", p=P)) for e in range(EN)]

        @block.sync
        def _(sp):
            for dst, src in loads:
                sp.dma_start(dst, src).then_inc(w_in, 16)
            with sp.Fori(0, NJ - 1) as j:
                take(sp, stored)
                sp.dma_start(out_dram[bass.ds(j * BLK, BLK), :].rearrange("(t p) d -> p t d", p=P),
                             c.X[:, bass.ds(j * 2, 2), :]).then_inc(written, 16)
            take(sp, stored)
            sp.dma_start(out_dram[FULL * P:N, :], c.X[0:REST, FULL, :]).then_inc(written, 16)
            sp.wait_ge(written, 16 * NJ)

        @block.scalar
        def _(act):
            def layer(dst, src, bias):
                return act.activation(dst, src, ACT.Relu, bias=bias)

            def upper(j):
                act.copy(gate_row, c.gate[:, bass.ds(j * 2, 2), :])
                take(act, up_ready)
                b, e = pcols(c, "L1_ffn_sb1"), pcols(c, "L1_ffn_eb1", EN)
                for m in range(KD):
                    layer(h1[:, m, :], up[0][:, m * BLK:(m + 1) * BLK], b[:, m:m + 1])
                for i in range(EN):
                    ins = layer(e1[:, i, :], up[1 + i // 2][:, i % 2 * BLK:(i % 2 + 1) * BLK], e[:, i:i + 1])
                ins.then_inc(up_done, 1)

            def lower(s):
                take(act, low_ready)
                b, e = pcols(c, "L1_ffn_sb2", 1), pcols(c, "L1_ffn_eb2", EP)
                act.copy(gate_col[s], low[0][0:EN + 1, BLK:2 * BLK])
                layer(h2[s], low[0][:, 0:BLK], b)
                for u in range(EP):
                    ins = layer(e2[s][:, u, :], low[1][:, u * BLK:(u + 1) * BLK], e[:, u:u + 1])
                ins.then_inc(low_done, 1)

            upper(0)
            lower(0)
            with act.Fori(0, NJ // 2) as q:
                for s in (1, 0):
                    upper(q * 2 + 2 - s)
                    lower(s)

        @block.tensor
        def _(pe):
            def upper_shared(j):
                x = cols_block(c, j)
                for m in range(KD):
                    for k in range(KD):
                        pe.matmul(up[0][:, m * BLK:(m + 1) * BLK], sw1[:, k, m * P:(m + 1) * P], x[:, k, :],
                                  start=(k == 0), stop=(k == KD - 1))

            def upper_experts(j):
                x = cols_block(c, j)
                for i in range(EN):
                    for k in range(KD):
                        mm = pe.matmul(up[1 + i // 2][:, i % 2 * BLK:(i % 2 + 1) * BLK], ew1[:, i, k, :], x[:, k, :],
                                       start=(k == 0), stop=(k == KD - 1))
                mm.then_inc(up_ready, 1)

            def lower():
                take(pe, up_done)
                for q in range(2):
                    pe.transpose(low[0][0:EN + 1, BLK + q * P:BLK + (q + 1) * P], gate_row[:, q, :], c.ident[:])
                for k in range(KD):
                    pe.matmul(low[0][:, 0:BLK], sw2[:, k, :], h1[:, k, :], start=(k == 0), stop=(k == KD - 1))
                for i in range(EN):
                    half = i % 2 * EH2
                    mm = pe.matmul(low[1][half:half + EH2, i // 2 * BLK:(i // 2 + 1) * BLK], ew2[:, i, :], e1[:, i, :],
                                   start=True, stop=True)
                mm.then_inc(low_ready, 1)

            def third(s, q):
                if q == 0:
                    take(pe, low_done)
                take(pe, res_free)
                at = slice(q * P, (q + 1) * P)
                pe.matmul(res_at(-1), h2[s][:, at], sw3, start=True, stop=False)
                pe.matmul(res_at(-1), gate_col[s][:, at], b3, start=False, stop=True)
                for i in range(EN):
                    half = i % 2 * EH2
                    mm = pe.matmul(res_at(i), e2[s][half:half + EH2, i // 2, at], ew3[half:half + EH2, i // 2, :],
                                   start=True, stop=True)
                mm.then_inc(res_ready, 1)

            pe.wait_ge(w_in, 16 * len(loads))
            upper_shared(0)
            upper_experts(0)
            lower()
            with pe.Fori(0, NJ // 2) as q2:
                for s in range(2):
                    upper_shared(q2 * 2 + s + 1)
                    third(s, 0)
                    upper_experts(q2 * 2 + s + 1)
                    third(s, 1)
                    lower()
            third(0, 0)
            third(0, 1)

        @block.vector
        def _(dve):
            def add(t):
                x = tile_at(c.X, t)
                gate = lambda e: c.gate[:, bass.ds(t, 1), e:e + 1].rearrange("p t e -> p (t e)")
                take(dve, res_ready)
                chain(dve, dve.tensor_tensor(x, x, res_at(-1), ALU.add), v)
                for e in range(EN):
                    chain(dve, dve.scalar_tensor_tensor(x, res_at(e), gate(e), x, ALU.mult, ALU.add), v)
                dve.sem_inc(res_free, 1)

            dve.sem_inc(res_free, 1)
            dve.wait_ge(w_in, 16 * len(loads))
            with dve.Fori(0, NJ) as j:
                add(j * 2)
                add(j * 2 + 1)
                dve.sem_inc(stored, 1)
    stage(nc, run, "gated_mlp")


def build(nc, a, out_dram):
    c = Chip()
    c.pat = {}
    at = 0
    for name, rows in (("L0_gnn_b1", 2), ("L0_gnn_g1", 2), ("L0_gnn_be1", 2), ("L0_gnn_b2", 2), ("L0_gnn_g2", 2),
                       ("L0_gnn_be2", 2), ("L1_gnn_c1_b2", 2), ("L1_gnn_c1_g", 2), ("L1_gnn_c1_b", 2),
                       ("L1_gnn_bn1_g", 2), ("L1_gnn_bn1_b", 2), ("L1_gnn_c2_b2", 2), ("L1_gnn_c2_g", 2),
                       ("L1_gnn_c2_b", 2), ("L1_gnn_bn2_g", 2), ("L1_gnn_bn2_b", 2), ("L1_ffn_sb1", 2),
                       ("L1_ffn_sb2", 1), ("L1_ffn_eb1", 4), ("L1_ffn_eb2", 2)):
        c.pat[name] = (at, rows)
        at += rows
    assert at <= P
    for name, at, rows in (("L0_ffn_ln_g", P, KD * E8), ("L0_ffn_ln_b", P + KD * E8, KD * E8),
                           ("L0_ffn_b1", P + 2 * KD * E8, KH * E8)):
        c.pat[name] = (at, rows)
    c.h_dram = nc.dram_tensor("h_rows", (NB * P, D), F32).ap()
    c.xs_dram = nc.dram_tensor("xs_rows", (XS_ROWS, D), F32).ap()
    c.ys_dram = nc.dram_tensor("ys_rows", (XS_ROWS, D), F32).ap()
    c.range_dram = nc.dram_tensor("ranges", (NG * 2,), I32).ap()
    c.record_dram = nc.dram_tensor("sorted_records", (EPT * P, 4), F32).ap()
    c.expert_dram = nc.dram_tensor("expert_cols", (E8, P, 2 * KD + KH), F32).ap()
    with ExitStack() as ctx:
        def sb(name, shape, dt=F32):
            return ctx.enter_context(nc.sbuf_tensor(name, shape, dt))

        c.X, c.A = sb("X", [P, NB, D]), sb("A", [P, NB, D])
        c.T = sb("T", [P, KD, NB * P])
        c.iota = sb("iota", [P, (FULL + 1) * P])
        c.edges = sb("edges", [P, 3, EPT])
        c.ident, c.upper, c.ones = (sb(n, [P, P]) for n in ("ident", "upper", "ones"))
        c.node, c.mean, c.var, c.rstd = (sb(n, [P, NB]) for n in ("node", "mean", "var", "rstd"))
        c.st = sb("st", [P, NB, 6])
        c.pcol, c.affine, c.eps = sb("pcol", [P, 2 * P]), sb("affine", [P, 2, KD]), sb("eps", [P, 1])
        c.dst_ranges, c.src_ranges = sb("dst_ranges", [P, NG * 2], I32), sb("src_ranges", [P, NG * 2], I32)
        c.sorted = carve(flat(c.T), D, (3, EPT))
        c.gate, c.pick = sb("gate", [P, NB, 5]), sb("pick", [P, NB, 2])
        c.slot, c.tile_expert = sb("slot", [P, NB, 2], I32), sb("tile_expert", [P, MT], I32)
        c.ps = [ctx.enter_context(nc.psum_tensor(f"bank{i}", [P, 512], F32)) for i in range(8)]
        col = lambda name: pcols(c, name)

        prepare(nc, c, a)
        sort_edges(nc, c)
        segment_sum(nc, c, c.sorted, DST, SRC, c.src_ranges, clear=False, fill=True)
        aggregate_product(nc, c, a["L0_gnn_W1"], col("L0_gnn_b1"), col("L0_gnn_g1"), col("L0_gnn_be1"))
        norm_product(nc, c, a["L0_gnn_W2"], col("L0_gnn_b2"), col("L0_gnn_g2"), col("L0_gnn_be2"))
        norm_to_rows(nc, c, residual=False)
        router(nc, c, a, "L0_ffn_Wr", "L0_ffn_br", E8, moe=True)
        expert_ffn(nc, c, a)
        combine(nc, c)
        message_rows(nc, c, a["L1_gnn_c1_w1"], a["L1_gnn_c1_b1"], from_x=True)
        segment_sum(nc, c, c.edges, SRC, DST, c.dst_ranges, clear=True, fill=False)
        aggregate_product(nc, c, a["L1_gnn_c1_w2"], col("L1_gnn_c1_b2"), col("L1_gnn_c1_g"), col("L1_gnn_c1_b"))
        norm_relu(nc, c, col("L1_gnn_bn1_g"), col("L1_gnn_bn1_b"))
        message_rows(nc, c, a["L1_gnn_c2_w1"], a["L1_gnn_c2_b1"], from_x=False)
        segment_sum(nc, c, c.edges, SRC, DST, c.dst_ranges, clear=True, fill=False)
        aggregate_product(nc, c, a["L1_gnn_c2_w2"], col("L1_gnn_c2_b2"), col("L1_gnn_c2_g"), col("L1_gnn_c2_b"))
        norm_relu(nc, c, col("L1_gnn_bn2_g"), col("L1_gnn_bn2_b"))
        norm_to_rows(nc, c, residual=True)
        router(nc, c, a, "L1_ffn_gW", "L1_ffn_gb", 4, moe=False)
        gated_mlp(nc, c, a, out_dram)


def kernel(**inputs):
    import concourse.bacc as _bacc
    from concourse.bass_utils import run_bass_kernel_spmd as _run

    nc = _bacc.Bacc("TRN2", target_bir_lowering=False, num_devices=1)
    arrays, args = {}, {}
    for name, value in inputs.items():
        v = np.ascontiguousarray(value)
        arrays[f"in_{name}"] = v
        args[name] = nc.dram_tensor(f"in_{name}", v.shape, mybir.dt.from_np(v.dtype), kind="ExternalInput").ap()
    out = nc.dram_tensor("out_x", (N, D), F32, kind="ExternalOutput").ap()
    build(nc, args, out)
    r = _run(nc, [arrays], core_ids=[0])
    return r.results[0]["out_x"]
```

```python
from contextlib import ExitStack

import numpy as np
import concourse.bass as bass
from concourse import mybir

F32 = mybir.dt.float32
I32 = mybir.dt.int32
BF16 = mybir.dt.bfloat16
ALU = mybir.AluOpType
ACT = mybir.ActivationFunctionType
AX = mybir.AxisListType

P = 128
N = 6250
D = 256
KD = D // P
NB = 50
FULL = N // P
REST = N - FULL * P
BLK = 2 * P
NJ = NB // 2
LAST = N - (NJ - 1) * BLK
EDGES = 100000
SRC, DST, WEIGHT = range(3)
EPT = 784
EC = 7
ER = EPT // EC
G = 4
NG = EPT // G
RING = 7
LEAD = 3
EPS = 1e-5
PARTS = 5
PW = NB // PARTS
E8, H = 8, 1024
KH = H // P
TOK = 256
MT = (2 * N - E8) // TOK + E8
DUMP = MT * TOK
XS_ROWS = DUMP + 4 * P
SLOTS_FFN = 4
STEPS_MIN = -(-2 * N // (TOK * SLOTS_FFN))
BIG = 1e4
CLAMPED = "node numbers are clamped to 0..N-1 before the ranges are made"


def take(eng, sem, n=1):
    eng.wait_ge(sem, n)
    eng.sem_inc(sem, -n)


def chain(eng, ins, sem):
    ins.then_inc(sem, 1)
    take(eng, sem)


class Chip:
    pass


def stage(nc, fn, name):
    with ExitStack() as ctx:
        tag, used = f"{name}{nc.next_id()}", []

        def sb(what, shape, dt=F32):
            return ctx.enter_context(nc.sbuf_tensor(f"{tag}_{what}", shape, dt))

        def sem(what):
            used.append(nc.alloc_semaphore(f"{tag}_{what}"))
            return used[-1]

        with nc.Block() as block:
            fn(block, sb, sem)
        nc.clear_and_free_semaphores(used)
        nc.all_engine_barrier()


def flat(t):
    return t[:].rearrange("p a b -> p (a b)")


def carve(area, start, shape):
    size = int(np.prod(shape))
    v = area[:, start:start + size]
    if len(shape) == 2:
        v = v.rearrange("p (a b) -> p a b", b=shape[1])
    if len(shape) == 3:
        v = v.rearrange("p (a b c) -> p a b c", b=shape[1], c=shape[2])
    return v


def tile_at(t, i):
    return t[:, bass.ds(i, 1), :].rearrange("p a d -> p (a d)")


def list_banks(lists):
    per = 512 // ER
    spans = [(k, min(k + per, EC)) for k in range(0, EC, per)]
    return [(i, k0, k1, i * len(spans) + m) for i in range(lists) for m, (k0, k1) in enumerate(spans)]


RANGE_BANK = len(list_banks(3))


def turn_lists(pe, c, lists, low_high, list_turned, range_rows):
    for i, k0, k1, bank in list_banks(len(lists)):
        for k in range(k0, k1):
            mm = pe.transpose(c.ps[bank][:, (k - k0) * ER:(k - k0 + 1) * ER], lists[i][:, k, :], c.ident[0:ER, 0:ER])
        mm.then_inc(list_turned, 1)
    take(pe, range_rows, 2)
    for w in range(2):
        pe.transpose(c.ps[RANGE_BANK][0:EC, w * P:w * P + ER], low_high[0:ER, w, :], c.ident[0:ER, 0:ER]).then_inc(list_turned, 1)


def copy_lists(dve, c, tables, keys, low_high, low_high_cols, range_f, range_i, list_turned, list_copied,
               range_rows, range_ready, v):
    for w, op in ((0, ALU.min), (1, ALU.max)):
        dve.tensor_reduce(low_high[0:ER, w, :], keys, AX.X, op).then_inc(range_rows, 1)
    for n, (i, k0, k1, bank) in enumerate(list_banks(len(tables))):
        dve.wait_ge(list_turned, n + 1)
        dve.tensor_copy(tables[i][:, k0 * ER:k1 * ER], c.ps[bank][:, 0:(k1 - k0) * ER]).then_inc(list_copied, 1)
    take(dve, list_copied, n + 1)
    dve.wait_ge(list_turned, n + 3)
    chain(dve, dve.tensor_scalar(low_high_cols[:], c.ps[RANGE_BANK][0:EC, 0:2 * P].rearrange("c (w e) -> c w e", w=2)[:, :, 0:ER],
                                 0.0, float(N - 1), ALU.max, ALU.min), v)
    for w, op in ((0, ALU.min), (1, ALU.max)):
        chain(dve, dve.tensor_reduce(range_f[:, :, w], low_high_cols[:, w, :].rearrange("c (g t) -> c g t", t=G),
                                     AX.X, op), v)
    chain(dve, dve.tensor_scalar(range_f[:, :, 1], range_f[:, :, 1], float(P), None, ALU.add), v)
    chain(dve, dve.tensor_copy(range_i[:], range_f[:]), v)
    dve.tensor_scalar(range_i[:], range_i[:], P.bit_length() - 1, None, ALU.logical_shift_right).then_inc(range_ready, 1)


def place_ranges(sp, c, ranges, range_i, range_ready, range_out, range_in):
    sp.wait_ge(range_ready, 1)
    sp.dma_start(c.range_dram.rearrange("(c g) -> c g", c=EC), range_i[:].rearrange("c g w -> c (g w)")).then_inc(range_out, 16)
    sp.wait_ge(range_out, 16)
    sp.dma_start(ranges[:], c.range_dram[None, :].to_broadcast([P, NG * 2])).then_inc(range_in, 16)
    sp.wait_ge(range_in, 16)


def range_buffers(sb):
    return (sb("low_high", [P, 2, EC]), sb("low_high_cols", [EC, 2, ER]), sb("range_f", [EC, NG // EC, 2]),
            sb("range_i", [EC, NG // EC, 2], I32))


def prepare(nc, c, a):
    def run(block, sb, sem):
        af, tf = flat(c.A), flat(c.T)
        names = ("src", "dst", "edge_weight")
        raw = [af[:, i * EC * P:(i + 1) * EC * P] for i in range(3)]
        raw = [raw[0].bitcast(I32), raw[1].bitcast(I32), raw[2]]
        asf = [tf[:, 0:EC * P], tf[:, EC * P:2 * EC * P], raw[2]]
        lists = [x[0:ER, :].rearrange("r (k e) -> r k e", e=P) for x in asf]
        prow = carve(tf, 2 * EC * P, (2, P))
        low_high, low_high_cols, range_f, range_i = range_buffers(sb)
        x_in, edges_in, par_in = sem("x_in"), sem("edges_in"), sem("par_in")
        pads, consts, floats, made, v = (sem(n) for n in ("pads", "consts", "floats", "made", "v"))
        list_turned, list_copied, par_turned = sem("list_turned"), sem("list_copied"), sem("par_turned")
        range_rows, range_ready, range_out, range_in = (sem(n) for n in ("range_rows", "range_ready", "range_out", "range_in"))
        cols, record_out = sem("cols"), sem("record_out")

        @block.sync
        def _(sp):
            sp.wait_ge(pads, 1)
            whole = (EC - 1) * ER
            tail = EDGES // P - whole
            for i, name in enumerate(names):
                e = a[name]
                sp.dma_start(raw[i][0:ER, 0:(EC - 1) * P].rearrange("r (c e) -> r c e", e=P),
                             e[0:whole * P].rearrange("(c r e) -> r c e", r=ER, e=P)).then_inc(edges_in, 16)
                sp.dma_start(raw[i][0:tail, (EC - 1) * P:EC * P],
                             e[whole * P:(whole + tail) * P].rearrange("(r e) -> r e", e=P)).then_inc(edges_in, 16)
                sp.dma_start(raw[i][tail:tail + 1, (EC - 1) * P:(EC - 1) * P + EDGES % P],
                             e[(whole + tail) * P:EDGES].rearrange("(r e) -> r e", r=1)).then_inc(edges_in, 16)
            sp.wait_ge(pads, 2)
            for half in range(2):
                lo, hi = half * FULL // 2, (half + 1) * FULL // 2
                sp.dma_start(c.X[:, lo:hi, :],
                             a["x"][lo * P:hi * P, :].rearrange("(t p) d -> p t d", p=P)).then_inc(x_in, 16)
            sp.dma_start(c.X[0:REST, FULL, :], a["x"][FULL * P:N, :]).then_inc(x_in, 16)
            sp.dma_start(c.eps[:], a["L0_gnn_eps"][None, :].to_broadcast([P, 1])).then_inc(x_in, 16)
            place_ranges(sp, c, c.dst_ranges, range_i, range_ready, range_out, range_in)
            sp.wait_ge(cols, 1)
            for lo, w, at in ((0, KD, 0), (KD * E8, KD, KD), (2 * KD * E8, KH, 2 * KD)):
                sp.dma_start(c.expert_dram[:, :, at:at + w].rearrange("e p w -> p e w"),
                             c.pcol[:, P + lo:P + lo + E8 * w].rearrange("p (e w) -> p e w", w=w)).then_inc(record_out, 16)
            sp.wait_ge(x_in, 64)
            sp.wait_ge(record_out, 48)

        @block.scalar
        def _(act):
            act.wait_ge(pads, 2)
            for name, (at, rows) in c.pat.items():
                ap = a[name]
                if len(ap.shape) == 2:
                    ap = ap.rearrange("a b -> (a b)")
                act.dma_start(prow[at % P:at % P + rows, at // P, :],
                              ap.rearrange("(r e) -> r e", e=P)).then_inc(par_in, 16)
            act.wait_ge(par_in, 16 * len(c.pat))

        @block.gpsimd
        def _(pool):
            pool.memset(c.ident[:], 0.0).then_inc(made, 1)
            pool.memset(c.upper[:], 1.0).then_inc(made, 1)
            pool.memset(c.ones[:], 1.0).then_inc(made, 1)
            pool.wait_ge(made, 3)
            pool.affine_select(out=c.ident[:], in_=c.ident[:], compare_op=ALU.not_equal, fill=1.0,
                               base=0, pattern=[[-1, P]], channel_multiplier=1).then_inc(consts, 1)
            pool.affine_select(out=c.upper[:], in_=c.upper[:], compare_op=ALU.is_gt, fill=0.0,
                               base=0, pattern=[[1, P]], channel_multiplier=-1).then_inc(consts, 1)
            pool.iota(c.iota[:], pattern=[[1, c.iota.shape[1]]], base=0, channel_multiplier=0,
                      allow_small_or_imprecise_dtypes=True).then_inc(consts, 1)
            pool.iota(c.node[:], pattern=[[P, NB]], base=0, channel_multiplier=1,
                      allow_small_or_imprecise_dtypes=True).then_inc(consts, 1)
            pool.wait_ge(consts, 4)

        @block.tensor
        def _(pe):
            pe.wait_ge(consts, 1)
            pe.wait_ge(floats, 2)
            turn_lists(pe, c, lists, low_high, list_turned, range_rows)
            pe.wait_ge(par_in, 16 * len(c.pat))
            for w in range(2):
                pe.transpose(c.ps[RANGE_BANK + 1][:, w * P:w * P + P], prow[:, w, :], c.ident[:]).then_inc(par_turned, 1)

        @block.vector
        def _(dve):
            last = slice((EC - 1) * P, EC * P)
            chain(dve, dve.memset(raw[0][0:ER, last], 0), v)
            chain(dve, dve.memset(raw[1][0:ER, last], N - 1), v)
            dve.memset(raw[2][0:ER, last], 0.0).then_inc(pads, 1)
            chain(dve, dve.memset(prow, 0.0), v)
            chain(dve, dve.memset(c.X[:, FULL:NB, :], 0.0), v)
            dve.sem_inc(pads, 1)
            dve.wait_ge(edges_in, 9 * 16)
            dve.tensor_copy(asf[0][0:ER, :], raw[0][0:ER, :]).then_inc(floats, 1)
            dve.tensor_copy(asf[1][0:ER, :], raw[1][0:ER, :]).then_inc(floats, 1)
            dve.wait_ge(floats, 2)
            copy_lists(dve, c, [c.edges[:, i, :] for i in range(3)], lists[1], low_high, low_high_cols, range_f, range_i,
                       list_turned, list_copied, range_rows, range_ready, v)
            dve.wait_ge(par_turned, 2)
            dve.tensor_copy(c.pcol[:], c.ps[RANGE_BANK + 1][:, 0:2 * P]).then_inc(cols, 1)
            dve.wait_ge(x_in, 64)
            chain(dve, dve.tensor_scalar(c.eps[:], c.eps[:], 1.0, None, ALU.add), v)
    stage(nc, run, "prepare")


def sort_edges(nc, c):
    NT = FULL + 1
    RB = 512 // ER
    RW = 8
    RP = 7
    STEPS = EPT // (RP * RW)

    def run(block, sb, sem):
        af, tf = flat(c.A), flat(c.T)
        tile_f, tile_i, place = tf[:, 0:EPT], tf[:, EPT:2 * EPT].bitcast(I32), tf[:, 2 * EPT:3 * EPT]
        rec = carve(tf, 3 * EPT, (EPT, 4))
        words = NT * ER // 2
        masks = [af[:, i * words:(i + 1) * words].bitcast(BF16).rearrange("p (b t) -> p b t", t=ER) for i in range(2)]
        mask = masks[0]
        prod = carve(af, words, (NT, ER))
        keep = af[:, 3 * words:3 * words + RB * ER]
        start, chunk_total, total = (sb(n, [P, NT]) for n in ("start", "chunk_total", "total"))
        not_before, ones = sb("not_before", [P, P], BF16), sb("ones", [P, P], BF16)
        ring_rec, ring_idx = sb("ring_rec", [P, RP, RW, 4]), sb("ring_idx", [P, RP, RW], I32)
        first_node = sb("first_node", [P, NG])
        back = carve(tf, 7 * EPT, (EC, 4 * P))[0:ER]
        lists = [back.rearrange("r k (e f) -> r k e f", f=4)[:, :, :, i] for i in range(3)]
        low_high, low_high_cols, range_f, range_i = range_buffers(sb)
        v, counted, mask_ready, chunk_placed = (sem(n) for n in ("v", "counted", "mask_ready", "chunk_placed"))
        count_mask, mask_free = pair(sem, "count_mask"), pair(sem, "mask_free")
        ranked, bank_free = pair(sem, "ranked"), pair(sem, "bank_free")
        ring_ready, scattered = ([sem(f"{n}{h}") for h in range(RP)] for n in ("ring_ready", "scattered"))
        laid, copied, back_in = sem("laid"), sem("copied"), sem("back_in")
        go, done, normed, h_out = sem("go"), sem("done"), sem("normed"), [sem(f"h_out{i}") for i in range(PARTS)]
        list_turned, list_copied = sem("list_turned"), sem("list_copied")
        range_rows, range_ready, range_out, range_in = (sem(n) for n in ("range_rows", "range_ready", "range_out", "range_in"))
        groups = [(g % 2, g * RB, min(RB, NT - g * RB)) for g in range(-(-NT // RB))]

        HALF = ER // 2
        CB = 512 // HALF
        count_banks = [(i, i * CB, min(CB, NT - i * CB)) for i in range(-(-NT // CB))]

        def build_mask(dve, k, mask=mask):
            return dve.tensor_tensor(mask, c.iota[:, 0:NT][:, :, None].to_broadcast([P, NT, ER]),
                                     tile_f[:, bass.ds(k * ER, ER)][:, None, :].to_broadcast([P, NT, ER]), ALU.is_equal)

        @block.vector
        def _(dve):
            tt, ts = dve.tensor_tensor, dve.tensor_scalar
            tt(not_before[:], c.upper[:], c.ones[:], ALU.subtract).then_inc(laid, 1)
            dve.tensor_copy(ones[:], c.ones[:]).then_inc(laid, 1)
            chain(dve, dve.memset(rec[:, :, 3], 0.0), v)
            for i in range(3):
                dve.tensor_copy(rec[:, :, i], c.edges[:, i, :]).then_inc(laid, 1)
            chain(dve, dve.memset(keep, 1.0), v)
            dve.memset(keep.rearrange("p (b t) -> p b t", t=ER)[:, :, 0:1], 0.0).then_inc(laid, 1)
            chain(dve, dve.tensor_copy(tile_i, c.edges[:, SRC, :]), v)
            chain(dve, ts(tile_i, tile_i, P.bit_length() - 1, None, ALU.logical_shift_right), v)
            dve.tensor_copy(tile_f, tile_i).then_inc(laid, 1)
            take(dve, laid, 7)
            def count_chunk(k, s):
                take(dve, mask_free[s])
                build_mask(dve, k, masks[s]).then_inc(count_mask[s], 1)

            for s in range(2):
                dve.sem_inc(mask_free[s], 1)
            with dve.Fori(0, EC // 2) as q:
                count_chunk(q * 2, 0)
                count_chunk(q * 2 + 1, 1)
            count_chunk(EC - 1, 0)
            take(dve, counted)
            for i, b0, nb in count_banks:
                dve.tensor_reduce(total[:, b0:b0 + nb], c.ps[i][:, 0:nb * HALF].rearrange("p (b t) -> p b t", t=HALF),
                                  AX.X, ALU.add).then_inc(v, 1)
            take(dve, v, len(count_banks))
            chain(dve, dve.tensor_tensor_scan(start[:], c.ones[:, 0:NT], total[:], 0.0, ALU.mult, ALU.add), v)
            chain(dve, tt(start[:], start[:], total[:], ALU.subtract), v)
            for s in range(2):
                dve.sem_inc(bank_free[s], 1)

            def place_chunk(k):
                chain(dve, build_mask(dve, k), v)
                dve.sem_inc(mask_ready, 1)
                for s, b0, nb in groups:
                    w = nb * ER
                    before_less, tot = c.ps[s][:, 0:w], c.ps[2 + s][:, 0:w]
                    out = prod[:, b0:b0 + nb, :]
                    flat_out = out.rearrange("p b t -> p (b t)")
                    take(dve, ranked[s])
                    chain(dve, dve.tensor_tensor_scan(flat_out, keep[:, 0:w], tot, 0.0, ALU.mult, ALU.add), v)
                    chain(dve, dve.tensor_copy(chunk_total[:, b0:b0 + nb], out[:, :, ER - 1]), v)
                    chain(dve, tt(flat_out, flat_out, before_less, ALU.add), v)
                    dve.sem_inc(bank_free[s], 1)
                chain(dve, tt(prod, prod, bcast(start[:], ER), ALU.add), v)
                chain(dve, tt(prod, prod, mask, ALU.mult), v)
                chain(dve, dve.tensor_reduce(place[:, bass.ds(k * ER, ER)], prod.rearrange("p b t -> p t b"), AX.X, ALU.add), v)
                dve.sem_inc(chunk_placed, ER // RW)
                chain(dve, tt(start[:], start[:], chunk_total[:], ALU.add), v)

            place_chunk(0)
            with dve.Fori(0, NB) as t:
                stat_tile(dve, c, t)
            dve.drain().then_inc(v, 1)
            take(dve, v)
            finish_stats(dve, go, done, c, v)
            with dve.Fori(1, EC) as k:
                place_chunk(k)
            for i in range(PARTS):
                x, h = (t[:, i * PW:(i + 1) * PW, :] for t in (c.X, c.A))
                mean, rstd = (bcast(t[:, i * PW:(i + 1) * PW], D) for t in (c.mean, c.rstd))
                chain(dve, tt(h, x, mean, ALU.subtract), v)
                tt(h, h, rstd, ALU.mult).then_inc(normed, 1)
            for i in range(PARTS):
                dve.wait_ge(h_out[i], 16)
                rows = c.A[:, i * PW:(i + 1) * PW, :]
                chain(dve, ts(rows, rows, c.eps[:, 0:1], None, ALU.mult), v)
            dve.wait_ge(back_in, 16)
            copy_lists(dve, c, [c.sorted[:, i, :] for i in range(3)], lists[0], low_high, low_high_cols, range_f, range_i,
                       list_turned, list_copied, range_rows, range_ready, v)
            dve.wait_ge(range_in, 16)
            for table, key, ranges in ((c.sorted, SRC, c.src_ranges), (c.edges, DST, c.dst_ranges)):
                first = ranges[:].rearrange("p (g w) -> p g w", w=2)[:, :, 0]
                keys = table[:, key, :].rearrange("p (g t) -> p g t", t=G)
                chain(dve, ts(first_node[:], first, float(P), None, ALU.mult), v)
                chain(dve, tt(keys, keys, bcast(first_node[:], G), ALU.subtract), v)

        @block.tensor
        def _(pe):
            def count_chunk(s, first, last):
                take(pe, count_mask[s])
                for i, b0, nb in count_banks:
                    for half in range(2):
                        mm = pe.matmul(c.ps[i][:, 0:nb * HALF], ones[:],
                                       masks[s][:, b0:b0 + nb, half * HALF:(half + 1) * HALF],
                                       start=(first and half == 0), stop=(last and half == 1))
                mm.then_inc(counted if last else mask_free[s], 1)

            count_chunk(0, True, False)
            with pe.Fori(0, EC // 2 - 1):
                count_chunk(1, False, False)
                count_chunk(0, False, False)
            count_chunk(1, False, False)
            count_chunk(0, False, True)
            with pe.Fori(0, EC):
                take(pe, mask_ready)
                for s, b0, nb in groups:
                    m = mask[:, b0:b0 + nb, :].rearrange("p b t -> p (b t)")
                    take(pe, bank_free[s])
                    pe.matmul(c.ps[s][:, 0:nb * ER], not_before[:], m, start=True, stop=True)
                    pe.matmul(c.ps[2 + s][:, 0:nb * ER], ones[:], m, start=True, stop=True).then_inc(ranked[s], 1)
            pe.wait_ge(back_in, 16)
            turn_lists(pe, c, lists, low_high, list_turned, range_rows)

        @block.scalar
        def _(act):
            def fill(i, h):
                take(act, chunk_placed)
                t = i * (RP * RW) + h * RW
                act.copy(ring_rec[:, h], rec[:, bass.ds(t, RW), :]).then_inc(copied, 1)
                act.copy(ring_idx[:, h], place[:, bass.ds(t, RW)]).then_inc(copied, 1)
                take(act, copied, 2)
                act.sem_inc(ring_ready[h], 1)

            for h in range(RP):
                fill(0, h)
            root(act, go, done, c.rstd)
            with act.Fori(1, STEPS) as i:
                for h in range(RP):
                    act.wait_ge(scattered[h], i * (16 * RW))
                    fill(i, h)

        @block.gpsimd
        def _(pool):
            with pool.Fori(0, STEPS):
                for h in range(RP):
                    take(pool, ring_ready[h])
                    for j in range(RW):
                        pool.indirect_dma_start(c.record_dram, bass.IndirectOffsetOnAxis(ap=ring_idx[:, h, j:j + 1], axis=0),
                                                ring_rec[:, h, j, :], None).then_inc(scattered[h], 16)

        @block.sync
        def _(sp):
            for i in range(PARTS):
                sp.wait_ge(normed, i + 1)
                sp.dma_start(c.h_dram[i * PW * P:(i + 1) * PW * P, :].rearrange("(t p) d -> p t d", p=P),
                             c.A[:, i * PW:(i + 1) * PW, :]).then_inc(h_out[i], 16)
            for i in range(PARTS):
                sp.wait_ge(h_out[i], 16)
            for h in range(RP):
                sp.wait_ge(scattered[h], STEPS * RW * 16)
            sp.dma_start(back, c.record_dram.rearrange("(k r e) f -> r k (e f)", r=ER, e=P)).then_inc(back_in, 16)
            place_ranges(sp, c, c.src_ranges, range_i, range_ready, range_out, range_in)
    stage(nc, run, "sort_edges")


def stat_tile(dve, c, t):
    return dve.bn_stats(c.st[:, bass.ds(t, 1), :].rearrange("p a s -> p (a s)"), tile_at(c.X, t))


def finish_stats(dve, act_go, act_done, c, v):
    st = c.st
    chain(dve, dve.tensor_tensor(c.mean[:], st[:, :, 1], st[:, :, 4], ALU.add), v)
    chain(dve, dve.tensor_scalar(c.mean[:], c.mean[:], 0.5, None, ALU.mult), v)
    chain(dve, dve.tensor_tensor(st[:, :, 0], st[:, :, 1], st[:, :, 4], ALU.subtract), v)
    chain(dve, dve.scalar_tensor_tensor(st[:, :, 1], st[:, :, 0], 0.25, st[:, :, 0], ALU.mult, ALU.mult), v)
    chain(dve, dve.tensor_tensor(st[:, :, 2], st[:, :, 2], st[:, :, 5], ALU.add), v)
    chain(dve, dve.scalar_tensor_tensor(c.var[:], st[:, :, 2], 1.0 / D, st[:, :, 1], ALU.mult, ALU.add), v)
    dve.tensor_scalar(c.rstd[:], c.var[:], EPS, None, ALU.add).then_inc(act_go, 1)
    take(dve, act_done)
    chain(dve, dve.reciprocal(c.rstd[:], c.rstd[:]), v)
    chain(dve, dve.scalar_tensor_tensor(c.shift[:], c.mean[:], -1.0, c.rstd[:], ALU.mult, ALU.mult), v)


def norm_block(act, c, out, j):
    for q in range(2):
        t = j * 2 + q
        ins = act.activation(out[:, q, :], tile_at(c.X, t), ACT.Identity,
                             bias=c.shift[:, bass.ds(t, 1)], scale=c.rstd[:, bass.ds(t, 1)])
    return ins


def norm_tile(dve, out, c, t, scale):
    return dve.tensor_scalar(out, tile_at(c.X, t), c.mean[:, bass.ds(t, 1)], scale[:, bass.ds(t, 1)],
                             ALU.subtract, ALU.mult)


def root(act, go, done, x):
    take(act, go)
    act.sqrt(x[:], x[:]).then_inc(done, 1)


def segment_sum(nc, c, edges, take_from, add_to, ranges, clear, fill):
    def run(block, sb, sem):
        free = flat(c.T)[:, D + 3 * EPT:]
        msg = carve(free, 0, (RING * G, D))
        hot = carve(free, RING * G * D, (3, G, P))
        idx, edge = sb("idx", [P, RING, G], I32), sb("edge", [P, RING, 3, G])
        acc = c.ps[0:3]
        rings = lambda name: [sem(f"{name}{h}") for h in range(RING)]
        copied, idx_ready, keys_ready = sem("copied"), rings("idx_ready"), rings("keys_ready")
        landed, scaled, slots_free = rings("landed"), rings("scaled"), rings("slots_free")
        hot_ready, summed = [sem(f"hot_ready{s}") for s in range(3)], [sem(f"summed{s}") for s in range(3)]
        v, zero, zeroed, filled, parts_filled = (sem(n) for n in ("v", "zero", "zeroed", "filled", "parts_filled"))
        skipped_filled = sem("skipped_filled")
        zeros = flat(c.T)[:, 0:D]

        def node_tiles(eng, g):
            _, (lo, hi) = nc.values_load_multi_w_load_instructions(
                ranges[0:1, bass.ds(g * 2, 2)], engines=[eng], min_val=0, max_val=FULL + 1, skip_runtime_bounds_check_because=CLAMPED)
            return nc.s_assert_within(lo, 0, FULL, skip_runtime_bounds_check_because=CLAMPED), hi

        if fill:
            @block.sync
            def _(sp):
                sp.wait_ge(zeroed, 1)
                share = 4
                skipped = c.ys_dram[STEPS_MIN * SLOTS_FFN * TOK:MT * TOK, :]
                sp.dma_start(skipped.rearrange("(p t) d -> p t d", p=P),
                             zeros[:, None, :].to_broadcast([P, skipped.shape[0] // P, D])).then_inc(skipped_filled, 16)
                sp.wait_ge(skipped_filled, 16)
                with sp.Fori(0, XS_ROWS // P // share) as k:
                    sp.dma_start(c.xs_dram[bass.ds(k * (share * P), share * P), :].rearrange("(p t) d -> p t d", p=P),
                                 zeros[:, None, :].to_broadcast([P, share, D])).then_inc(filled, 16)
                    sp.wait_ge(filled, k * 16 + 16)
                    sp.sem_inc(parts_filled, 1)

        @block.gpsimd
        def _(pool):
            with pool.Fori(0, NG // RING):
                for h in range(RING):
                    take(pool, idx_ready[h])
                    for j in range(G):
                        pool.indirect_dma_start(msg[:, h * G + j, :], None, c.h_dram,
                                                bass.IndirectOffsetOnAxis(ap=idx[:, h, j:j + 1], axis=0)
                                                ).then_inc(landed[h], 16)

        @block.scalar
        def _(act):
            def fetch(g, h):
                chain(act, act.copy(edge[:, h], edges[:, :, bass.ds(g * G, G)]), copied)
                act.sem_inc(keys_ready[h], 1)
                act.copy(idx[:, h, :], edge[:, h, take_from, :]).then_inc(idx_ready[h], 1)

            def scale(q, h):
                act.wait_ge(landed[h], q * (16 * G) + 16 * G)
                for j in range(G):
                    m = msg[:, h * G + j, :]
                    ins = act.activation(m, m, ACT.Identity, scale=edge[:, h, WEIGHT, j:j + 1])
                ins.then_inc(scaled[h], 1)

            for h in range(RING):
                fetch(h, h)
            for h in range(LEAD):
                scale(0, h)
            with act.Fori(0, NG // RING - 1) as q:
                for h in range(RING):
                    scale(q + (h + LEAD) // RING, (h + LEAD) % RING)
                    take(act, slots_free[h])
                    fetch((q + 1) * RING + h, h)
            for h in range(LEAD, RING):
                scale(NG // RING - 1, h)

        @block.tensor
        def _(pe):
            def products(h, s):
                take(pe, hot_ready[s])
                for j in range(G):
                    mm = pe.matmul(acc[s][:, 0:D], hot[:, s, j, :], msg[:, h * G + j, :],
                                   start=(j == 0), stop=(j == G - 1))
                mm.then_inc(summed[s], 1)

            with pe.Fori(0, NG // RING) as q:
                for h in range(RING):
                    take(pe, scaled[h])
                    products(h, h % 2)
                    lo, hi = node_tiles(mybir.EngineType.PE, q * RING + h)
                    with pe.If(lo + 1 < hi):
                        with pe.Fori(lo + 1, hi):
                            products(h, 2)

        @block.vector
        def _(dve):
            def matrices(h, skip, s):
                cols = c.iota[:, 0:P] if skip is None else c.iota[:, bass.ds(skip * P, P)]
                dve.tensor_tensor(hot[:, s], cols[:, None, :].to_broadcast([P, G, P]),
                                  edge[:, h, add_to, :][:, :, None].to_broadcast([P, G, P]), ALU.is_equal).then_inc(hot_ready[s], 1)

            def add(b, s):
                take(dve, summed[s])
                chain(dve, dve.tensor_tensor(tile_at(c.A, b), tile_at(c.A, b), acc[s][:, 0:D], ALU.add), v)

            def finish(h, lo, hi):
                with dve.If(lo + 1 < hi):
                    with dve.Fori(lo + 1, hi) as b:
                        skip = nc.s_assert_within(b - lo, 1, FULL, skip_runtime_bounds_check_because=CLAMPED)
                        matrices(h, skip, 2)
                        add(b, 2)
                add(lo, h % 2)
                dve.sem_inc(slots_free[h], 1)

            if fill:
                dve.memset(zeros, 0.0).then_inc(zeroed, 1)
            if clear:
                chain(dve, dve.memset(c.A[:], 0.0), zero)
            with dve.Fori(0, NG // RING) as q:
                last = None
                for h in range(RING):
                    take(dve, keys_ready[h])
                    matrices(h, None, h % 2)
                    if last:
                        finish(*last)
                    last = (h, *node_tiles(mybir.EngineType.DVE, q * RING + h))
                finish(*last)
    stage(nc, run, "segment_sum")


def blocks(eng, body):
    with eng.Fori(0, NJ // 2) as q:
        body(q * 2, 0)
        body(q * 2 + 1, 1)
    body(NJ - 1, 0)


def ahead(eng, first, second):
    first(0)
    with eng.Fori(0, NJ // 2) as q:
        first(1)
        second(q * 2, 0)
        first(0)
        second(q * 2 + 1, 1)
    second(NJ - 1, 0)


def two_ahead(eng, first, second):
    first(0, 0)
    first(1, 1)
    with eng.Fori(0, NJ // 2 - 1) as q:
        first(q * 2 + 2, 0)
        second(q * 2, 0)
        first(q * 2 + 3, 1)
        second(q * 2 + 1, 1)
    first(NJ - 1, 0)
    second(NJ - 3, 0)
    second(NJ - 2, 1)
    second(NJ - 1, 0)


def pair(sem, name):
    return [sem(f"{name}{s}") for s in range(2)]


def cols_block(c, j):
    return c.T[:, :, bass.ds(j * BLK, BLK)]


def pcols(c, name, n=KD, skip=0):
    at = c.pat[name][0] + skip
    return c.pcol[:, at:at + n]


def turn_to_cols(pe, c, row, turn):
    for s in range(2):
        for k in range(KD):
            mm = pe.transpose(turn[:, k * BLK + s * P:k * BLK + (s + 1) * P], row[:, s, k * P:(k + 1) * P], c.ident[:])
    return mm


def store_cols(act, c, j, src, bias):
    for m in range(KD):
        ins = act.activation(c.T[:, m, bass.ds(j * BLK, BLK)], src[:, m * BLK:(m + 1) * BLK], ACT.Identity,
                             bias=bias[:, m:m + 1])
    return ins


def apply_affine(act, c, out, src, func):
    for m in range(KD):
        ins = act.activation(out[:, m, :], src[:, m, :], func, bias=c.affine[:, 1, m:m + 1], scale=c.affine[:, 0, m:m + 1])
    return ins


def product_cols(pe, w, rhs, out):
    for m in range(KD):
        for k in range(KD):
            mm = pe.matmul(out[:, m * BLK:(m + 1) * BLK], w[:, k, m * P:(m + 1) * P], rhs[:, k, :],
                           start=(k == 0), stop=(k == KD - 1))
    return mm


def stats_blocks(dve, c, stats, stored):
    def one(j, n):
        take(dve, stored)
        for m in range(KD):
            ins = dve.bn_stats(stats[:, m, bass.ds(j, 1), :].rearrange("p a s -> p (a s)"), c.T[:, m, bass.ds(j * BLK, n)])
        return ins
    return one


def finish_affine(dve, c, stats, agg, gamma, beta, go, done, v):
    for m in range(KD):
        chain(dve, dve.bn_aggr(agg[:, m, :], stats[:, m, :, :].rearrange("p j s -> p (j s)")), v)
    dve.tensor_scalar(c.affine[:, 0, :], agg[:, :, 1], EPS, None, ALU.add).then_inc(go, 1)
    take(dve, done)
    chain(dve, dve.reciprocal(c.affine[:, 0, :], c.affine[:, 0, :]), v)
    chain(dve, dve.tensor_tensor(c.affine[:, 0, :], c.affine[:, 0, :], gamma, ALU.mult), v)
    chain(dve, dve.tensor_tensor(c.affine[:, 1, :], agg[:, :, 0], c.affine[:, 0, :], ALU.mult), v)
    chain(dve, dve.tensor_tensor(c.affine[:, 1, :], beta, c.affine[:, 1, :], ALU.subtract), v)


def root_affine(act, c, go, done):
    take(act, go)
    act.sqrt(c.affine[:, 0, :], c.affine[:, 0, :]).then_inc(done, 1)


def aggregate_product(nc, c, w_dram, bias, gamma, beta):
    def run(block, sb, sem):
        w, row = sb("w", [P, KD, D]), [sb(f"row{s}", [P, 2, D]) for s in range(2)]
        stats, agg = sb("stats", [P, KD, NJ, 6]), sb("agg", [P, KD, 2])
        turn, out = c.ps[0:2], c.ps[2:4]
        w_in, v, go, done, kept, stored = (sem(n) for n in ("w_in", "v", "go", "done", "kept", "stored"))
        row_ready, row_free = pair(sem, "row_ready"), pair(sem, "row_free")
        turned, in_t, prod, out_free = pair(sem, "turned"), sem("in_t"), pair(sem, "prod"), pair(sem, "out_free")

        @block.sync
        def _(sp):
            sp.dma_start(w[:], w_dram.rearrange("(k p) n -> p k n", p=P)).then_inc(w_in, 16)
            sp.wait_ge(w_in, 16)

        @block.gpsimd
        def _(pool):
            def rows(j, s):
                take(pool, row_free[s])
                pool.tensor_copy(row[s][:], c.A[:, bass.ds(j * 2, 2), :]).then_inc(row_ready[s], 1)
            blocks(pool, rows)

        @block.scalar
        def _(act):
            def store(j, s):
                take(act, prod[s])
                chain(act, store_cols(act, c, j, out[s], bias), kept)
                act.sem_inc(out_free[s], 1)
                act.sem_inc(stored, 1)

            blocks(act, store)
            root_affine(act, c, go, done)

        @block.tensor
        def _(pe):
            def turn_rows(s):
                take(pe, row_ready[s])
                turn_to_cols(pe, c, row[s], turn[s]).then_inc(turned[s], 1)

            def product(j, s):
                take(pe, in_t)
                take(pe, out_free[s])
                product_cols(pe, w, cols_block(c, j), out[s]).then_inc(prod[s], 1)

            pe.wait_ge(w_in, 16)
            ahead(pe, turn_rows, product)

        @block.vector
        def _(dve):
            def copy(j, s):
                take(dve, turned[s])
                dve.sem_inc(row_free[s], 1)
                dve.tensor_copy(cols_block(c, j), turn[s][:].rearrange("p (k n) -> p k n", k=KD)).then_inc(in_t, 1)

            stat = stats_blocks(dve, c, stats, stored)
            for s in range(2):
                dve.sem_inc(row_free[s], 1)
                dve.sem_inc(out_free[s], 1)
            copy(0, 0)
            copy(1, 1)
            with dve.Fori(0, NJ // 2 - 1) as q:
                copy(q * 2 + 2, 0)
                stat(q * 2, BLK)
                copy(q * 2 + 3, 1)
                stat(q * 2 + 1, BLK)
            copy(NJ - 1, 0)
            stat(NJ - 3, BLK)
            stat(NJ - 2, BLK)
            chain(dve, stat(NJ - 1, LAST), v)
            finish_affine(dve, c, stats, agg, gamma, beta, go, done, v)
    stage(nc, run, "aggregate_product")


def norm_product(nc, c, w_dram, bias, gamma, beta):
    def run(block, sb, sem):
        w = sb("w", [P, KD, D])
        stats, agg = sb("stats", [P, KD, NJ, 6]), sb("agg", [P, KD, 2])
        out = c.ps[2:4]
        w_in, v, go, done, stored = (sem(n) for n in ("w_in", "v", "go", "done", "stored"))
        normed, prod, out_free = sem("normed"), pair(sem, "prod"), pair(sem, "out_free")

        @block.sync
        def _(sp):
            sp.dma_start(w[:], w_dram.rearrange("(k p) n -> p k n", p=P)).then_inc(w_in, 16)
            sp.wait_ge(w_in, 16)

        @block.scalar
        def _(act):
            def norm(j, s):
                apply_affine(act, c, cols_block(c, j), cols_block(c, j), ACT.Relu).then_inc(normed, 1)

            blocks(act, norm)
            root_affine(act, c, go, done)

        @block.tensor
        def _(pe):
            def product(j, s):
                take(pe, normed)
                take(pe, out_free[s])
                product_cols(pe, w, cols_block(c, j), out[s]).then_inc(prod[s], 1)

            pe.wait_ge(w_in, 16)
            blocks(pe, product)

        @block.vector
        def _(dve):
            stat = stats_blocks(dve, c, stats, stored)

            def store(j, s, n=BLK):
                take(dve, prod[s])
                for m in range(KD):
                    ins = dve.tensor_scalar(c.T[:, m, bass.ds(j * BLK, BLK)], out[s][:, m * BLK:(m + 1) * BLK],
                                            bias[:, m:m + 1], None, ALU.add)
                ins.then_inc(stored, 1)
                stat(j, n)
                dve.sem_inc(out_free[s], 1)

            for s in range(2):
                dve.sem_inc(out_free[s], 1)
            with dve.Fori(0, NJ // 2) as q:
                store(q * 2, 0)
                store(q * 2 + 1, 1)
            store(NJ - 1, 0, LAST)
            dve.drain().then_inc(v, 1)
            take(dve, v)
            finish_affine(dve, c, stats, agg, gamma, beta, go, done, v)
    stage(nc, run, "norm_product")


def norm_relu(nc, c, gamma, beta):
    def run(block, sb, sem):
        stats, agg = sb("stats", [P, KD, NJ, 6]), sb("agg", [P, KD, 2])
        v, go, done, stored = (sem(n) for n in ("v", "go", "done", "stored"))

        @block.scalar
        def _(act):
            with act.Fori(0, NJ) as j:
                apply_affine(act, c, cols_block(c, j), cols_block(c, j), ACT.Relu).then_inc(stored, 1)
            root_affine(act, c, go, done)

        @block.vector
        def _(dve):
            stat = stats_blocks(dve, c, stats, stored)
            with dve.Fori(0, NJ - 1) as j:
                stat(j, BLK)
            chain(dve, stat(NJ - 1, LAST), v)
            finish_affine(dve, c, stats, agg, gamma, beta, go, done, v)
    stage(nc, run, "norm_relu")


def norm_to_rows(nc, c, residual):
    def run(block, sb, sem):
        col = [sb(f"col{s}", [P, KD, BLK]) for s in range(2)]
        sum_ = [sb(f"sum{s}", [P, 2, D]) for s in range(2)]
        turn = c.ps[0:2]
        ready, free, turned, v = pair(sem, "ready"), pair(sem, "free"), pair(sem, "turned"), sem("v")
        residual_ready = pair(sem, "residual_ready")
        func = ACT.Identity if residual else ACT.Relu

        @block.scalar
        def _(act):
            def norm(j, s):
                take(act, free[s])
                if residual:
                    norm_block(act, c, sum_[s], j).then_inc(residual_ready[s], 1)
                apply_affine(act, c, col[s], cols_block(c, j), func).then_inc(ready[s], 1)
            blocks(act, norm)

        @block.tensor
        def _(pe):
            def turn_cols(j, s):
                take(pe, ready[s])
                for q in range(2):
                    for k in range(KD):
                        mm = pe.transpose(turn[s][:, q * D + k * P:q * D + (k + 1) * P],
                                          col[s][:, k, q * P:(q + 1) * P], c.ident[:])
                mm.then_inc(turned[s], 1)
            blocks(pe, turn_cols)

        @block.vector
        def _(dve):
            for s in range(2):
                dve.sem_inc(free[s], 1)

            def add(j, s):
                x = c.X[:, bass.ds(j * 2, 2), :]
                h = turn[s][:].rearrange("p (t d) -> p t d", t=2)
                if residual:
                    take(dve, residual_ready[s])
                    take(dve, turned[s])
                    chain(dve, dve.tensor_tensor(sum_[s][:], sum_[s][:], h, ALU.add), v)
                    chain(dve, dve.scalar_tensor_tensor(x, sum_[s][:], 0.0, x, ALU.max, ALU.add), v)
                else:
                    take(dve, turned[s])
                    chain(dve, dve.tensor_tensor(x, x, h, ALU.add), v)
                dve.sem_inc(free[s], 1)
                for q in range(2):
                    stat_tile(dve, c, j * 2 + q)
            blocks(dve, add)
    stage(nc, run, "norm_to_rows")


def message_rows(nc, c, w_dram, b_dram, from_x):
    def run(block, sb, sem):
        w, bias = sb("w", [P, KD, D]), sb("bias", [P, D])
        col = [sb(f"col{s}", [P, KD, BLK]) for s in range(2)]
        row = [sb(f"row{s}", [P, 2, D]) for s in range(2)]
        rows = c.A
        turn, out = c.ps[0:2], c.ps[2:4]
        w_in, v, go, done, kept, stored = (sem(n) for n in ("w_in", "v", "go", "done", "kept", "stored"))
        h_out, stats_ready, row_free = sem("h_out"), sem("stats_ready"), pair(sem, "row_free")
        row_ready, turned, col_ready, col_free = (pair(sem, n) for n in ("row_ready", "turned", "col_ready", "col_free"))
        prod, out_free, added = pair(sem, "prod"), pair(sem, "out_free"), sem("added")

        @block.sync
        def _(sp):
            sp.dma_start(w[:], w_dram.rearrange("(k p) n -> p k n", p=P)).then_inc(w_in, 16)
            sp.dma_start(bias[:], b_dram[None, :].to_broadcast([P, D])).then_inc(w_in, 16)
            sp.wait_ge(w_in, 32)
            with sp.Fori(0, NJ) as j:
                take(sp, stored)
                sp.dma_start(c.h_dram[bass.ds(j * BLK, BLK), :].rearrange("(t p) d -> p t d", p=P),
                             rows[:, bass.ds(j * 2, 2), :]).then_inc(h_out, 16)
            sp.wait_ge(h_out, 16 * NJ)

        @block.scalar
        def _(act):
            if from_x:
                root(act, go, done, c.rstd)
                take(act, stats_ready)

                def norm(j, s):
                    take(act, row_free[s])
                    norm_block(act, c, row[s], j).then_inc(row_ready[s], 1)
            else:
                def norm(j, s):
                    take(act, col_free[s])
                    apply_affine(act, c, col[s], cols_block(c, j), ACT.Relu).then_inc(col_ready[s], 1)

            def relu(j, s):
                take(act, added)
                r = rows[:, bass.ds(j * 2, 2), :]
                act.activation(r, r, ACT.Relu).then_inc(stored, 1)

            two_ahead(act, norm, relu)

        @block.tensor
        def _(pe):
            def turn_rows(s):
                take(pe, row_ready[s])
                turn_to_cols(pe, c, row[s], turn[s]).then_inc(turned[s], 1)

            def product(j, s):
                take(pe, col_ready[s])
                take(pe, out_free[s])
                for q in range(2):
                    for k in range(KD):
                        mm = pe.matmul(out[s][:, q * D:(q + 1) * D], col[s][:, k, q * P:(q + 1) * P], w[:, k, :],
                                       start=(k == 0), stop=(k == KD - 1))
                mm.then_inc(prod[s], 1)

            pe.wait_ge(w_in, 32)
            if from_x:
                ahead(pe, turn_rows, product)
            else:
                blocks(pe, product)

        @block.vector
        def _(dve):
            def copy(s):
                take(dve, turned[s])
                take(dve, col_free[s])
                dve.sem_inc(row_free[s], 1)
                dve.tensor_copy(col[s][:], turn[s][:].rearrange("p (k n) -> p k n", k=KD)).then_inc(col_ready[s], 1)

            def add(j, s):
                take(dve, prod[s])
                dve.sem_inc(col_free[s], 1)
                for q in range(2):
                    dve.tensor_tensor(tile_at(rows, j * 2 + q), out[s][:, q * D:(q + 1) * D], bias[:], ALU.add).then_inc(kept, 1)
                take(dve, kept, 2)
                dve.sem_inc(out_free[s], 1)
                dve.sem_inc(added, 1)

            for s in range(2):
                dve.sem_inc(col_free[s], 1)
                dve.sem_inc(out_free[s], 1)
            dve.wait_ge(w_in, 32)
            if from_x:
                finish_stats(dve, go, done, c, v)
                for s in range(2):
                    dve.sem_inc(row_free[s], 1)
                dve.sem_inc(stats_ready, 1)
                ahead(dve, copy, add)
            else:
                blocks(dve, add)
    stage(nc, run, "message_rows")


def bcast(ap, n):
    return ap[:, :, None].to_broadcast([ap.shape[0], ap.shape[1], n])


def router(nc, c, a, wr_name, br_name, ne, moe):
    SLOTS = 10

    def run(block, sb, sem):
        wr, br = sb("wr", [P, KD, ne]), sb("br", [P, ne])
        row = [sb(f"row{s}", [P, 2, D]) for s in range(2)]
        col = [sb(f"col{s}", [P, KD, BLK]) for s in range(2)]
        work = flat(c.T) if moe else flat(c.A)[:, NB * D // 2:]
        n3 = NB * ne
        logit, prob, eid, cand, pick1, pick2 = (carve(work, i * n3, (NB, ne)) for i in range(6))
        small = [carve(work, 6 * n3 + i * NB, (NB,)) for i in range(12)]
        top, total, p1, p2, first, q1, q2 = small[:7]
        tot, cum, cum2, pos = (carve(work, 3600 + i * n3, (NB, ne)) for i in range(4))
        turn, lg = c.ps[0:2], c.ps[2:4]
        w_in, v, go, done, mlp_in = (sem(n) for n in ("w_in", "v", "go", "done", "mlp_in"))
        row_ready, turned, col_ready, col_free, lg_ready = (pair(sem, n) for n in ("row_ready", "turned", "col_ready", "col_free", "lg_ready"))
        iota_done, exp_go, exp_done, kept = (sem(n) for n in ("iota_done", "exp_go", "exp_done", "kept"))
        rank_go, rank_done = sem("rank_go"), sem("rank_done")
        x_ready, scattered = ([sem(f"{n}{s}") for s in range(SLOTS)] for n in ("x_ready", "scattered"))
        in_t, stats_ready, row_free = sem("in_t"), sem("stats_ready"), pair(sem, "row_free")
        xr = carve(flat(c.T), 8192, (SLOTS, D)) if moe else None
        ring = sb("ring", [P, SLOTS, 2], I32) if moe else None
        idx = sb("idx", [P, NB, 2]) if moe else None
        scale2 = sb("scale2", [P, NB]) if moe else None
        end, endi = sb("end", [P, E8]), sb("endi", [P, E8], I32)
        base, end_last = sb("base", [P, E8]), sb("end_last", [P, 1])
        tiles = sb("tiles", [P, MT]) if moe else None
        tmp_t = sb("tmp_t", [P, MT]) if moe else None

        @block.sync
        def _(sp):
            sp.dma_start(wr[:], a[wr_name].rearrange("(k p) n -> p k n", p=P)).then_inc(w_in, 16)
            sp.dma_start(br[:], a[br_name][None, :].to_broadcast([P, ne])).then_inc(w_in, 16)
            sp.wait_ge(w_in, 32)
            if not moe:
                loads, _ = mlp_weights(c, a)
                for view, source in loads:
                    sp.dma_start(view, source).then_inc(mlp_in, 16)
                sp.wait_ge(mlp_in, 16 * len(loads))

        @block.gpsimd
        def _(pool):
            pool.iota(eid, pattern=[[0, NB], [1, ne]], base=0, channel_multiplier=0,
                      allow_small_or_imprecise_dtypes=True).then_inc(iota_done, 1)
            if moe:
                pool.iota(tiles[:], pattern=[[1, MT]], base=0, channel_multiplier=0,
                          allow_small_or_imprecise_dtypes=True).then_inc(iota_done, 1)

                def scatter(s):
                    take(pool, x_ready[s])
                    for i in range(2):
                        pool.indirect_dma_start(c.xs_dram, bass.IndirectOffsetOnAxis(ap=ring[:, s, i:i + 1], axis=0),
                                                xr[:, s, :], None).then_inc(scattered[s], 16)
                with pool.Fori(0, NB // SLOTS):
                    for s in range(SLOTS):
                        scatter(s)
                for s in range(SLOTS):
                    pool.wait_ge(scattered[s], 32 * (NB // SLOTS))
            else:
                pool.wait_ge(iota_done, 1)

        @block.scalar
        def _(act):
            root(act, go, done, c.rstd)
            if moe:
                root(act, go, done, scale2)
            take(act, stats_ready)

            def norm(j, s):
                take(act, row_free[s])
                norm_block(act, c, row[s], j).then_inc(row_ready[s], 1)

            def to_t(j, s):
                take(act, in_t)
                chain(act, act.copy(cols_block(c, j), col[s][:]), kept)
                act.sem_inc(col_free[s], 1)

            if moe:
                blocks(act, norm)
            else:
                two_ahead(act, norm, to_t)
            take(act, exp_go)
            act.activation(prob, logit, ACT.Exp).then_inc(exp_done, 1)
            if not moe:
                take(act, exp_go)
                act.activation(q1, q1, ACT.Exp).then_inc(exp_done, 1)
                act.activation(q2, q2, ACT.Exp).then_inc(exp_done, 1)

        @block.tensor
        def _(pe):
            def turn_rows(s):
                take(pe, row_ready[s])
                turn_to_cols(pe, c, row[s], turn[s]).then_inc(turned[s], 1)

            def logits(j, s):
                take(pe, col_ready[s])
                for q in range(2):
                    for k in range(KD):
                        mm = pe.matmul(lg[s][:, q * ne:(q + 1) * ne], col[s][:, k, q * P:(q + 1) * P], wr[:, k, :],
                                       start=(k == 0), stop=(k == KD - 1))
                mm.then_inc(lg_ready[s], 1)

            pe.wait_ge(w_in, 32)
            ahead(pe, turn_rows, logits)
            if moe:
                take(pe, rank_go)
                pe.matmul(c.ps[4][:, 0:n3], c.upper[:], cand.rearrange("p t e -> p (t e)"), start=True, stop=True)
                pe.matmul(c.ps[5][:, 0:n3], c.ones[:], cand.rearrange("p t e -> p (t e)"), start=True, stop=True).then_inc(rank_done, 1)

        @block.vector
        def _(dve):
            tt, ts = dve.tensor_tensor, dve.tensor_scalar
            finish_stats(dve, go, done, c, v)
            if moe:
                chain(dve, tt(scale2[:], c.rstd[:], c.rstd[:], ALU.mult), v)
                chain(dve, tt(scale2[:], scale2[:], c.var[:], ALU.mult), v)
                ts(scale2[:], scale2[:], EPS, None, ALU.add).then_inc(go, 1)
                take(dve, done)
                chain(dve, dve.reciprocal(scale2[:], scale2[:]), v)
                chain(dve, tt(scale2[:], scale2[:], c.rstd[:], ALU.mult), v)

            def copy(s):
                take(dve, turned[s])
                dve.sem_inc(row_free[s], 1)
                if not moe:
                    take(dve, col_free[s])
                chain(dve, dve.tensor_copy(col[s][:], turn[s][:].rearrange("p (k n) -> p k n", k=KD)), v)
                dve.sem_inc(col_ready[s], 1)
                if not moe:
                    dve.sem_inc(in_t, 1)

            def read(j, s):
                take(dve, lg_ready[s])
                for q in range(2):
                    tt(logit[:, bass.ds(j * 2 + q, 1), :].rearrange("p t e -> p (t e)"),
                       lg[s][:, q * ne:(q + 1) * ne], br[:], ALU.add).then_inc(v, 1)
                take(dve, v, 2)

            if not moe:
                for s in range(2):
                    dve.sem_inc(col_free[s], 1)
            for s in range(2):
                dve.sem_inc(row_free[s], 1)
            dve.sem_inc(stats_ready, 1)
            dve.wait_ge(w_in, 32)
            ahead(dve, copy, read)

            dve.wait_ge(iota_done, 2 if moe else 1)
            chain(dve, dve.tensor_reduce(top, logit, AX.X, ALU.max), v)
            tt(logit, logit, bcast(top, ne), ALU.subtract).then_inc(exp_go, 1)
            take(dve, exp_done)
            chain(dve, dve.tensor_reduce(total, prob, AX.X, ALU.add), v)
            chain(dve, dve.reciprocal(total, total), v)
            chain(dve, tt(prob, prob, bcast(total, ne), ALU.mult), v)

            def choose(pick, p):
                chain(dve, dve.tensor_reduce(p, prob, AX.X, ALU.max), v)
                chain(dve, tt(cand, prob, bcast(p, ne), ALU.is_equal), v)
                chain(dve, dve.scalar_tensor_tensor(cand, cand, -BIG, eid, ALU.mult, ALU.add), v)
                chain(dve, dve.tensor_reduce(first, cand, AX.X, ALU.min), v)
                chain(dve, tt(pick, cand, bcast(first, ne), ALU.is_equal), v)

            choose(pick1, p1)
            chain(dve, dve.scalar_tensor_tensor(prob, pick1, -2.0, prob, ALU.mult, ALU.add), v)
            choose(pick2, p2)
            if moe:
                chain(dve, tt(total, p1, p2, ALU.add), v)
                chain(dve, dve.reciprocal(total, total), v)
                chain(dve, tt(c.pick[:, :, 0], p1, total, ALU.mult), v)
                chain(dve, tt(c.pick[:, :, 1], p2, total, ALU.mult), v)
            else:
                chain(dve, tt(q1, p1, p1, ALU.subtract), v)
                tt(q2, p2, p1, ALU.subtract).then_inc(exp_go, 1)
                take(dve, exp_done, 2)
                chain(dve, tt(total, q1, q2, ALU.add), v)
                chain(dve, dve.reciprocal(total, total), v)
                chain(dve, tt(q1, q1, total, ALU.mult), v)
                chain(dve, tt(q2, q2, total, ALU.mult), v)
                chain(dve, tt(pick1, pick1, bcast(q1, ne), ALU.mult), v)
                chain(dve, tt(pick2, pick2, bcast(q2, ne), ALU.mult), v)
                chain(dve, tt(c.gate[:, :, 0:ne], pick1, pick2, ALU.add), v)
                chain(dve, dve.memset(c.gate[:, :, ne:ne + 1], 1.0), v)
                return

            real, pad_at = small[7], small[8]
            chain(dve, ts(real, c.node[:], float(N), None, ALU.is_lt), v)
            chain(dve, tt(pick1, pick1, bcast(real, ne), ALU.mult), v)
            chain(dve, tt(pick2, pick2, bcast(real, ne), ALU.mult), v)
            tt(cand, pick1, pick2, ALU.add).then_inc(rank_go, 1)
            take(dve, rank_done)
            chain(dve, dve.tensor_copy(tot.rearrange("p t e -> p (t e)"), c.ps[5][:, 0:n3]), v)
            chain(dve, dve.tensor_copy(cum, tot), v)
            here, there = cum, cum2
            step = 1
            while step < NB:
                chain(dve, dve.tensor_copy(there[:, 0:step, :], here[:, 0:step, :]), v)
                chain(dve, tt(there[:, step:NB, :], here[:, step:NB, :], here[:, 0:NB - step, :], ALU.add), v)
                here, there = there, here
                step *= 2
            chain(dve, ts(end[:], here[:, NB - 1, :], 1.0, float(TOK - 1), ALU.max, ALU.add), v)
            chain(dve, dve.tensor_copy(endi[:], end[:]), v)
            chain(dve, ts(endi[:], endi[:], TOK.bit_length() - 1, None, ALU.logical_shift_right), v)
            chain(dve, dve.tensor_copy(end[:], endi[:]), v)
            for e in range(1, E8):
                chain(dve, tt(end[:, e:e + 1], end[:, e:e + 1], end[:, e - 1:e], ALU.add), v)
            chain(dve, ts(end_last[:], end[:, E8 - 1:E8], -1.0, None, ALU.add), v)
            chain(dve, dve.tensor_copy(c.last_step[:], end_last[:]), v)
            chain(dve, ts(c.last_step[:], c.last_step[:], SLOTS_FFN.bit_length() - 1, None, ALU.logical_shift_right), v)
            chain(dve, dve.memset(base[:, 0:1], 0.0), v)
            chain(dve, ts(base[:, 1:E8], end[:, 0:E8 - 1], float(TOK), None, ALU.mult), v)
            chain(dve, tt(pos, here, tot, ALU.subtract), v)
            chain(dve, tt(pos.rearrange("p t e -> p (t e)"), pos.rearrange("p t e -> p (t e)"), c.ps[4][:, 0:n3], ALU.add), v)
            chain(dve, tt(pos, pos, base[:, None, :].to_broadcast([P, NB, E8]), ALU.add), v)
            chain(dve, ts(pad_at, c.node[:], float(DUMP - (NB - 2) * P), None, ALU.add), v)
            chain(dve, ts(real, real, -1.0, 1.0, ALU.mult, ALU.add), v)
            chain(dve, tt(pad_at, pad_at, real, ALU.mult), v)
            for i, pick in enumerate((pick1, pick2)):
                chain(dve, tt(pick, pick, pos, ALU.mult), v)
                chain(dve, dve.tensor_reduce(idx[:, :, i], pick, AX.X, ALU.add), v)
                chain(dve, dve.scalar_tensor_tensor(first, real, float(i * 2 * P), pad_at, ALU.mult, ALU.add), v)
                chain(dve, tt(idx[:, :, i], idx[:, :, i], first, ALU.add), v)
            chain(dve, dve.tensor_copy(c.slot[:], idx[:]), v)
            chain(dve, ts(tmp_t[:], tiles[:], end[:, 0:1], None, ALU.is_ge), v)
            for e in range(1, E8 - 1):
                chain(dve, dve.scalar_tensor_tensor(tmp_t[:], tiles[:], end[:, e:e + 1], tmp_t[:], ALU.is_ge, ALU.add), v)
            chain(dve, dve.tensor_copy(c.tile_expert[:], tmp_t[:]), v)

            def send(t, s):
                dve.tensor_copy(ring[:, s, :], c.slot[:, bass.ds(t, 1), :].rearrange("p t i -> p (t i)")).then_inc(v, 1)
                norm_tile(dve, xr[:, s, :], c, t, scale2).then_inc(v, 1)
                take(dve, v, 2)
                dve.sem_inc(x_ready[s], 1)
            for s in range(SLOTS):
                send(s, s)
            with dve.Fori(1, NB // SLOTS) as q:
                for s in range(SLOTS):
                    dve.wait_ge(scattered[s], q * 32)
                    send(q * SLOTS + s, s)
    stage(nc, run, "router")


def expert_ffn(nc, c, a):
    SLOTS = SLOTS_FFN
    LOADS = 5 * 16
    last_step = lambda eng: eng.value_load(c.last_step[0:1, 0:1], min_val=STEPS_MIN - 1, max_val=MT // SLOTS - 1)

    def run(block, sb, sem):
        tf, af = flat(c.T), flat(c.A)
        WW = KD * H
        places = [(tf, 0), (tf, 2 * WW), (af, 0), (af, 2 * WW)]
        w1 = [carve(area, o, (KD, H)) for area, o in places]
        w2 = [carve(area, o + WW, (KH, D)) for area, o in places]
        hid = carve(tf, 4 * WW, (KH, TOK))
        xs = [carve(tf, 4 * WW + KH * TOK + s * 2 * D, (2, D)) for s in range(SLOTS)]
        rest = af[:, 4 * WW:]
        ys = [carve(rest, s * 2 * D, (2, D)) for s in range(SLOTS)]
        b2 = [carve(rest, (2 * SLOTS + s) * D, (D,)) for s in range(SLOTS)]
        xe = carve(rest, 3 * SLOTS * D, (KD, TOK))
        par = [carve(rest, 3 * SLOTS * D + KD * TOK + s * (2 * KD + KH), (2 * KD + KH,)) for s in range(SLOTS)]
        turn, ph, py = c.ps[0], c.ps[1:3], c.ps[3:5]
        slots = lambda name: [sem(f"{name}{s}") for s in range(SLOTS)]
        slot_in, y_done, y_free, y_out = (slots(n) for n in ("slot_in", "y_done", "y_free", "y_out"))
        turned, xe_ready, h_ready, g_ready, y_read = (sem(n) for n in ("turned", "xe_ready", "h_ready", "g_ready", "y_read"))
        v, y_sum, pad_out = sem("v"), sem("y_sum"), sem("pad_out")

        @block.sync
        def _(sp):
            def load(i, s):
                e = sp.value_load(c.tile_expert[0:1, bass.ds(i, 1)], min_val=0, max_val=E8 - 1)
                one = lambda t: t[bass.ds(e, 1)]
                sp.dma_start(xs[s], c.xs_dram[bass.ds(i * TOK, TOK), :].rearrange("(t p) d -> p t d", p=P)).then_inc(slot_in[s], 16)
                sp.dma_start(w1[s], one(a["L0_ffn_W1"]).rearrange("e (k p) h -> p (e k) h", p=P)).then_inc(slot_in[s], 16)
                sp.dma_start(w2[s], one(a["L0_ffn_W2"]).rearrange("e (k p) d -> p (e k) d", p=P)).then_inc(slot_in[s], 16)
                sp.dma_start(par[s], one(c.expert_dram).rearrange("e p w -> p (e w)")).then_inc(slot_in[s], 16)
                sp.dma_start(b2[s], one(a["L0_ffn_b2"]).to_broadcast([P, D])).then_inc(slot_in[s], 16)

            def store(q, s):
                take(sp, y_done[s])
                sp.dma_start(c.ys_dram[bass.ds((q * SLOTS + s) * TOK, TOK), :].rearrange("(t p) d -> p t d", p=P),
                             ys[s]).then_inc(y_out[s], 16)

            for s in range(SLOTS):
                load(s, s)
            last = last_step(sp)
            with sp.Fori(0, last) as q:
                for s in range(SLOTS):
                    store(q, s)
                    load((q + 1) * SLOTS + s, s)
                    sp.wait_ge(y_out[s], q * 16 + 16)
                    sp.sem_inc(y_free[s], 1)
            for s in range(SLOTS):
                store(last, s)
            sp.dma_start(c.ys_dram[DUMP:XS_ROWS, :], c.xs_dram[DUMP:XS_ROWS, :]).then_inc(pad_out, 16)
            for s in range(SLOTS):
                sp.wait_ge(y_out[s], last * 16 + 16)
                sp.sem_inc(y_free[s], 1)
            sp.wait_ge(pad_out, 16)

        @block.scalar
        def _(act):
            with act.Fori(0, last_step(act) + 1) as q:
                for s in range(SLOTS):
                    for k in range(KH):
                        take(act, h_ready)
                        if k == 0:
                            act.wait_ge(slot_in[s], q * LOADS + LOADS)
                        act.activation(hid[:, k, :], ph[k % 2][:, 0:TOK], ACT.Gelu,
                                       bias=par[s][:, 2 * KD + k:2 * KD + k + 1]).then_inc(g_ready, 1)

        @block.tensor
        def _(pe):
            def turn_x(q, s):
                pe.wait_ge(slot_in[s], q * LOADS + LOADS)
                turn_to_cols(pe, c, xs[s], turn).then_inc(turned, 1)

            def body(q, s, more=True):
                take(pe, xe_ready)
                for k in range(KH):
                    if k >= 2:
                        take(pe, g_ready)
                    for d in range(KD):
                        mm = pe.matmul(ph[k % 2][:, 0:TOK], w1[s][:, d, k * P:(k + 1) * P], xe[:, d, :],
                                       start=(d == 0), stop=(d == KD - 1))
                    mm.then_inc(h_ready, 1)
                if more:
                    turn_x(q + (s + 1) // SLOTS, (s + 1) % SLOTS)
                take(pe, y_read)
                for k in range(KH):
                    if k >= KH - 2:
                        take(pe, g_ready)
                    for t in range(2):
                        mm = pe.matmul(py[t][:, 0:D], hid[:, k, t * P:(t + 1) * P], w2[s][:, k, :],
                                       start=(k == 0), stop=(k == KH - 1))
                mm.then_inc(y_sum, 1)

            turn_x(0, 0)
            last = last_step(pe)
            with pe.Fori(0, last) as q:
                for s in range(SLOTS):
                    body(q, s)
            for s in range(SLOTS):
                body(last, s, more=(s < SLOTS - 1))

        @block.vector
        def _(dve):
            def scale(q, s):
                dve.wait_ge(slot_in[s], q * LOADS + LOADS)
                take(dve, turned)
                for k in range(KD):
                    dve.tensor_scalar(xe[:, k, :], turn[:, k * TOK:(k + 1) * TOK], par[s][:, k:k + 1],
                                      par[s][:, KD + k:KD + k + 1], ALU.mult, ALU.add).then_inc(v, 1)
                take(dve, v, 2)
                dve.sem_inc(xe_ready, 1)

            def result(s):
                take(dve, y_sum)
                take(dve, y_free[s])
                for t in range(2):
                    dve.tensor_tensor(ys[s][:, t, :], py[t][:, 0:D], b2[s], ALU.add).then_inc(v, 1)
                take(dve, v, 2)
                dve.sem_inc(y_read, 1)
                dve.sem_inc(y_done[s], 1)

            dve.sem_inc(y_read, 1)
            for s in range(SLOTS):
                dve.sem_inc(y_free[s], 1)
            scale(0, 0)
            last = last_step(dve)
            with dve.Fori(0, last) as q:
                for s in range(SLOTS):
                    scale(q + (s + 1) // SLOTS, (s + 1) % SLOTS)
                    result(s)
            for s in range(SLOTS):
                if s + 1 < SLOTS:
                    scale(last, s + 1)
                result(s)
    stage(nc, run, "expert_ffn")


def combine(nc, c):
    SLOTS = 10
    STEPS = NB // SLOTS

    def run(block, sb, sem):
        y = carve(flat(c.T), 0, (SLOTS * 2, D))
        slots_free, landed, v = ([sem(f"{n}{s}") for s in range(SLOTS)] for n in ("slots_free", "landed", "v"))
        idx_ready, ring = [sem(f"idx_ready{s}") for s in range(SLOTS)], sb("ring", [P, SLOTS, 2], I32)

        @block.gpsimd
        def _(pool):
            with pool.Fori(0, STEPS):
                for s in range(SLOTS):
                    take(pool, idx_ready[s])
                    for i in range(2):
                        pool.indirect_dma_start(y[:, s * 2 + i, :], None, c.ys_dram,
                                                bass.IndirectOffsetOnAxis(ap=ring[:, s, i:i + 1], axis=0)
                                                ).then_inc(landed[s], 16)

        @block.scalar
        def _(act):
            for s in range(SLOTS):
                act.sem_inc(slots_free[s], 1)
            with act.Fori(0, STEPS) as q:
                for s in range(SLOTS):
                    take(act, slots_free[s])
                    act.copy(ring[:, s, :], c.slot[:, bass.ds(q * SLOTS + s, 1), :].rearrange("p t i -> p (t i)")
                             ).then_inc(idx_ready[s], 1)

        @block.vector
        def _(dve):
            with dve.Fori(0, STEPS) as q:
                for s in range(SLOTS):
                    t = q * SLOTS + s
                    x = tile_at(c.X, t)
                    dve.wait_ge(landed[s], q * 32 + 32)
                    for i in range(2):
                        chain(dve, dve.scalar_tensor_tensor(
                            x, y[:, s * 2 + i, :], c.pick[:, bass.ds(t, 1), i:i + 1].rearrange("p t i -> p (t i)"), x,
                            ALU.mult, ALU.add), v[s])
                    dve.sem_inc(slots_free[s], 1)
                    stat_tile(dve, c, t)
    stage(nc, run, "combine")


SH2, EN, EH1, EH2 = 128, 4, 128, 64
EP = EN // 2


def mlp_weights(c, a):
    af = flat(c.A)
    sw1, sw2, sw3 = carve(af, 0, (KD, D)), carve(af, 512, (KD, SH2)), carve(af, 768, (D,))
    ew1 = carve(af, 1024, (EN, KD, EH1))
    ew2, ew3 = carve(af, 2048, (EN, EH2)), carve(af, 2304, (EP, D))
    b3 = carve(af, 2816, (D,))[0:EN + 1]
    loads = [(sw1, a["L1_ffn_sW1"].rearrange("(k p) n -> p k n", p=P)),
             (sw2, a["L1_ffn_sW2"].rearrange("(k p) n -> p k n", p=P)),
             (sw3, a["L1_ffn_sW3"]),
             (ew2, a["L1_ffn_eW2"].rearrange("e h g -> h e g")),
             (b3[0:EN], a["L1_ffn_eb3"]), (b3[EN:EN + 1], a["L1_ffn_sb3"][None, :])]
    loads += [(ew3[:, u], a["L1_ffn_eW3"][2 * u:2 * u + 2].rearrange("v g o -> (v g) o")) for u in range(EP)]
    loads += [(ew1[:, e], a["L1_ffn_eW1"][e].rearrange("(k p) h -> p k h", p=P)) for e in range(EN)]
    return loads, (sw1, sw2, sw3, ew1, ew2, ew3, b3)


def gated_mlp(nc, c, a, out_dram):
    def run(block, sb, sem):
        af = flat(c.A)
        _, (sw1, sw2, sw3, ew1, ew2, ew3, b3) = mlp_weights(c, a)
        gate_row = carve(af, 3072, (2, EN + 1))
        gate_col = [carve(af, 3328 + s * BLK, (BLK,))[0:EN + 1] for s in range(2)]
        h1, e1 = carve(af, 4096, (KD, BLK)), carve(af, 4608, (EN, BLK))
        h2, e2 = [carve(af, 5632 + s * BLK, (BLK,)) for s in range(2)], [carve(af, 6144 + s * EP * BLK, (EP, BLK)) for s in range(2)]
        up_ready, up_done, low_ready, low_done = (sem(n) for n in ("up_ready", "up_done", "low_ready", "low_done"))
        res_ready, res_free, stored, written, v = (sem(n) for n in ("res_ready", "res_free", "stored", "written", "v"))
        up = c.ps[0:3]
        low = c.ps[3:5]
        res = c.ps[5:8]
        res_at = lambda e: res[0][:, 0:D] if e < 0 else res[1 + e % 2][:, e // 2 * D:(e // 2 + 1) * D]

        @block.sync
        def _(sp):
            with sp.Fori(0, NJ - 1) as j:
                take(sp, stored)
                sp.dma_start(out_dram[bass.ds(j * BLK, BLK), :].rearrange("(t p) d -> p t d", p=P),
                             c.X[:, bass.ds(j * 2, 2), :]).then_inc(written, 16)
            take(sp, stored)
            sp.dma_start(out_dram[FULL * P:N, :], c.X[0:REST, FULL, :]).then_inc(written, 16)
            sp.wait_ge(written, 16 * NJ)

        @block.scalar
        def _(act):
            def layer(dst, src, bias):
                return act.activation(dst, src, ACT.Relu, bias=bias)

            def upper(j):
                act.copy(gate_row, c.gate[:, bass.ds(j * 2, 2), :])
                take(act, up_ready)
                b, e = pcols(c, "L1_ffn_sb1"), pcols(c, "L1_ffn_eb1", EN)
                for m in range(KD):
                    layer(h1[:, m, :], up[0][:, m * BLK:(m + 1) * BLK], b[:, m:m + 1])
                for i in range(EN):
                    ins = layer(e1[:, i, :], up[1 + i // 2][:, i % 2 * BLK:(i % 2 + 1) * BLK], e[:, i:i + 1])
                ins.then_inc(up_done, 1)

            def lower(s):
                take(act, low_ready)
                b, e = pcols(c, "L1_ffn_sb2", 1), pcols(c, "L1_ffn_eb2", EP)
                act.copy(gate_col[s], low[0][0:EN + 1, BLK:2 * BLK])
                layer(h2[s], low[0][:, 0:BLK], b)
                for u in range(EP):
                    ins = layer(e2[s][:, u, :], low[1][:, u * BLK:(u + 1) * BLK], e[:, u:u + 1])
                ins.then_inc(low_done, 1)

            upper(0)
            lower(0)
            with act.Fori(0, NJ // 2) as q:
                for s in (1, 0):
                    upper(q * 2 + 2 - s)
                    lower(s)

        @block.tensor
        def _(pe):
            def upper_shared(j):
                x = cols_block(c, j)
                for m in range(KD):
                    for k in range(KD):
                        pe.matmul(up[0][:, m * BLK:(m + 1) * BLK], sw1[:, k, m * P:(m + 1) * P], x[:, k, :],
                                  start=(k == 0), stop=(k == KD - 1))

            def upper_experts(j):
                x = cols_block(c, j)
                for i in range(EN):
                    for k in range(KD):
                        mm = pe.matmul(up[1 + i // 2][:, i % 2 * BLK:(i % 2 + 1) * BLK], ew1[:, i, k, :], x[:, k, :],
                                       start=(k == 0), stop=(k == KD - 1))
                mm.then_inc(up_ready, 1)

            def lower():
                take(pe, up_done)
                for q in range(2):
                    pe.transpose(low[0][0:EN + 1, BLK + q * P:BLK + (q + 1) * P], gate_row[:, q, :], c.ident[:])
                for k in range(KD):
                    pe.matmul(low[0][:, 0:BLK], sw2[:, k, :], h1[:, k, :], start=(k == 0), stop=(k == KD - 1))
                for i in range(EN):
                    half = i % 2 * EH2
                    mm = pe.matmul(low[1][half:half + EH2, i // 2 * BLK:(i // 2 + 1) * BLK], ew2[:, i, :], e1[:, i, :],
                                   start=True, stop=True)
                mm.then_inc(low_ready, 1)

            def third(s, q):
                if q == 0:
                    take(pe, low_done)
                take(pe, res_free)
                at = slice(q * P, (q + 1) * P)
                pe.matmul(res_at(-1), h2[s][:, at], sw3, start=True, stop=False)
                pe.matmul(res_at(-1), gate_col[s][:, at], b3, start=False, stop=True)
                for i in range(EN):
                    half = i % 2 * EH2
                    mm = pe.matmul(res_at(i), e2[s][half:half + EH2, i // 2, at], ew3[half:half + EH2, i // 2, :],
                                   start=True, stop=True)
                mm.then_inc(res_ready, 1)

            upper_shared(0)
            upper_experts(0)
            lower()
            with pe.Fori(0, NJ // 2) as q2:
                for s in range(2):
                    upper_shared(q2 * 2 + s + 1)
                    third(s, 0)
                    upper_experts(q2 * 2 + s + 1)
                    third(s, 1)
                    lower()
            third(0, 0)
            third(0, 1)

        @block.vector
        def _(dve):
            def add(t):
                x = tile_at(c.X, t)
                gate = lambda e: c.gate[:, bass.ds(t, 1), e:e + 1].rearrange("p t e -> p (t e)")
                take(dve, res_ready)
                chain(dve, dve.tensor_tensor(x, x, res_at(-1), ALU.add), v)
                for e in range(EN):
                    chain(dve, dve.scalar_tensor_tensor(x, res_at(e), gate(e), x, ALU.mult, ALU.add), v)
                dve.sem_inc(res_free, 1)

            dve.sem_inc(res_free, 1)
            with dve.Fori(0, NJ) as j:
                add(j * 2)
                add(j * 2 + 1)
                dve.sem_inc(stored, 1)
    stage(nc, run, "gated_mlp")


def build(nc, a, out_dram):
    c = Chip()
    c.pat = {}
    at = 0
    for name, rows in (("L0_gnn_b1", 2), ("L0_gnn_g1", 2), ("L0_gnn_be1", 2), ("L0_gnn_b2", 2), ("L0_gnn_g2", 2),
                       ("L0_gnn_be2", 2), ("L1_gnn_c1_b2", 2), ("L1_gnn_c1_g", 2), ("L1_gnn_c1_b", 2),
                       ("L1_gnn_bn1_g", 2), ("L1_gnn_bn1_b", 2), ("L1_gnn_c2_b2", 2), ("L1_gnn_c2_g", 2),
                       ("L1_gnn_c2_b", 2), ("L1_gnn_bn2_g", 2), ("L1_gnn_bn2_b", 2), ("L1_ffn_sb1", 2),
                       ("L1_ffn_sb2", 1), ("L1_ffn_eb1", 4), ("L1_ffn_eb2", 2)):
        c.pat[name] = (at, rows)
        at += rows
    assert at <= P
    for name, at, rows in (("L0_ffn_ln_g", P, KD * E8), ("L0_ffn_ln_b", P + KD * E8, KD * E8),
                           ("L0_ffn_b1", P + 2 * KD * E8, KH * E8)):
        c.pat[name] = (at, rows)
    c.h_dram = nc.dram_tensor("h_rows", (NB * P, D), F32).ap()
    c.xs_dram = nc.dram_tensor("xs_rows", (XS_ROWS, D), F32).ap()
    c.ys_dram = nc.dram_tensor("ys_rows", (XS_ROWS, D), F32).ap()
    c.range_dram = nc.dram_tensor("ranges", (NG * 2,), I32).ap()
    c.record_dram = nc.dram_tensor("sorted_records", (EPT * P, 4), F32).ap()
    c.expert_dram = nc.dram_tensor("expert_cols", (E8, P, 2 * KD + KH), F32).ap()
    with ExitStack() as ctx:
        def sb(name, shape, dt=F32):
            return ctx.enter_context(nc.sbuf_tensor(name, shape, dt))

        c.X, c.A = sb("X", [P, NB, D]), sb("A", [P, NB, D])
        c.T = sb("T", [P, KD, NB * P])
        c.iota = sb("iota", [P, (FULL + 1) * P])
        c.edges = sb("edges", [P, 3, EPT])
        c.ident, c.upper, c.ones = (sb(n, [P, P]) for n in ("ident", "upper", "ones"))
        c.node, c.mean, c.var, c.rstd, c.shift = (sb(n, [P, NB]) for n in ("node", "mean", "var", "rstd", "shift"))
        c.st = sb("st", [P, NB, 6])
        c.pcol, c.affine, c.eps = sb("pcol", [P, 2 * P]), sb("affine", [P, 2, KD]), sb("eps", [P, 1])
        c.dst_ranges, c.src_ranges = sb("dst_ranges", [P, NG * 2], I32), sb("src_ranges", [P, NG * 2], I32)
        c.sorted = carve(flat(c.T), D, (3, EPT))
        c.gate, c.pick = sb("gate", [P, NB, 5]), sb("pick", [P, NB, 2])
        c.last_step = sb("last_step", [P, 1], I32)
        c.slot, c.tile_expert = sb("slot", [P, NB, 2], I32), sb("tile_expert", [P, MT], I32)
        c.ps = [ctx.enter_context(nc.psum_tensor(f"bank{i}", [P, 512], F32)) for i in range(8)]
        col = lambda name: pcols(c, name)

        prepare(nc, c, a)
        sort_edges(nc, c)
        segment_sum(nc, c, c.sorted, DST, SRC, c.src_ranges, clear=False, fill=True)
        aggregate_product(nc, c, a["L0_gnn_W1"], col("L0_gnn_b1"), col("L0_gnn_g1"), col("L0_gnn_be1"))
        norm_product(nc, c, a["L0_gnn_W2"], col("L0_gnn_b2"), col("L0_gnn_g2"), col("L0_gnn_be2"))
        norm_to_rows(nc, c, residual=False)
        router(nc, c, a, "L0_ffn_Wr", "L0_ffn_br", E8, moe=True)
        expert_ffn(nc, c, a)
        combine(nc, c)
        message_rows(nc, c, a["L1_gnn_c1_w1"], a["L1_gnn_c1_b1"], from_x=True)
        segment_sum(nc, c, c.edges, SRC, DST, c.dst_ranges, clear=True, fill=False)
        aggregate_product(nc, c, a["L1_gnn_c1_w2"], col("L1_gnn_c1_b2"), col("L1_gnn_c1_g"), col("L1_gnn_c1_b"))
        norm_relu(nc, c, col("L1_gnn_bn1_g"), col("L1_gnn_bn1_b"))
        message_rows(nc, c, a["L1_gnn_c2_w1"], a["L1_gnn_c2_b1"], from_x=False)
        segment_sum(nc, c, c.edges, SRC, DST, c.dst_ranges, clear=True, fill=False)
        aggregate_product(nc, c, a["L1_gnn_c2_w2"], col("L1_gnn_c2_b2"), col("L1_gnn_c2_g"), col("L1_gnn_c2_b"))
        norm_relu(nc, c, col("L1_gnn_bn2_g"), col("L1_gnn_bn2_b"))
        norm_to_rows(nc, c, residual=True)
        router(nc, c, a, "L1_ffn_gW", "L1_ffn_gb", 4, moe=False)
        gated_mlp(nc, c, a, out_dram)


def kernel(**inputs):
    import concourse.bacc as _bacc
    from concourse.bass_utils import run_bass_kernel_spmd as _run

    nc = _bacc.Bacc("TRN2", target_bir_lowering=False, num_devices=1)
    arrays, args = {}, {}
    for name, value in inputs.items():
        v = np.ascontiguousarray(value)
        arrays[f"in_{name}"] = v
        args[name] = nc.dram_tensor(f"in_{name}", v.shape, mybir.dt.from_np(v.dtype), kind="ExternalInput").ap()
    out = nc.dram_tensor("out_x", (N, D), F32, kind="ExternalOutput").ap()
    build(nc, args, out)
    r = _run(nc, [arrays], core_ids=[0])
    return r.results[0]["out_x"]
```
